# Optimizing a Trainium2 kernel written in Bass

```python
import numpy as np
import jax
import jax.numpy as jnp

def _softmax(x, axis=-1):
    return jax.nn.softmax(x, axis=axis)

def _gelu(x):
    return jax.nn.gelu(x, approximate=True)

def _silu(x):
    return jax.nn.silu(x)

def _sigmoid(x):
    return jax.nn.sigmoid(x)

def _layernorm(x, axis=-1, eps=1e-05):
    m = jnp.mean(x, axis=axis, keepdims=True)
    v = jnp.var(x, axis=axis, keepdims=True)
    return (x - m) / jnp.sqrt(v + eps)

def _scatter_add(tgt, idx, src, axis=0):
    return tgt.at[idx].add(src)

def _segment_sum(src, seg, n):
    return jax.ops.segment_sum(src, seg, n)
kernel_name = 'mk_vit_tower_postln_d2_tok_img256_r4_bf5f98'

def setup_inputs(seed: int=0):
    np.random.seed(seed)
    _w = jnp.asarray

    def _rec_inputs():
        import jax
        import jax.numpy as jnp
        _rk = jax.random.key(seed)
        x = -0.000125008 + 0.999885 * jax.random.normal(jax.random.fold_in(_rk, 1), (32, 64, 128, 128), jnp.float32)
        return x
    x = _rec_inputs()

    def _L0_tok_setup():
        import jax, jax.numpy as jnp
        import numpy as np
        D_MODEL = 64
        NHEAD = 8
        DS = 4
        OFFSET_SCALE = 4.0

        def bilinear_sample(fm, pts):
            B, C, H, W = fm.shape
            x = (pts[..., 0] + 1.0) * 0.5 * (W - 1)
            y = (pts[..., 1] + 1.0) * 0.5 * (H - 1)
            x0 = jnp.clip(jnp.floor(x), 0.0, W - 2)
            y0 = jnp.clip(jnp.floor(y), 0.0, H - 2)
            wx = jnp.clip(x - x0, 0.0, 1.0)
            wy = jnp.clip(y - y0, 0.0, 1.0)
            x0i = x0.astype(jnp.int32)
            y0i = y0.astype(jnp.int32)
            fm2 = fm.reshape(B, C, H * W)
            N, P = (pts.shape[1], pts.shape[2])

            def gather(yi, xi):
                idx = (yi * W + xi).reshape(B, N * P)
                g = jnp.take_along_axis(fm2, idx[:, None, :], axis=2)
                return g.reshape(B, C, N, P)
            v00 = gather(y0i, x0i)
            v01 = gather(y0i, x0i + 1)
            v10 = gather(y0i + 1, x0i)
            v11 = gather(y0i + 1, x0i + 1)
            wx_ = wx[:, None]
            wy_ = wy[:, None]
            out = v00 * (1 - wx_) * (1 - wy_) + v01 * wx_ * (1 - wy_) + v10 * (1 - wx_) * wy_ + v11 * wx_ * wy_
            return jnp.moveaxis(out, 1, -1)

        def layer_norm(x, g, b, eps=1e-05):
            mu = jnp.mean(x, axis=-1, keepdims=True)
            var = jnp.var(x, axis=-1, keepdims=True)
            return (x - mu) * jax.lax.rsqrt(var + eps) * g + b

        def reference_points(B, H, W):
            yc = jnp.linspace(-1.0, 1.0, H // DS)
            xc = jnp.linspace(-1.0, 1.0, W // DS)
            yg, xg = jnp.meshgrid(yc, xc, indexing='ij')
            ref = jnp.stack([xg.reshape(-1), yg.reshape(-1)], axis=-1)
            return jnp.broadcast_to(ref[None], (B,) + ref.shape)
        key = jax.random.key(seed)
        ks = jax.random.split(key, 6)
        B, C, H, W = (8, D_MODEL, 128, 128)
        s = 0.05
        return {'feature_map': jax.random.normal(ks[0], (B, C, H, W), jnp.float32), 'W_q': jax.random.normal(ks[1], (C, C), jnp.float32) * s, 'W_k': jax.random.normal(ks[2], (C, C), jnp.float32) * s, 'W_v': jax.random.normal(ks[3], (C, C), jnp.float32) * s, 'W_o1': jax.random.normal(ks[4], (C, C // DS), jnp.float32) * s, 'b_o1': jnp.zeros((C // DS,), jnp.float32), 'ln_g': jnp.ones((C // DS,), jnp.float32), 'ln_b': jnp.zeros((C // DS,), jnp.float32), 'W_o2': jax.random.normal(ks[5], (C // DS, NHEAD * 2), jnp.float32) * s, 'b_o2': jnp.zeros((NHEAD * 2,), jnp.float32)}
    _L0_tok_all = _L0_tok_setup()
    _L0_tok_in = {k: v for k, v in _L0_tok_all.items() if k in ('W_q', 'W_k', 'W_v', 'W_o1', 'b_o1', 'ln_g', 'ln_b', 'W_o2', 'b_o2')}
    del _L0_tok_all

    def _L0_attn_setup():
        import jax, jax.numpy as jnp
        import numpy as np
        DIM = 64
        HEADS = 4
        DIM_HEAD = 32
        NUM_MEM = 4
        HIDDEN = HEADS * DIM_HEAD
        SCALE = DIM_HEAD ** (-0.5)

        def rmsnorm(x, g):
            n = jnp.linalg.norm(x, axis=-1, keepdims=True)
            return x / jnp.maximum(n, 1e-12) * g * x.shape[-1] ** 0.5
        key = jax.random.key(seed)
        ks = jax.random.split(key, 8)
        B, N = (4, 4096)
        return {'x': jax.random.normal(ks[0], (B, N, DIM), jnp.float32), 't': jax.random.normal(ks[1], (B,), jnp.float32), 'w_qkv': jax.random.normal(ks[2], (DIM, 3 * HIDDEN), jnp.float32) * 0.02, 'mem_kv': jax.random.normal(ks[3], (2, HEADS, DIM_HEAD, NUM_MEM), jnp.float32), 'w_out': jax.random.normal(ks[4], (HIDDEN, DIM), jnp.float32) * 0.02, 'b_out': jnp.zeros((DIM,), jnp.float32), 'g_out': jnp.ones((DIM,), jnp.float32), 'g_pre': jnp.ones((DIM,), jnp.float32)}
    _L0_attn_all = _L0_attn_setup()
    _L0_attn_in = {k: v for k, v in _L0_attn_all.items() if k in ('t', 'w_qkv', 'mem_kv', 'w_out', 'b_out', 'g_out', 'g_pre')}
    del _L0_attn_all

    def _L0_ffn_setup():
        import jax, jax.numpy as jnp
        import numpy as np
        B, S, D = (8, 1024, 64)
        H = 4 * D
        CAPACITY = 0.5
        key = jax.random.key(seed)
        ks = jax.random.split(key, 6)
        x = jax.random.normal(ks[0], (B, S, D), dtype=jnp.float32)
        attention_mask = jnp.zeros((B, 1, 1, S), dtype=jnp.float32)
        wr = jax.random.normal(ks[1], (D, 1), dtype=jnp.float32) * 0.02
        br = jnp.zeros((1,), dtype=jnp.float32)
        w1 = jax.random.normal(ks[2], (D, H), dtype=jnp.float32) * 0.02
        b1 = jnp.zeros((H,), dtype=jnp.float32)
        w2 = jax.random.normal(ks[3], (H, D), dtype=jnp.float32) * 0.02
        b2 = jnp.zeros((D,), dtype=jnp.float32)
        return {'x': x, 'attention_mask': attention_mask, 'wr': wr, 'br': br, 'w1': w1, 'b1': b1, 'w2': w2, 'b2': b2}
    _L0_ffn_all = _L0_ffn_setup()
    _L0_ffn_in = {k: v for k, v in _L0_ffn_all.items() if k in ('attention_mask', 'wr', 'br', 'w1', 'b1', 'w2', 'b2')}
    del _L0_ffn_all

    def _L1_attn_setup():
        import jax, jax.numpy as jnp
        import numpy as np
        B, T, C, H = (8, 512, 64, 4)
        D = C // H
        SCALE = D ** (-0.5)
        key = jax.random.key(seed)
        ks = jax.random.split(key, 5)
        return {'x': jax.random.normal(ks[0], (B, T, C), dtype=jnp.float32), 'Wqkv': jax.random.normal(ks[1], (C, 3 * C), dtype=jnp.float32) * C ** (-0.5), 'bqkv': jax.random.normal(ks[2], (3 * C,), dtype=jnp.float32) * 0.02, 'Wproj': jax.random.normal(ks[3], (C, C), dtype=jnp.float32) * C ** (-0.5), 'bproj': jax.random.normal(ks[4], (C,), dtype=jnp.float32) * 0.02}
    _L1_attn_all = _L1_attn_setup()
    _L1_attn_in = {k: v for k, v in _L1_attn_all.items() if k in ('Wqkv', 'bqkv', 'Wproj', 'bproj')}
    del _L1_attn_all

    def _L1_ffn_setup():
        import jax, jax.numpy as jnp
        import numpy as np
        E, D, H, TOP_K = (6, 64, 64, 2)
        ROUTER_H = D // 2
        key = jax.random.key(seed)
        ks = jax.random.split(key, 12)
        s = 1.0 / np.sqrt(D)
        sh = 1.0 / np.sqrt(H)
        sr = 1.0 / np.sqrt(ROUTER_H)
        return {'features': jax.random.normal(ks[0], (8, 1024, D), dtype=jnp.float32), 'router_w1': jax.random.uniform(ks[1], (D, ROUTER_H), jnp.float32, -s, s), 'router_b1': jnp.zeros((ROUTER_H,), jnp.float32), 'router_w2': jax.random.uniform(ks[2], (ROUTER_H, E), jnp.float32, -sr, sr), 'router_b2': jnp.zeros((E,), jnp.float32), 'expert_w1': jax.random.uniform(ks[3], (E, D, H), jnp.float32, -s, s), 'expert_b1': jnp.zeros((E, H), jnp.float32), 'expert_w2': jax.random.uniform(ks[4], (E, H, H), jnp.float32, -sh, sh), 'expert_b2': jnp.zeros((E, H), jnp.float32), 'expert_w3': jax.random.uniform(ks[5], (E, H, D), jnp.float32, -sh, sh), 'expert_b3': jnp.zeros((E, D), jnp.float32)}
    _L1_ffn_all = _L1_ffn_setup()
    _L1_ffn_in = {k: v for k, v in _L1_ffn_all.items() if k in ('router_w1', 'router_b1', 'router_w2', 'router_b2', 'expert_w1', 'expert_b1', 'expert_w2', 'expert_b2', 'expert_w3', 'expert_b3')}
    del _L1_ffn_all
    return {'x': x, 'L0_tok_W_q': _L0_tok_in['W_q'], 'L0_tok_W_k': _L0_tok_in['W_k'], 'L0_tok_W_v': _L0_tok_in['W_v'], 'L0_tok_W_o1': _L0_tok_in['W_o1'], 'L0_tok_b_o1': _L0_tok_in['b_o1'], 'L0_tok_ln_g': _L0_tok_in['ln_g'], 'L0_tok_ln_b': _L0_tok_in['ln_b'], 'L0_tok_W_o2': _L0_tok_in['W_o2'], 'L0_tok_b_o2': _L0_tok_in['b_o2'], 'L0_attn_t': _L0_attn_in['t'], 'L0_attn_w_qkv': _L0_attn_in['w_qkv'], 'L0_attn_mem_kv': _L0_attn_in['mem_kv'], 'L0_attn_w_out': _L0_attn_in['w_out'], 'L0_attn_b_out': _L0_attn_in['b_out'], 'L0_attn_g_out': _L0_attn_in['g_out'], 'L0_attn_g_pre': _L0_attn_in['g_pre'], 'L0_ffn_attention_mask': _L0_ffn_in['attention_mask'], 'L0_ffn_wr': _L0_ffn_in['wr'], 'L0_ffn_br': _L0_ffn_in['br'], 'L0_ffn_w1': _L0_ffn_in['w1'], 'L0_ffn_b1': _L0_ffn_in['b1'], 'L0_ffn_w2': _L0_ffn_in['w2'], 'L0_ffn_b2': _L0_ffn_in['b2'], 'L1_attn_Wqkv': _L1_attn_in['Wqkv'], 'L1_attn_bqkv': _L1_attn_in['bqkv'], 'L1_attn_Wproj': _L1_attn_in['Wproj'], 'L1_attn_bproj': _L1_attn_in['bproj'], 'L1_ffn_router_w1': _L1_ffn_in['router_w1'], 'L1_ffn_router_b1': _L1_ffn_in['router_b1'], 'L1_ffn_router_w2': _L1_ffn_in['router_w2'], 'L1_ffn_router_b2': _L1_ffn_in['router_b2'], 'L1_ffn_expert_w1': _L1_ffn_in['expert_w1'], 'L1_ffn_expert_b1': _L1_ffn_in['expert_b1'], 'L1_ffn_expert_w2': _L1_ffn_in['expert_w2'], 'L1_ffn_expert_b2': _L1_ffn_in['expert_b2'], 'L1_ffn_expert_w3': _L1_ffn_in['expert_w3'], 'L1_ffn_expert_b3': _L1_ffn_in['expert_b3']}

def reference(x, L0_tok_W_q, L0_tok_W_k, L0_tok_W_v, L0_tok_W_o1, L0_tok_b_o1, L0_tok_ln_g, L0_tok_ln_b, L0_tok_W_o2, L0_tok_b_o2, L0_attn_t, L0_attn_w_qkv, L0_attn_mem_kv, L0_attn_w_out, L0_attn_b_out, L0_attn_g_out, L0_attn_g_pre, L0_ffn_attention_mask, L0_ffn_wr, L0_ffn_br, L0_ffn_w1, L0_ffn_b1, L0_ffn_w2, L0_ffn_b2, L1_attn_Wqkv, L1_attn_bqkv, L1_attn_Wproj, L1_attn_bproj, L1_ffn_router_w1, L1_ffn_router_b1, L1_ffn_router_w2, L1_ffn_router_b2, L1_ffn_expert_w1, L1_ffn_expert_b1, L1_ffn_expert_w2, L1_ffn_expert_b2, L1_ffn_expert_w3, L1_ffn_expert_b3):
    import jax
    import jax.numpy as jnp

    def _L0_tok_ref(feature_map, W_q, W_k, W_v, W_o1, b_o1, ln_g, ln_b, W_o2, b_o2):
        import jax, jax.numpy as jnp
        import numpy as np
        D_MODEL = 64
        NHEAD = 8
        DS = 4
        OFFSET_SCALE = 4.0

        def bilinear_sample(fm, pts):
            B, C, H, W = fm.shape
            x = (pts[..., 0] + 1.0) * 0.5 * (W - 1)
            y = (pts[..., 1] + 1.0) * 0.5 * (H - 1)
            x0 = jnp.clip(jnp.floor(x), 0.0, W - 2)
            y0 = jnp.clip(jnp.floor(y), 0.0, H - 2)
            wx = jnp.clip(x - x0, 0.0, 1.0)
            wy = jnp.clip(y - y0, 0.0, 1.0)
            x0i = x0.astype(jnp.int32)
            y0i = y0.astype(jnp.int32)
            fm2 = fm.reshape(B, C, H * W)
            N, P = (pts.shape[1], pts.shape[2])

            def gather(yi, xi):
                idx = (yi * W + xi).reshape(B, N * P)
                g = jnp.take_along_axis(fm2, idx[:, None, :], axis=2)
                return g.reshape(B, C, N, P)
            v00 = gather(y0i, x0i)
            v01 = gather(y0i, x0i + 1)
            v10 = gather(y0i + 1, x0i)
            v11 = gather(y0i + 1, x0i + 1)
            wx_ = wx[:, None]
            wy_ = wy[:, None]
            out = v00 * (1 - wx_) * (1 - wy_) + v01 * wx_ * (1 - wy_) + v10 * (1 - wx_) * wy_ + v11 * wx_ * wy_
            return jnp.moveaxis(out, 1, -1)

        def layer_norm(x, g, b, eps=1e-05):
            mu = jnp.mean(x, axis=-1, keepdims=True)
            var = jnp.var(x, axis=-1, keepdims=True)
            return (x - mu) * jax.lax.rsqrt(var + eps) * g + b

        def reference_points(B, H, W):
            yc = jnp.linspace(-1.0, 1.0, H // DS)
            xc = jnp.linspace(-1.0, 1.0, W // DS)
            yg, xg = jnp.meshgrid(yc, xc, indexing='ij')
            ref = jnp.stack([xg.reshape(-1), yg.reshape(-1)], axis=-1)
            return jnp.broadcast_to(ref[None], (B,) + ref.shape)
        B, C, H, W = feature_map.shape
        dh = C // NHEAD
        ref = reference_points(B, H, W)
        Nq = ref.shape[1]
        q_feat = bilinear_sample(feature_map, ref[:, :, None, :])[:, :, 0]
        queries = q_feat @ W_q.T
        h = jax.nn.gelu(layer_norm(q_feat @ W_o1 + b_o1, ln_g, ln_b))
        off = (h @ W_o2 + b_o2).reshape(B, Nq, NHEAD, 2) * OFFSET_SCALE
        scale = jnp.array([2.0 / (W - 1), 2.0 / (H - 1)], jnp.float32)
        sampling_points = ref[:, :, None, :] + off * scale
        sampled = bilinear_sample(feature_map, sampling_points)
        keys = jnp.einsum('bnpc,dc->bnpd', sampled, W_k)
        values = jnp.einsum('bnpc,dc->bnpd', sampled, W_v)
        q = queries.reshape(B, Nq, NHEAD, dh)
        k = keys.reshape(B, Nq, NHEAD, NHEAD, dh)
        v = values.reshape(B, Nq, NHEAD, NHEAD, dh)
        scores = jnp.einsum('bnhd,bnphd->bnhp', q, k) / jnp.sqrt(jnp.float32(dh))
        attn = jax.nn.softmax(scores, axis=-1)
        out = jnp.einsum('bnhp,bnphd->bnhd', attn, v).reshape(B, Nq, C)
        return out

    def _L0_attn_ref(x, t, w_qkv, mem_kv, w_out, b_out, g_out, g_pre):
        import jax, jax.numpy as jnp
        import numpy as np
        DIM = 64
        HEADS = 4
        DIM_HEAD = 32
        NUM_MEM = 4
        HIDDEN = HEADS * DIM_HEAD
        SCALE = DIM_HEAD ** (-0.5)

        def rmsnorm(x, g):
            n = jnp.linalg.norm(x, axis=-1, keepdims=True)
            return x / jnp.maximum(n, 1e-12) * g * x.shape[-1] ** 0.5
        b, n, c = x.shape
        xn = rmsnorm(x, g_pre)
        qkv = xn @ w_qkv
        q, k, v = jnp.split(qkv, 3, axis=-1)

        def to_heads(z):
            return z.reshape(b, n, HEADS, DIM_HEAD).transpose(0, 2, 3, 1)
        q, k, v = map(to_heads, (q, k, v))
        mk = jnp.broadcast_to(mem_kv[0], (b, HEADS, DIM_HEAD, NUM_MEM))
        mv = jnp.broadcast_to(mem_kv[1], (b, HEADS, DIM_HEAD, NUM_MEM))
        k = jnp.concatenate([mk, k], axis=-1)
        v = jnp.concatenate([mv, v], axis=-1)
        q = jax.nn.softmax(q, axis=-2) * SCALE
        k = jax.nn.softmax(k, axis=-1)
        context = jnp.einsum('bhdn,bhen->bhde', k, v)
        out = jnp.einsum('bhde,bhdn->bhen', context, q)
        out = out.transpose(0, 3, 1, 2).reshape(b, n, HIDDEN)
        out = rmsnorm(out @ w_out + b_out, g_out)
        return out + x

    def _L0_ffn_ref(x, attention_mask, wr, br, w1, b1, w2, b2):
        import jax, jax.numpy as jnp
        import numpy as np
        B, S, D = (8, 1024, 64)
        H = 4 * D
        CAPACITY = 0.5
        b, s, d = x.shape
        weights = (jnp.einsum('bsd,do->bso', x, wr) + br)[..., 0]
        k = max(1, int(CAPACITY * s))
        kk = k - 1 if k > 1 else 1
        _, idx = jax.lax.top_k(weights, k)
        sel_idx = idx[:, :kk]
        sel = jnp.take_along_axis(x, sel_idx[:, :, None], axis=1)
        h = jax.nn.gelu(jnp.einsum('bkd,dh->bkh', sel, w1) + b1)
        y = jnp.einsum('bkh,hd->bkd', h, w2) + b2
        w_sel = jnp.take_along_axis(weights, sel_idx, axis=1)
        y = y * w_sel[..., None]
        batch_idx = jnp.arange(b)[:, None]
        processed = jnp.zeros_like(x).at[batch_idx, sel_idx].set(y)
        return processed + x

    def _L1_attn_ref(x, Wqkv, bqkv, Wproj, bproj):
        import jax, jax.numpy as jnp
        import numpy as np
        B, T, C, H = (8, 512, 64, 4)
        D = C // H
        SCALE = D ** (-0.5)
        b, t, c = x.shape
        qkv = (x @ Wqkv + bqkv).reshape(b, t, 3, H, D)
        qkv = jnp.transpose(qkv, (2, 0, 3, 1, 4))
        q, k, v = (qkv[0], qkv[1], qkv[2])
        attn = jnp.einsum('bhqd,bhkd->bhqk', q, k) * SCALE
        causal = jnp.triu(jnp.ones((t, t), dtype=bool), k=1)
        attn = jnp.where(causal, -jnp.inf, attn)
        attn = jax.nn.softmax(attn, axis=-1)
        out = jnp.einsum('bhqk,bhkd->bhqd', attn, v)
        out = jnp.transpose(out, (0, 2, 1, 3)).reshape(b, t, c)
        return out @ Wproj + bproj

    def _L1_ffn_ref(features, router_w1, router_b1, router_w2, router_b2, expert_w1, expert_b1, expert_w2, expert_b2, expert_w3, expert_b3):
        import jax, jax.numpy as jnp
        import numpy as np
        E, D, H, TOP_K = (6, 64, 64, 2)
        ROUTER_H = D // 2
        rh = jax.nn.relu(features @ router_w1 + router_b1)
        expert_logits = jax.nn.softmax(rh @ router_w2 + router_b2, axis=-1)
        top_w, top_i = jax.lax.top_k(expert_logits, TOP_K)
        routing_weights = jax.nn.softmax(top_w, axis=-1)
        h1 = jax.nn.relu(jnp.einsum('bsd,edh->bseh', features, expert_w1) + expert_b1)
        h2 = jax.nn.relu(jnp.einsum('bseh,ehf->bsef', h1, expert_w2) + expert_b2)
        expert_out = jnp.einsum('bsef,efo->bseo', h2, expert_w3) + expert_b3
        sel = jnp.take_along_axis(expert_out, top_i[:, :, :, None], axis=2)
        combined = jnp.sum(sel * routing_weights[..., None], axis=2)
        return combined
    h = _L0_tok_ref(x, L0_tok_W_q, L0_tok_W_k, L0_tok_W_v, L0_tok_W_o1, L0_tok_b_o1, L0_tok_ln_g, L0_tok_ln_b, L0_tok_W_o2, L0_tok_b_o2)
    h = _layernorm(h + _L0_attn_ref(h, L0_attn_t, L0_attn_w_qkv, L0_attn_mem_kv, L0_attn_w_out, L0_attn_b_out, L0_attn_g_out, L0_attn_g_pre), axis=-1)
    h = _layernorm(h + _L0_ffn_ref(h, L0_ffn_attention_mask, L0_ffn_wr, L0_ffn_br, L0_ffn_w1, L0_ffn_b1, L0_ffn_w2, L0_ffn_b2), axis=-1)
    h = _layernorm(h + _L1_attn_ref(h, L1_attn_Wqkv, L1_attn_bqkv, L1_attn_Wproj, L1_attn_bproj), axis=-1)
    h = _layernorm(h + _L1_ffn_ref(h, L1_ffn_router_w1, L1_ffn_router_b1, L1_ffn_router_w2, L1_ffn_router_b2, L1_ffn_expert_w1, L1_ffn_expert_b1, L1_ffn_expert_w2, L1_ffn_expert_b2, L1_ffn_expert_w3, L1_ffn_expert_b3), axis=-1)
    return h

_drawn_inputs = setup_inputs


def setup_inputs(seed=0):
    import zlib

    import numpy as np

    out = dict(_drawn_inputs(seed))
    spreads = {'L0_tok_b_o1': (0.0, 0.1),
     'L0_tok_ln_g': (1.0, 0.2),
     'L0_tok_ln_b': (0.0, 0.472),
     'L0_tok_b_o2': (0.0, 0.1),
     'L0_attn_b_out': (0.0, 0.1),
     'L0_attn_g_out': (1.0, 0.2),
     'L0_attn_g_pre': (1.0, 0.6),
     'L0_ffn_b1': (0.0, 0.8),
     'L0_ffn_b2': (0.0, 0.8),
     'L1_ffn_router_b1': (0.0, 0.1),
     'L1_ffn_router_b2': (0.0, 0.694),
     'L1_ffn_expert_b1': (0.0, 0.8),
     'L1_ffn_expert_b2': (0.0, 0.268),
     'L1_ffn_expert_b3': (0.0, 0.1)}
    factors = {'L0_tok_W_q': 5.393,
     'L0_tok_W_k': 5.414,
     'L0_attn_w_qkv': 8.0,
     'L0_attn_mem_kv': 8.0,
     'L0_attn_w_out': 8.0,
     'L0_ffn_wr': 8.0,
     'L0_ffn_w1': 8.0,
     'L0_ffn_w2': 8.0,
     'L1_attn_bqkv': 3.831,
     'L1_attn_bproj': 4.117}
    for name, (base, spread) in spreads.items():
        noise = np.random.default_rng([zlib.crc32(name.encode()), seed]).standard_normal(out[name].shape)
        drawn = base * np.exp(spread * noise) if base else spread * noise
        out[name] = jnp.asarray(drawn.astype(out[name].dtype))
    for name, factor in factors.items():
        out[name] = (out[name] * factor).astype(out[name].dtype)
    return out
```

```python
from contextlib import ExitStack

import numpy as np

import concourse.bass as bass
from concourse import mybir

F32 = mybir.dt.float32
I32 = mybir.dt.int32
U32 = mybir.dt.uint32
ALU = mybir.AluOpType
ACT = mybir.ActivationFunctionType
AX = mybir.AxisListType

P = 128
NT = 8
C = 64
GRID = 32
SIDE = 128
CELLS = SIDE - 1
NPT = 8
L0H, L0D = 4, 32
L1H, L1D = 4, 16
NMEM = 4
NE = 6
KEEP = 511
N = P * NT


def pack_columns(parts):
    at, out = 0, {}
    for name, width in parts:
        out[name] = (at, at + width)
        at += width
    return out, at


COLS, WIDTH = pack_columns([
    ("ident", 128), ("neg_mask", 128), ("lower", 128), ("head_mask", 128),
    ("ref_xy", NT * NPT * 2), ("q_corner", NT * 4), ("iota_e", NE),
    ("wq_o1", 80), ("b_o1", 16), ("ln_g", 16), ("ln_b", 16), ("w_o2", 128), ("b_o2", 16),
    ("w_kv", 256), ("w_qkv", 384), ("g_pre", 1), ("mem_k", NMEM), ("mem_v", 128), ("w_out", 64),
    ("b_out", 64), ("g_out", 64), ("wr", 128), ("br", 1), ("w1", 256), ("b1", 2), ("w2", 128),
    ("b2", 64), ("w_q1", 128), ("w_k1", 128), ("w_v1", 64), ("b_q1", 1), ("b_k1", 1),
    ("b_v1", 64), ("w_proj", 64), ("b_proj", 64), ("rw1", 32), ("rb1", 1), ("rw2", NE),
    ("rb2", NE), ("ew1", 384), ("eb1", 3), ("ew2", 384), ("eb2", 3), ("ew3", 192), ("eb3", 64),
    ("spread", 384),
])

Q_STEPS = 41
S_STEPS = 37
B_STEPS = 218
UNITS = L1H * NT


def tower(nc, xq, table, packed, out):
    nb = xq.shape[0]
    ctx = ExitStack()
    with ctx:
        def sb(name, shape, dt=F32):
            return ctx.enter_context(nc.sbuf_tensor(name, shape, dt))

        def sem(name):
            return ctx.enter_context(nc.semaphore(name))

        bank = [ctx.enter_context(nc.psum_tensor(f"bank{i}", [P, 512], F32)) for i in range(8)]

        consts = sb("consts", [P, WIDTH])

        def con(name, rows=P):
            a, z = COLS[name]
            return consts[0:rows, a:z]

        gathered = sb("gathered", [P, NT, NPT * 4 * C])
        cells_q = sb("cells_q", [P, NT, 4, C])
        corner_w = sb("corner_w", [P, NT * NPT, 4])
        cell_idx = sb("cell_idx", [P, NT * NPT], U32)
        base_cell = sb("base_cell", [P, 1])
        queries = sb("queries", [P, NT, C])
        values = sb("values", [P, NT, NPT * C])
        samples = sb("samples", [P, 2, NPT * C])
        samples_t = sb("samples_t", [P, 2, 512])
        work = sb("work", [P, 6144])
        feats = sb("feats", [P, 1024])
        prod = sb("prod", [P, 512])
        score = sb("score", [P, 512])
        h = sb("h", [P, NT * C])
        z = sb("z", [P, NT * C])
        sq = sb("sq", [P, NT * C])
        small = sb("small", [P, 24, 64])
        qs = sb("qs", [P, 12, 128])
        wsum = sb("wsum", [P, 64])
        w_lin = sb("w_lin", [P, 64])
        ctx_m = sb("ctx_m", [P, 128])
        emk = sb("emk", [P, NMEM])
        emk_t = sb("emk_t", [NMEM, 128])
        gates = sb("gates", [P, NT, NE])

        loaded = sem("consts_loaded")
        const_ready = sem("const_ready")
        qcells = sem("qcells_loaded")
        q_step = sem("q_step")
        s_step = sem("s_step")
        b_step = sem("b_step")
        qfeat_ready = sem("qfeat_ready")
        q_pe = sem("q_pe_done")
        q_act = sem("q_act_done")
        q_read = sem("q_bank_read")
        offs_ready = sem("hidden_ready")
        idx_ready = sem("idx_ready")
        tile_gathered = [sem(f"tile_gathered{t}") for t in range(NT)]
        samp_ready = sem("samp_ready")
        samp_turned = sem("samp_turned")
        samp_copied = sem("samp_copied")
        kv_ready = sem("kv_ready")
        v_copied = sem("v_copied")
        k_used = sem("k_used")
        shifted = sem("score_shifted")
        exped = sem("score_exped")
        act_in = sem("to_pe")
        pe_out = sem("pe_result")
        act_out = sem("act_result")
        dve_act = sem("to_act")
        s_scores = sem("s_scores")
        s_rowmax = sem("s_rowmax")
        s_probs = sem("s_probs")
        s_pt_lo = sem("s_pt_lo")
        s_pt_hi = sem("s_pt_hi")
        s_pts_lo = sem("s_pts_lo")
        s_pts_hi = sem("s_pts_hi")
        s_av = sem("s_av")
        shifted_r = sem("router_shifted")
        exped_r = sem("router_exped")
        pe_passed = sem("pe_passed")
        pool_passed = sem("pool_passed")
        stored = sem("stored")
        out_free = sem("out_free")

        ident = con("ident")
        block = ctx.enter_context(nc.Block())

        def w(col0, width, rows=P):
            return work[0:rows, col0:col0 + width]

        PE_OUT = {n: k + 1 for k, n in enumerate([
            "x0T", "kT", "qv", "ek_tok", "ctxT", "lin_w", "q_tok", "lin_y",
            "x1T", "w_row", "w_col", "mlp_hid", "mlp_y",
            "x2T", "q1", "k1", "v1", "oT", "proj",
            "x3T", "router_h", "logits", "gate_t",
            "e1_0", "e2_0", "gb_0", "e1_1", "e2_1", "gb_1", "e1_2", "e2_2", "gb_2", "moe_y"])}
        ACT_OUT = {n: k + 1 for k, n in enumerate([
            "x0T", "ekT", "qv", "ek_tok", "q_exp", "q_tok",
            "x1T", "w_row", "mlp_hid",
            "x2T", "q1", "k1", "oT",
            "x3T", "router_h", "gate_t",
            "e1_0", "e2_0", "e1_1", "e2_1", "e1_2", "e2_2"])}
        TO_PE = {n: k + 1 for k, n in enumerate([
            "x0", "ctx", "lin_w", "q_soft", "x1", "x2", "v1", "o", "x3", "gates",
            "g_0", "g_1", "g_2"])}
        TO_ACT = {n: k + 1 for k, n in enumerate(["neg_kmax", "q_shift"])}

        @block.sync
        def _(sp):
            sp.dma_start(consts[:, :], packed).then_inc(loaded, 16)

            def load_cells(b, first):
                if not first:
                    sp.wait_ge(qfeat_ready, b)
                sp.dma_start(cells_q[:, :, :, :].rearrange("p t k c -> p (t k c)"),
                             xq[b]).then_inc(qcells, 16)

            def store(b):
                sp.wait_ge(b_step, b * B_STEPS + B_STEPS)
                sp.dma_start(out[b], h[:, :]).then_inc(stored, 16)
                sp.wait_ge(stored, 16 * b + 16)
                sp.sem_inc(out_free, 1)

            sp.sem_inc(out_free, 1)
            load_cells(0, True)
            with sp.Fori(0, nb - 1) as b:
                load_cells(b + 1, False)
                store(b)
            store(nb - 1)

        @block.gpsimd
        def _(pool):
            def gather(b, first):
                pool.wait_ge(idx_ready, b + 1)
                for t in range(NT):
                    if not first:
                        pool.wait_ge(samp_ready, (b - 1) * NT + t + 1)
                        pool.sem_inc(pool_passed, 1)
                    for p in range(NPT):
                        j = t * NPT + p
                        pool.indirect_dma_start(
                            out=gathered[:, t, p * 4 * C:(p + 1) * 4 * C], out_offset=None,
                            in_=table,
                            in_offset=bass.IndirectOffsetOnAxis(ap=cell_idx[:, j:j + 1], axis=0),
                        ).then_inc(tile_gathered[t], 16)

            gather(0, True)
            with pool.Fori(1, nb) as b:
                gather(b, False)

        @block.tensor
        def _(pe):
            pe.wait_ge(const_ready, 1)

            def alone():
                pe.sem_inc(pe_passed, 1)

            def turn_tiles(src, lo, hi):
                for t in range(NT):
                    dst = (lo if t < 4 else hi)[0:C, (t % 4) * P:(t % 4 + 1) * P]
                    last = nc.tensor.transpose(dst, src[:, t * C:(t + 1) * C], ident)
                return last

            def positions(b):
                k = b * 4
                a = b * 2
                pe.wait_ge(qfeat_ready, b + 1)
                alone()
                turn_tiles(sq, bank[0], bank[1]).then_inc(q_pe, 1)
                pe.wait_ge(q_act, a + 1)
                for t in range(NT):
                    last = nc.tensor.matmul(bank[t // 4][:, (t % 4) * 80:(t % 4 + 1) * 80],
                                            feats[0:C, t * P:(t + 1) * P], con("wq_o1", C),
                                            start=True, stop=True)
                last.then_inc(q_pe, 1)
                pe.wait_ge(offs_ready, b + 1)
                nc.tensor.transpose(bank[2][:, 0:P], qs[:, 1, :], ident).then_inc(q_pe, 1)
                pe.wait_ge(q_act, a + 2)
                nc.tensor.matmul(bank[3][:, 0:P], qs[:, 2, :], con("w_o2"),
                                 start=True, stop=True).then_inc(q_pe, 1)

            def sampling(b):
                def turn(t):
                    pe.wait_ge(samp_ready, b * NT + t + 1)
                    for g in range(4):
                        last = nc.tensor.transpose(bank[t % 2][:, g * P:(g + 1) * P],
                                                   samples[:, t % 2, g * P:(g + 1) * P], ident)
                    last.then_inc(samp_turned, 1)

                def project(t):
                    pe.wait_ge(samp_copied, b * NT + t + 1)
                    if t >= 2:
                        pe.wait_ge(k_used, b * NT + t - 1)
                        pe.wait_ge(v_copied, b * NT + t - 1)
                    for kv in range(2):
                        for g in range(4):
                            last = nc.tensor.matmul(bank[2 + 2 * (t % 2) + kv][:, g * P:(g + 1) * P],
                                                    samples_t[:, t % 2, g * P:(g + 1) * P],
                                                    con("w_kv")[:, kv * P:(kv + 1) * P],
                                                    start=True, stop=True)
                    last.then_inc(kv_ready, 1)

                for t in range(NT + 1):
                    if t < NT:
                        turn(t)
                    if t >= 1:
                        project(t - 1)

            def network(b):
                def given(sem_, table_, name):
                    pe.wait_ge(sem_, b * len(table_) + table_[name])

                def done(ins):
                    ins.then_inc(pe_out, 1)

                def turn_acts(src, ready):
                    given(act_in, TO_PE, ready)
                    alone()
                    done(turn_tiles(src, bank[0], bank[1]))

                def wide(weights, rows, lo, hi, src=None):
                    for n, bk in enumerate((lo, hi)):
                        moving = feats[0:C, n * 512:(n + 1) * 512] if src is None else src[:, n * 512:(n + 1) * 512]
                        last = nc.tensor.matmul(bk[0:rows, :], weights, moving, start=True, stop=True)
                    return last

                def per_tile(weights, width, dst):
                    for t in range(NT):
                        last = nc.tensor.matmul(dst[:, t * width:(t + 1) * width],
                                                feats[0:C, t * P:(t + 1) * P], weights,
                                                start=True, stop=True)
                    return last

                turn_acts(z, "x0")
                given(act_out, ACT_OUT, "x0T")
                wq = con("w_qkv", C)
                done(wide(wq[:, 128:256], P, bank[6], bank[7]))
                for t in range(NT):
                    for part, c0 in ((0, 0), (1, 256)):
                        last = nc.tensor.matmul(
                            bank[2 + t // 2][:, (t % 2) * 256 + part * 128:(t % 2) * 256 + part * 128 + 128],
                            feats[0:C, t * P:(t + 1) * P], wq[:, c0:c0 + 128], start=True, stop=True)
                done(last)
                qv, ek_t, ek, q_soft, q_t = w(0, 2048), w(2048, 1024), w(3072, 1024), w(4096, 1024), w(5120, 1024)
                given(act_out, ACT_OUT, "ekT")
                for t in range(NT):
                    nc.tensor.transpose(bank[t // 4][:, (t % 4) * P:(t % 4 + 1) * P],
                                        ek_t[:, t * P:(t + 1) * P], ident)
                done(nc.tensor.transpose(bank[6][0:NMEM, 0:P], emk[:, :], ident))
                given(act_out, ACT_OUT, "ek_tok")
                for t in range(NT):
                    nc.tensor.matmul(bank[2][:, 0:P], qv[:, t * 256 + 128:t * 256 + 256],
                                     ek[:, t * P:(t + 1) * P], start=(t == 0), stop=False)
                done(nc.tensor.matmul(bank[2][:, 0:P], con("mem_v", NMEM), emk_t[:, :],
                                      start=False, stop=True))
                given(act_in, TO_PE, "ctx")
                done(nc.tensor.matmul(bank[3][:, 0:C], ctx_m[:, :], con("w_out"), start=True, stop=True))
                given(act_in, TO_PE, "q_soft")
                for t in range(NT):
                    last = nc.tensor.transpose(bank[4 + t // 4][:, (t % 4) * P:(t % 4 + 1) * P],
                                               q_soft[:, t * P:(t + 1) * P], ident)
                done(last)
                given(act_out, ACT_OUT, "q_tok")
                for t in range(NT):
                    last = nc.tensor.matmul(bank[6][:, t * C:(t + 1) * C], q_t[:, t * P:(t + 1) * P],
                                            w_lin[:, :], start=True, stop=True)
                done(last)

                turn_acts(h, "x1")
                given(act_out, ACT_OUT, "x1T")
                done(wide(con("wr", C), P, bank[2], bank[3]))
                w_row = w(2048, 1024)
                given(act_out, ACT_OUT, "w_row")
                alone()
                for t in range(NT):
                    last = nc.tensor.transpose(bank[4][:, t:t + 1], w_row[0:1, t * P:(t + 1) * P],
                                               ident[0:1, 0:1])
                done(last)
                for half in range(2):
                    last = wide(con("w1", C)[:, half * P:(half + 1) * P], P,
                                bank[(5, 7)[half]], bank[(6, 0)[half]])
                done(last)
                given(act_out, ACT_OUT, "mlp_hid")
                for t in range(NT):
                    for half in range(2):
                        last = nc.tensor.matmul(bank[1][:, t * C:(t + 1) * C],
                                                w(0, 2048)[:, half * 1024 + t * P:half * 1024 + (t + 1) * P],
                                                con("w2")[:, half * C:(half + 1) * C],
                                                start=(half == 0), stop=(half == 1))
                done(last)

                turn_acts(h, "x2")
                given(act_out, ACT_OUT, "x2T")
                done(wide(con("w_q1", C), P, bank[2], bank[3]))
                done(wide(con("w_k1", C), P, bank[4], bank[5]))
                done(per_tile(con("w_v1", C), C, bank[6]))
                given(act_out, ACT_OUT, "k1")
                given(act_in, TO_PE, "v1")
                q1, k1, probs, probs_t = w(0, 1024), w(1024, 1024), w(2048, 2048), w(4096, 2048)

                def scores(u):
                    hd, qt = divmod(u, NT)
                    width = (qt + 1) * P
                    rows = slice(32 * hd, 32 * hd + L1D)
                    for n in range((width + 511) // 512):
                        cols = min(512, width - n * 512)
                        diag = n == (width - 1) // 512
                        bk = bank[2 * (u % 2) + n]
                        last = nc.tensor.matmul(bk[:, 0:cols], q1[rows, qt * P:(qt + 1) * P],
                                                k1[rows, n * 512:n * 512 + cols], start=True, stop=not diag)
                        if diag:
                            at = qt * P - n * 512
                            last = nc.tensor.matmul(bk[:, at:at + P], ident, con("neg_mask"),
                                                    start=False, stop=True)
                    last.then_inc(s_scores, 1)

                def turn_probs(u):
                    qt = u % NT
                    pe.wait_ge(s_probs, b * UNITS + u + 1)
                    src = probs[:, (u % 2) * 1024:(u % 2 + 1) * 1024]
                    if qt >= 4:
                        for kt in range(4, qt + 1):
                            last = nc.tensor.transpose(bank[5][:, (kt - 4) * P:(kt - 3) * P],
                                                       src[:, kt * P:(kt + 1) * P], ident)
                        last.then_inc(s_pt_hi, 1)
                    for kt in range(min(4, qt + 1)):
                        last = nc.tensor.transpose(bank[4][:, kt * P:(kt + 1) * P],
                                                   src[:, kt * P:(kt + 1) * P], ident)
                    last.then_inc(s_pt_lo, 1)

                def attend(u):
                    hd, qt = divmod(u, NT)
                    pe.wait_ge(s_pts_lo, b * UNITS + u + 1)
                    if qt >= 4:
                        pe.wait_ge(s_pts_hi, b * (UNITS // 2) + hd * 4 + qt - 3)
                    src = probs_t[:, (u % 2) * 1024:(u % 2 + 1) * 1024]
                    dst = bank[7][:, qt * C + hd * L1D:qt * C + (hd + 1) * L1D]
                    for kt in range(qt + 1):
                        last = nc.tensor.matmul(dst, src[:, kt * P:(kt + 1) * P],
                                                z[:, kt * C + hd * L1D:kt * C + (hd + 1) * L1D],
                                                start=(kt == 0), stop=(kt == qt))
                    last.then_inc(s_av, 1)

                scores(0)
                scores(1)
                for u in range(UNITS):
                    turn_probs(u)
                    if u + 2 < UNITS:
                        scores(u + 2)
                    attend(u)
                given(act_in, TO_PE, "o")
                alone()
                done(turn_tiles(sq, bank[0], bank[1]))
                given(act_out, ACT_OUT, "oT")
                done(per_tile(con("w_proj", C), C, bank[2]))

                turn_acts(h, "x3")
                given(act_out, ACT_OUT, "x3T")
                alone()
                done(wide(con("rw1", C), 32, bank[2], bank[3]))
                a1, a2, r_h, g_t = w(0, 1024), w(1024, 3072), w(4096, 1024), w(5120, 1024)
                given(act_out, ACT_OUT, "router_h")
                for t in range(NT):
                    last = nc.tensor.matmul(bank[4][:, t * NE:(t + 1) * NE], r_h[0:32, t * P:(t + 1) * P],
                                            con("rw2", 32), start=True, stop=True)
                done(last)
                given(act_in, TO_PE, "gates")
                for t in range(NT):
                    last = nc.tensor.transpose(bank[5 + t // 4][0:NE, (t % 4) * P:(t % 4 + 1) * P],
                                               gates[:, t, :], ident)
                done(last)
                given(act_out, ACT_OUT, "gate_t")
                for pr in range(3):
                    done(wide(con("ew1", C)[:, pr * P:(pr + 1) * P], P, bank[0], bank[1]))
                    given(act_out, ACT_OUT, f"e1_{pr}")
                    done(wide(con("ew2")[:, pr * P:(pr + 1) * P], P, bank[2], bank[3], src=a1))
                    if pr:
                        given(act_in, TO_PE, f"g_{pr - 1}")
                    done(wide(con("spread", NE)[:, pr * P:(pr + 1) * P], P, bank[5], bank[6],
                              src=g_t[0:NE, :]))
                    if pr < 2:
                        given(act_out, ACT_OUT, f"e2_{pr}")
                given(act_in, TO_PE, "g_2")
                for t in range(NT):
                    dst = bank[7][:, t * C:(t + 1) * C]
                    for pr in range(3):
                        nc.tensor.matmul(dst, a2[:, pr * 1024 + t * P:pr * 1024 + (t + 1) * P],
                                         con("ew3")[:, pr * C:(pr + 1) * C], start=(pr == 0), stop=False)
                    last = nc.tensor.matmul(dst, g_t[0:NE, t * P:(t + 1) * P], con("eb3", NE),
                                            start=False, stop=True)
                done(last)

            positions(0)
            with pe.Fori(0, nb - 1) as b:
                sampling(b)
                positions(b + 1)
                network(b)
            sampling(nb - 1)
            network(nb - 1)

        @block.scalar
        def _(act):
            act.wait_ge(const_ready, 1)

            def positions(b):
                k = b * 4
                act.wait_ge(q_pe, k + 1)
                nc.scalar.copy(feats[0:C, 0:512], bank[0][0:C, :])
                nc.scalar.copy(feats[0:C, 512:1024], bank[1][0:C, :]).then_inc(q_act, 1)
                act.wait_ge(q_read, b + 1)
                nc.scalar.activation(qs[:, 1, :], qs[:, 0, :], ACT.Gelu_apprx_tanh).then_inc(offs_ready, 1)
                act.wait_ge(q_pe, k + 3)
                nc.scalar.copy(qs[:, 2, :], bank[2][:, 0:P]).then_inc(q_act, 1)

            def sampling(b):
                def copy_turned(t):
                    act.wait_ge(samp_turned, b * NT + t + 1)
                    nc.scalar.copy(samples_t[:, t % 2, :], bank[t % 2][:, :]).then_inc(samp_copied, 1)

                def copy_values(t):
                    act.wait_ge(kv_ready, b * NT + t + 1)
                    nc.scalar.copy(values[:, t, :], bank[3 + 2 * (t % 2)][:, :]).then_inc(v_copied, 1)

                for t in range(NT + 1):
                    if t < NT:
                        copy_turned(t)
                    if t >= 1:
                        copy_values(t - 1)
                act.wait_ge(shifted, b + 1)
                nc.scalar.activation(score[:, :], score[:, :], ACT.Exp,
                                     scale=float(C // NPT) ** -0.5).then_inc(exped, 1)

            def network(b):
                def pe_gave(name):
                    act.wait_ge(pe_out, b * len(PE_OUT) + PE_OUT[name])

                def done(ins):
                    ins.then_inc(act_out, 1)

                def copy_feats(name):
                    pe_gave(name)
                    nc.scalar.copy(feats[0:C, 0:512], bank[0][0:C, :])
                    done(nc.scalar.copy(feats[0:C, 512:1024], bank[1][0:C, :]))

                def copy_pair(dst, lo, hi, rows=P):
                    nc.scalar.copy(dst[:, 0:512], lo[0:rows, :])
                    return nc.scalar.copy(dst[:, 512:1024], hi[0:rows, :])

                def mapped(dst, lo, hi, func, bias, rows=P, scale=1.0):
                    nc.scalar.activation(dst[:, 0:512], lo[0:rows, :], func, bias=bias, scale=scale)
                    return nc.scalar.activation(dst[:, 512:1024], hi[0:rows, :], func, bias=bias, scale=scale)

                copy_feats("x0T")
                act.wait_ge(dve_act, b * len(TO_ACT) + TO_ACT["neg_kmax"])
                neg = small[:, 3, 3:4]
                nc.scalar.activation(w(2048, 512), bank[6][:, :], ACT.Exp, bias=neg, accum_out=wsum[:, 0:1])
                nc.scalar.activation(w(2560, 512), bank[7][:, :], ACT.Exp, bias=neg, accum_out=wsum[:, 1:2])
                done(nc.scalar.activation(emk[:, :], con("mem_k"), ACT.Exp, bias=neg, accum_out=wsum[:, 2:3]))
                pe_gave("qv")
                for g in range(4):
                    last = nc.scalar.copy(w(g * 512, 512), bank[2 + g][:, :])
                done(last)
                pe_gave("ek_tok")
                copy_pair(w(3072, 1024), bank[0], bank[1])
                done(nc.scalar.copy(emk_t[:, :], bank[6][0:NMEM, 0:P]))
                act.wait_ge(dve_act, b * len(TO_ACT) + TO_ACT["q_shift"])
                done(nc.scalar.activation(w(4096, 1024), w(4096, 1024), ACT.Exp))
                pe_gave("q_tok")
                done(copy_pair(w(5120, 1024), bank[4], bank[5]))

                copy_feats("x1T")
                pe_gave("w_row")
                done(mapped(w(2048, 1024), bank[2], bank[3], ACT.Identity, con("br")))
                pe_gave("mlp_hid")
                for half in range(2):
                    last = mapped(w(half * 1024, 1024), bank[(5, 7)[half]], bank[(6, 0)[half]],
                                  ACT.Gelu_apprx_tanh, con("b1")[:, half:half + 1])
                done(last)

                copy_feats("x2T")
                pe_gave("q1")
                done(mapped(w(0, 1024), bank[2], bank[3], ACT.Identity, con("b_q1"), scale=L1D ** -0.5))
                pe_gave("k1")
                done(mapped(w(1024, 1024), bank[4], bank[5], ACT.Identity, con("b_k1")))

                def exponentiate(u):
                    width = (u % NT + 1) * P
                    act.wait_ge(s_rowmax, b * UNITS + u + 1)
                    dst = w(2048 + (u % 2) * 1024, 1024)
                    lo = min(512, width)
                    last = nc.scalar.activation(dst[:, 0:lo], bank[2 * (u % 2)][:, 0:lo], ACT.Exp,
                                                bias=small[:, 4, u:u + 1], accum_out=small[:, 5, u:u + 1])
                    if width > 512:
                        last = nc.scalar.activation(dst[:, 512:width], bank[2 * (u % 2) + 1][:, 0:width - 512],
                                                    ACT.Exp, bias=small[:, 4, u:u + 1],
                                                    accum_out=small[:, 6, u:u + 1])
                    last.then_inc(s_probs, 1)

                def copy_turned(u):
                    cols = min(4, u % NT + 1) * P
                    act.wait_ge(s_pt_lo, b * UNITS + u + 1)
                    nc.scalar.copy(w(4096 + (u % 2) * 1024, cols), bank[4][:, 0:cols]).then_inc(s_pts_lo, 1)

                exponentiate(0)
                exponentiate(1)
                for u in range(UNITS):
                    copy_turned(u)
                    if u + 2 < UNITS:
                        exponentiate(u + 2)
                copy_feats("oT")

                copy_feats("x3T")
                pe_gave("router_h")
                done(mapped(w(4096, 1024, 32), bank[2], bank[3], ACT.Relu, con("rb1", 32), rows=32))
                lg, d21 = small[:, 11, 0:48], small[:, 15, 24:32]
                for k, x in enumerate((lg, d21)):
                    act.wait_ge(shifted_r, b * 2 + k + 1)
                    nc.scalar.activation(x, x, ACT.Exp).then_inc(exped_r, 1)
                pe_gave("gate_t")
                done(copy_pair(w(5120, 1024, NE), bank[5], bank[6], rows=NE))
                for pr in range(3):
                    pe_gave(f"e1_{pr}")
                    done(mapped(w(0, 1024), bank[0], bank[1], ACT.Relu, con("eb1")[:, pr:pr + 1]))
                    pe_gave(f"e2_{pr}")
                    done(mapped(w(1024 + pr * 1024, 1024), bank[2], bank[3], ACT.Relu,
                                con("eb2")[:, pr:pr + 1]))

            positions(0)
            with act.Fori(0, nb - 1) as b:
                sampling(b)
                positions(b + 1)
                network(b)
            sampling(nb - 1)
            network(nb - 1)

        @block.vector
        def _(dve):
            v = nc.vector

            class Steps:

                def __init__(self, sem_, base):
                    self.sem, self.base, self.n = sem_, base, 0

                def __call__(self, ins):
                    self.n += 1
                    ins.then_inc(self.sem, 1)
                    dve.wait_ge(self.sem, self.base + self.n)

                def end(self, per, what):
                    assert self.n == per, (what, self.n)

            def v3(ap, a):
                return ap.rearrange("p (a c) -> p a c", a=a)

            def rows_of(ap, n, m):
                return ap.unsqueeze(1).to_broadcast([P, n, m])

            def over(ap, m):
                return ap.unsqueeze(2).to_broadcast([P, ap.shape[1], m])

            def inverse_root(step, x, n):
                y, half, t = small[:, 20, 0:n], small[:, 21, 0:n], small[:, 22, 0:n]
                step(v.tensor_scalar(y.bitcast(I32), x.bitcast(I32), -0.5, 1597463007.0, ALU.mult, ALU.add))
                step(v.tensor_scalar(half, x, -0.5, None, ALU.mult))
                for last in (False, False, True):
                    step(v.tensor_tensor(t, y, y, ALU.mult))
                    step(v.tensor_tensor(t, t, half, ALU.mult))
                    step(v.scalar_tensor_tensor(x if last else y, t, 1.5, y, ALU.add, ALU.mult))

            def layernorm(step, x, dst, groups, width):
                s, d = small[:, 0, 0:groups], v3(x, groups)
                step(v.tensor_reduce(s, d, AX.X, ALU.add))
                step(v.tensor_scalar(s, s, 1.0 / width, None, ALU.mult))
                step(v.tensor_tensor(d, d, over(s, width), ALU.subtract))
                q = v3(sq[:, 0:groups * width], groups)
                step(v.tensor_tensor(q, d, d, ALU.mult))
                step(v.tensor_reduce(s, q, AX.X, ALU.add))
                step(v.tensor_scalar(s, s, 1.0 / width, 1e-5, ALU.mult, ALU.add))
                inverse_root(step, s, groups)
                return v.tensor_tensor(v3(dst, groups), d, over(s, width), ALU.mult)

            def inverse_norm(step, x):
                s = small[:, 0, 0:NT]
                step(v.tensor_tensor(sq[:, :], x, x, ALU.mult))
                step(v.tensor_reduce(s, v3(sq[:, :], NT), AX.X, ALU.add))
                step(v.tensor_scalar(s, s, 1e-24, None, ALU.max))
                inverse_root(step, s, NT)
                return s

            def prepare():
                dve.wait_ge(loaded, 16)
                v.tensor_scalar(con("w_qkv", C), con("w_qkv", C), con("g_pre", C), float(C) ** 0.5,
                                ALU.mult, ALU.mult)
                v.tensor_scalar(con("g_out"), con("g_out"), float(C) ** 0.5, None, ALU.mult)
                v.tensor_scalar(con("b_q1"), con("b_q1"), L1D ** -0.5, None, ALU.mult)
                v.tensor_reduce(small[:, 23, 0:1], con("mem_k"), AX.X, ALU.max)
                v.memset(base_cell[:, :], 0.0).then_inc(const_ready, 1)
                dve.wait_ge(const_ready, 1)

            def positions(b):
                step = Steps(q_step, b * Q_STEPS)
                dve.wait_ge(qcells, 16 * b + 16)
                cw = con("q_corner").unsqueeze(2).to_broadcast([P, NT * 4, C])
                c3 = cells_q[:, :, :, :].rearrange("p t k c -> p (t k) c")
                step(v.tensor_tensor(c3, c3, cw, ALU.mult))
                c4 = cells_q[:, :, :, :].rearrange("p t (y x) c -> p t y (x c)", y=2)
                step(v.tensor_tensor(c4[:, :, 0, :], c4[:, :, 0, :], c4[:, :, 1, :], ALU.add))
                v.tensor_tensor(v3(sq[:, :], NT), cells_q[:, :, 0, :], cells_q[:, :, 1, :],
                                ALU.add).then_inc(qfeat_ready, 1)
                dve.wait_ge(q_pe, b * 4 + 2)
                for g in range(2):
                    src = bank[g][:, 0:320].rearrange("p (t c) -> p t c", t=4)
                    step(v.tensor_copy(queries[:, 4 * g:4 * g + 4, :], src[:, :, 0:C]))
                    step(v.tensor_tensor(v3(qs[:, 0, g * 64:(g + 1) * 64], 4), src[:, :, C:C + 16],
                                         rows_of(con("b_o1"), 4, 16), ALU.add))
                hid = qs[:, 0, :]
                step(layernorm(step, hid, hid, NT, 16))
                step(v.tensor_tensor(v3(hid, NT), v3(hid, NT), rows_of(con("ln_g"), NT, 16), ALU.mult))
                v.tensor_tensor(v3(hid, NT), v3(hid, NT), rows_of(con("ln_b"), NT, 16),
                                ALU.add).then_inc(q_read, 1)
                dve.wait_ge(q_pe, b * 4 + 4)
                px, cl, fl, ge, wt, om = (qs[:, k, :] for k in range(3, 9))
                step(v.tensor_tensor(v3(px, NT), v3(bank[3][:, 0:P], NT), rows_of(con("b_o2"), NT, 16), ALU.add))
                step(v.scalar_tensor_tensor(px, px, 4.0, con("ref_xy"), ALU.mult, ALU.add))
                step(v.tensor_scalar(cl, px, 0.0, float(SIDE - 2), ALU.max, ALU.min))
                whole = qs[:, 9, :].bitcast(I32)
                step(v.tensor_copy(whole, cl))
                step(v.tensor_copy(fl, whole))
                step(v.tensor_tensor(ge, fl, cl, ALU.is_gt))
                step(v.tensor_tensor(fl, fl, ge, ALU.subtract))
                step(v.tensor_tensor(wt, px, fl, ALU.subtract))
                step(v.tensor_scalar(wt, wt, 0.0, 1.0, ALU.max, ALU.min))
                step(v.tensor_scalar(om, wt, -1.0, 1.0, ALU.mult, ALU.add))
                cell = qs[:, 10, 0:64]
                step(v.scalar_tensor_tensor(cell, fl[:, 1:128:2], float(CELLS), fl[:, 0:128:2], ALU.mult, ALU.add))
                v.tensor_scalar(cell_idx[:, :], cell, base_cell[:, 0:1], None, ALU.add).then_inc(idx_ready, 1)
                for k, (fy, fx) in enumerate(((om, om), (om, wt), (wt, om), (wt, wt))):
                    step(v.tensor_tensor(corner_w[:, :, k], fy[:, 1:128:2], fx[:, 0:128:2], ALU.mult))
                dve.wait_ge(idx_ready, b + 1)
                step(v.tensor_scalar(base_cell[:, :], base_cell[:, :], float(CELLS * CELLS), None, ALU.add))
                step.end(Q_STEPS, "Q_STEPS")

            def sampling(b):
                step = Steps(s_step, b * S_STEPS)

                def sum_corners(t):
                    dve.wait_ge(tile_gathered[t], b * (16 * NPT) + 16 * NPT)
                    g = gathered[:, t, :]
                    step(v.tensor_tensor(v3(g, 32), v3(g, 32),
                                         over(corner_w[:, t * NPT:(t + 1) * NPT, :]
                                              .rearrange("p a k -> p (a k)"), C), ALU.mult))
                    g4 = g.rearrange("p (s y c) -> p s y c", s=NPT, y=2)
                    step(v.tensor_tensor(g4[:, :, 0, :], g4[:, :, 0, :], g4[:, :, 1, :], ALU.add))
                    if t >= 2:
                        dve.wait_ge(samp_turned, b * NT + t - 1)
                    v.tensor_tensor(v3(samples[:, t % 2, :], NPT), g4[:, :, 0, 0:C], g4[:, :, 0, C:2 * C],
                                    ALU.add).then_inc(samp_ready, 1)

                def score_tile(t):
                    dve.wait_ge(kv_ready, b * NT + t + 1)
                    v.tensor_tensor(v3(prod[:, :], NPT), v3(bank[2 + 2 * (t % 2)][:, :], NPT),
                                    queries[:, t:t + 1, :].to_broadcast([P, NPT, C]),
                                    ALU.mult).then_inc(k_used, 1)
                    dve.wait_ge(k_used, b * NT + t + 1)
                    step(v.tensor_reduce(score[:, t * 64:(t + 1) * 64], v3(prod[:, :], 64), AX.X, ALU.add))

                for t in range(NT + 1):
                    if t < NT:
                        sum_corners(t)
                    if t >= 1:
                        score_tile(t - 1)
                s4 = score[:, :].rearrange("p (t s h) -> p t s h", t=NT, s=NPT)
                top, tot = small[:, 1, :], small[:, 2, :]
                step(v.tensor_reduce(v3(top, NT), score[:, :].rearrange("p (t s h) -> p t h s", t=NT, s=NPT),
                                     AX.X, ALU.max))
                tb = v3(top, NT).unsqueeze(2).to_broadcast([P, NT, NPT, NPT])
                v.tensor_tensor(s4, s4, tb, ALU.subtract).then_inc(shifted, 1)
                dve.wait_ge(exped, b + 1)
                step(v.tensor_reduce(v3(tot, NT), score[:, :].rearrange("p (t s h) -> p t h s", t=NT, s=NPT),
                                     AX.X, ALU.add))
                step(v.reciprocal(tot, tot))
                dve.wait_ge(v_copied, b * NT + NT)
                vals = values[:, :, :].rearrange("p t (s d) -> p (t s) d", s=64)
                step(v.tensor_tensor(vals, vals, over(score[:, :], 8), ALU.mult))
                for t in range(NT):
                    step(v.tensor_reduce(z[:, t * C:(t + 1) * C],
                                         values[:, t, :].rearrange("p (s c) -> p c s", s=NPT), AX.X, ALU.add))
                dve.wait_ge(out_free, b + 1)
                step(v.tensor_tensor(v3(h[:, :], 64), v3(z[:, :], 64), over(tot, 8), ALU.mult))
                step.end(S_STEPS, "S_STEPS")

            def network(b):
                step = Steps(b_step, b * B_STEPS)

                def to_pe(ins):
                    ins.then_inc(act_in, 1)

                def pe_gave(name):
                    dve.wait_ge(pe_out, b * len(PE_OUT) + PE_OUT[name])

                def act_gave(name):
                    dve.wait_ge(act_out, b * len(ACT_OUT) + ACT_OUT[name])

                s = inverse_norm(step, h[:, :])
                to_pe(v.tensor_tensor(v3(z[:, :], NT), v3(h[:, :], NT), over(s, C), ALU.mult))
                pe_gave("kT")
                km = small[:, 3, :]
                step(v.tensor_reduce(km[:, 0:1], bank[6][:, :], AX.X, ALU.max))
                step(v.tensor_reduce(km[:, 1:2], bank[7][:, :], AX.X, ALU.max))
                step(v.tensor_copy(km[:, 2:3], small[:, 23, 0:1]))
                v.tensor_reduce(km[:, 3:4], km[:, 0:3], AX.X, ALU.max, negate=True).then_inc(dve_act, 1)
                act_gave("qv")
                qv = w(0, 2048).rearrange("p (t m) -> p t m", t=NT)[:, :, 0:128]
                q_soft = w(4096, 1024)
                qm = small[:, 7, 0:32]
                q4 = qv.rearrange("p t (a d) -> p t a d", a=L0H)
                step(v.tensor_reduce(v3(qm, NT), q4, AX.X, ALU.max))
                qm4 = v3(qm, NT).unsqueeze(3).to_broadcast([P, NT, L0H, L0D])
                v.tensor_tensor(q_soft.rearrange("p (t a d) -> p t a d", t=NT, a=L0H), q4, qm4,
                                ALU.subtract).then_inc(dve_act, 1)
                pe_gave("ctxT")
                to_pe(v.tensor_tensor(ctx_m[:, :], bank[2][:, 0:P], con("head_mask"), ALU.mult))
                step(v.tensor_reduce(small[:, 8, 0:1], wsum[:, 0:3], AX.X, ALU.add))
                step(v.reciprocal(small[:, 8, 0:1], small[:, 8, 0:1]))
                pe_gave("lin_w")
                to_pe(v.tensor_scalar(w_lin[:, :], bank[3][:, 0:C], small[:, 8, 0:1], L0D ** -0.5,
                                      ALU.mult, ALU.mult))
                act_gave("q_exp")
                step(v.tensor_reduce(qm, v3(q_soft, 32), AX.X, ALU.add))
                step(v.reciprocal(qm, qm))
                to_pe(v.tensor_tensor(v3(q_soft, 32), v3(q_soft, 32), over(qm, L0D), ALU.mult))
                pe_gave("lin_y")
                step(v.tensor_tensor(v3(z[:, :], NT), v3(bank[6][:, :], NT), rows_of(con("b_out"), NT, C), ALU.add))
                s = inverse_norm(step, z[:, :])
                step(v.tensor_tensor(v3(z[:, :], NT), v3(z[:, :], NT), over(s, C), ALU.mult))
                step(v.tensor_tensor(v3(z[:, :], NT), v3(z[:, :], NT), rows_of(con("g_out"), NT, C), ALU.mult))
                step(v.scalar_tensor_tensor(z[:, :], h[:, :], 2.0, z[:, :], ALU.mult, ALU.add))
                to_pe(layernorm(step, z[:, :], h[:, :], NT, C))

                pe_gave("w_col")
                wc, rank = small[:, 9, 0:NT], small[:, 10, :]
                step(v.tensor_copy(wc, bank[4][:, 0:NT]))
                w_row, junk = w(2048, 1024), w(3072, 1024)
                step(v.memset(rank, 0.0))
                for t in range(NT):
                    step(v.tensor_scalar(junk[:, t * P:N], w_row[:, t * P:N], wc[:, t:t + 1], None,
                                         ALU.is_gt, ALU.add, accum_out=rank[:, t:t + 1]))
                    if t:
                        step(v.tensor_scalar(junk[:, 0:t * P], w_row[:, 0:t * P], wc[:, t:t + 1], None,
                                             ALU.is_ge, ALU.add, accum_out=rank[:, 8 + t:9 + t]))
                    step(v.tensor_scalar(junk[:, 0:P], w_row[:, t * P:(t + 1) * P], wc[:, t:t + 1], None,
                                         ALU.is_equal))
                    step(v.tensor_tensor(junk[:, 0:P], junk[:, 0:P], con("lower"), ALU.mult))
                    step(v.tensor_reduce(rank[:, 16 + t:17 + t], junk[:, 0:P], AX.X, ALU.add))
                step(v.tensor_tensor(rank[:, 0:8], rank[:, 0:8], rank[:, 8:16], ALU.add))
                step(v.tensor_tensor(rank[:, 0:8], rank[:, 0:8], rank[:, 16:24], ALU.add))
                step(v.scalar_tensor_tensor(wc, rank[:, 0:8], float(KEEP), wc, ALU.is_lt, ALU.mult))
                pe_gave("mlp_y")
                step(v.tensor_tensor(v3(z[:, :], NT), v3(bank[1][:, :], NT), rows_of(con("b2"), NT, C), ALU.add))
                step(v.tensor_tensor(v3(z[:, :], NT), v3(z[:, :], NT), over(wc, C), ALU.mult))
                step(v.scalar_tensor_tensor(z[:, :], h[:, :], 2.0, z[:, :], ALU.mult, ALU.add))
                to_pe(layernorm(step, z[:, :], h[:, :], NT, C))

                pe_gave("v1")
                to_pe(v.tensor_tensor(v3(z[:, :], NT), v3(bank[6][:, :], NT), rows_of(con("b_v1"), NT, C), ALU.add))
                step(v.memset(small[:, 6, 0:UNITS], 0.0))

                def row_max(u):
                    width = (u % NT + 1) * P
                    dve.wait_ge(s_scores, b * UNITS + u + 1)
                    if width <= 512:
                        v.tensor_reduce(small[:, 4, u:u + 1], bank[2 * (u % 2)][:, 0:width], AX.X, ALU.max,
                                        negate=True).then_inc(s_rowmax, 1)
                    else:
                        k = 32 + 2 * (u % 2)
                        pair = small[:, 4, k:k + 2]
                        step(v.tensor_reduce(pair[:, 0:1], bank[2 * (u % 2)][:, :], AX.X, ALU.max))
                        step(v.tensor_reduce(pair[:, 1:2], bank[2 * (u % 2) + 1][:, 0:width - 512], AX.X, ALU.max))
                        v.tensor_reduce(small[:, 4, u:u + 1], pair, AX.X, ALU.max,
                                        negate=True).then_inc(s_rowmax, 1)

                def copy_turned(u):
                    hd, qt = divmod(u, NT)
                    if qt >= 4:
                        cols = (qt - 3) * P
                        dve.wait_ge(s_pt_hi, b * (UNITS // 2) + hd * 4 + qt - 3)
                        v.tensor_copy(w(4096 + (u % 2) * 1024 + 512, cols), bank[5][:, 0:cols]).then_inc(s_pts_hi, 1)

                row_max(0)
                row_max(1)
                for u in range(UNITS):
                    copy_turned(u)
                    if u + 2 < UNITS:
                        row_max(u + 2)
                dve.wait_ge(s_av, b * UNITS + UNITS)
                tot = small[:, 5, 0:UNITS]
                step(v.tensor_tensor(tot, tot, small[:, 6, 0:UNITS], ALU.add))
                step(v.reciprocal(tot, tot))
                o4 = bank[7][:, :].rearrange("p (t a d) -> p t a d", t=NT, a=L1H)
                r4 = tot.rearrange("p (a t) -> p t a", t=NT).unsqueeze(3).to_broadcast([P, NT, L1H, L1D])
                to_pe(v.tensor_tensor(sq[:, :].rearrange("p (t a d) -> p t a d", t=NT, a=L1H), o4, r4, ALU.mult))
                pe_gave("proj")
                step(v.tensor_tensor(v3(z[:, :], NT), v3(bank[2][:, :], NT), rows_of(con("b_proj"), NT, C), ALU.add))
                step(v.tensor_tensor(z[:, :], z[:, :], h[:, :], ALU.add))
                to_pe(layernorm(step, z[:, :], h[:, :], NT, C))

                pe_gave("logits")
                lg, e1, e2, tmp = (small[:, k, 0:48] for k in (11, 12, 13, 14))
                m1, m2, i1, d21 = (small[:, 15, k * 8:k * 8 + 8] for k in range(4))
                iota = rows_of(con("iota_e"), NT, NE)
                step(v.tensor_tensor(v3(lg, NT), v3(bank[4][:, 0:48], NT), rows_of(con("rb2"), NT, NE), ALU.add))
                step(v.tensor_reduce(m1, v3(lg, NT), AX.X, ALU.max))
                v.tensor_tensor(v3(lg, NT), v3(lg, NT), over(m1, NE), ALU.subtract).then_inc(shifted_r, 1)
                dve.wait_ge(exped_r, b * 2 + 1)
                step(v.tensor_reduce(m1, v3(lg, NT), AX.X, ALU.add))
                step(v.reciprocal(m1, m1))
                step(v.tensor_tensor(v3(lg, NT), v3(lg, NT), over(m1, NE), ALU.mult))

                def pick(onehot, best):
                    step(v.tensor_reduce(best, v3(lg, NT), AX.X, ALU.max))
                    step(v.tensor_tensor(v3(tmp, NT), v3(lg, NT), over(best, NE), ALU.is_lt))
                    step(v.scalar_tensor_tensor(v3(tmp, NT), v3(tmp, NT), float(2 * NE), iota, ALU.mult, ALU.add))
                    step(v.tensor_reduce(i1, v3(tmp, NT), AX.X, ALU.min))
                    step(v.tensor_tensor(v3(onehot, NT), iota, over(i1, NE), ALU.is_equal))

                pick(e1, m1)
                step(v.scalar_tensor_tensor(lg, e1, -2.0, lg, ALU.mult, ALU.add))
                pick(e2, m2)
                v.tensor_tensor(d21, m2, m1, ALU.subtract).then_inc(shifted_r, 1)
                dve.wait_ge(exped_r, b * 2 + 2)
                step(v.tensor_scalar(m1, d21, 1.0, None, ALU.add))
                step(v.reciprocal(m1, m1))
                step(v.tensor_tensor(m2, d21, m1, ALU.mult))
                step(v.tensor_tensor(v3(e1, NT), v3(e1, NT), over(m1, NE), ALU.mult))
                step(v.tensor_tensor(v3(e2, NT), v3(e2, NT), over(m2, NE), ALU.mult))
                to_pe(v.tensor_tensor(gates[:, :, :], v3(e1, NT), v3(e2, NT), ALU.add))
                for pr in range(3):
                    act_gave(f"e2_{pr}")
                    pe_gave(f"gb_{pr}")
                    a2 = w(1024 + pr * 1024, 1024)
                    step(v.tensor_tensor(a2[:, 0:512], a2[:, 0:512], bank[5][:, :], ALU.mult))
                    to_pe(v.tensor_tensor(a2[:, 512:1024], a2[:, 512:1024], bank[6][:, :], ALU.mult))
                pe_gave("moe_y")
                step(v.tensor_tensor(z[:, :], bank[7][:, :], h[:, :], ALU.add))
                step(layernorm(step, z[:, :], h[:, :], NT, C))
                step.end(B_STEPS, "B_STEPS")

            prepare()
            positions(0)
            with dve.Fori(0, nb - 1) as b:
                sampling(b)
                positions(b + 1)
                network(b)
            sampling(nb - 1)
            network(nb - 1)


def _rows(v, n=P):
    return np.broadcast_to(np.asarray(v).reshape(1, -1), (n, np.asarray(v).size))


def _blocks(mats):
    rows, cols = sum(m.shape[0] for m in mats), sum(m.shape[1] for m in mats)
    out = np.zeros((rows, cols), np.float32)
    r = c = 0
    for m in mats:
        out[r:r + m.shape[0], c:c + m.shape[1]] = m
        r, c = r + m.shape[0], c + m.shape[1]
    return out


def _apart(m):
    out = np.zeros((m.shape[0], P), np.float32)
    for a in range(L1H):
        out[:, 32 * a:32 * a + L1D] = m[:, a * L1D:(a + 1) * L1D]
    return out


def _shape_constants():
    line = np.linspace(-1.0, 1.0, GRID, dtype=np.float32)
    pix = (line + np.float32(1)) * np.float32(0.5) * np.float32(SIDE - 1)
    cell = np.clip(np.floor(pix), 0, SIDE - 2).astype(np.float32)
    frac = np.clip(pix - cell, 0, 1).astype(np.float32)
    tok = np.arange(N)
    gx, gy = tok % GRID, tok // GRID
    ref = np.tile(np.stack([pix[gx], pix[gy]], -1), (1, NPT))
    wx, wy = frac[gx], frac[gy]
    one = np.float32(1)
    corner = np.stack([(one - wx) * (one - wy), wx * (one - wy), (one - wx) * wy, wx * wy], -1)
    by_tile = lambda a: a.reshape(NT, P, -1).transpose(1, 0, 2).reshape(P, -1)
    i = np.arange(P)
    head = (i[:, None] // L0D == i[None, :] // L0D)
    spread = np.zeros((NE, 3 * P))
    for e in range(NE):
        spread[e, e * C:(e + 1) * C] = 1
    return cell.astype(np.int64), {
        "ident": np.eye(P), "neg_mask": np.where(i[None, :] > i[:, None], -1e30, 0.0),
        "lower": (i[None, :] < i[:, None]), "head_mask": head,
        "ref_xy": by_tile(ref), "q_corner": by_tile(corner), "iota_e": _rows(np.arange(NE)),
        "spread": spread,
    }


def _layout(a):
    cell, parts = _shape_constants()
    x = a["x"]
    nb = x.shape[0]
    xc = x.transpose(0, 2, 3, 1)
    cells = np.concatenate([xc[:, :-1, :-1], xc[:, :-1, 1:], xc[:, 1:, :-1], xc[:, 1:, 1:]], -1)
    table = cells.reshape(nb * CELLS * CELLS, 4 * C)
    xq = cells[:, cell][:, :, cell].reshape(nb, NT, P, 4 * C).transpose(0, 2, 1, 3)
    xq = np.ascontiguousarray(xq).reshape(nb, P, NT * 4 * C)
    kv = np.concatenate([_blocks([a[f"L0_tok_W_{m}"].T] * 2) for m in "kv"], 1)
    mem = a["L0_attn_mem_kv"]
    w3, b3 = a["L1_attn_Wqkv"], a["L1_attn_bqkv"]
    e1, e2, e3 = (a[f"L1_ffn_expert_w{k}"] for k in (1, 2, 3))
    pairs = range(0, NE, 2)
    parts.update({
        "wq_o1": np.concatenate([a["L0_tok_W_q"].T, a["L0_tok_W_o1"]], 1),
        "b_o1": _rows(a["L0_tok_b_o1"]), "ln_g": _rows(a["L0_tok_ln_g"]), "ln_b": _rows(a["L0_tok_ln_b"]),
        "w_o2": _blocks([a["L0_tok_W_o2"]] * NT), "b_o2": _rows(a["L0_tok_b_o2"]),
        "w_kv": kv, "w_qkv": a["L0_attn_w_qkv"], "g_pre": a["L0_attn_g_pre"][:, None],
        "mem_k": mem[0].reshape(P, NMEM), "mem_v": mem[1].reshape(P, NMEM).T,
        "w_out": a["L0_attn_w_out"], "b_out": _rows(a["L0_attn_b_out"]), "g_out": _rows(a["L0_attn_g_out"]),
        "wr": np.broadcast_to(a["L0_ffn_wr"], (C, P)), "br": _rows(a["L0_ffn_br"]),
        "w1": a["L0_ffn_w1"], "b1": a["L0_ffn_b1"].reshape(2, P).T,
        "w2": np.concatenate([a["L0_ffn_w2"][:P], a["L0_ffn_w2"][P:]], 1), "b2": _rows(a["L0_ffn_b2"]),
        "w_q1": _apart(w3[:, 0:C]), "w_k1": _apart(w3[:, C:2 * C]), "w_v1": w3[:, 2 * C:],
        "b_q1": _apart(b3[None, 0:C]).T, "b_k1": _apart(b3[None, C:2 * C]).T, "b_v1": _rows(b3[2 * C:]),
        "w_proj": a["L1_attn_Wproj"], "b_proj": _rows(a["L1_attn_bproj"]),
        "rw1": a["L1_ffn_router_w1"], "rb1": a["L1_ffn_router_b1"][:, None],
        "rw2": a["L1_ffn_router_w2"], "rb2": _rows(a["L1_ffn_router_b2"]),
        "ew1": e1.transpose(1, 0, 2).reshape(C, NE * C), "eb1": a["L1_ffn_expert_b1"].reshape(3, P).T,
        "ew2": np.concatenate([_blocks([e2[e], e2[e + 1]]) for e in pairs], 1),
        "eb2": a["L1_ffn_expert_b2"].reshape(3, P).T,
        "ew3": np.concatenate([e3[e:e + 2].reshape(P, C) for e in pairs], 1),
        "eb3": a["L1_ffn_expert_b3"],
    })
    packed = np.zeros((P, WIDTH), np.float32)
    for name, m in parts.items():
        lo, hi = COLS[name]
        assert m.shape[1] == hi - lo, name
        packed[:m.shape[0], lo:hi] = m
    return xq, table, packed


def kernel(**inputs):
    import concourse.bacc as _bacc
    from concourse.bass_utils import run_bass_kernel_spmd as _run

    xq, table, packed = _layout({k: np.asarray(v) for k, v in inputs.items()})
    nb = xq.shape[0]
    nc = _bacc.Bacc("TRN2", target_bir_lowering=False, num_devices=1)
    arrays, args = {}, []
    for name, a in (("cells", xq), ("table", table), ("weights", packed)):
        arrays[f"in_{name}_dram"] = a
        args.append(nc.dram_tensor(f"in_{name}_dram", a.shape, F32, kind="ExternalInput").ap())
    args.append(nc.dram_tensor("out_0_dram", (nb, P, NT * C), F32, kind="ExternalOutput").ap())
    tower(nc, *args)
    r = _run(nc, [arrays], core_ids=[0])
    got = r.results[0]["out_0_dram"]
    return np.ascontiguousarray(got.reshape(nb, P, NT, C).transpose(0, 2, 1, 3)).reshape(nb, N, C)
```

```python
from contextlib import ExitStack

import numpy as np

import concourse.bass as bass
from concourse import mybir

F32 = mybir.dt.float32
BF16 = mybir.dt.bfloat16
I32 = mybir.dt.int32
U32 = mybir.dt.uint32
ALU = mybir.AluOpType
ACT = mybir.ActivationFunctionType
AX = mybir.AxisListType

P = 128
NT = 8
C = 64
GRID = 32
SIDE = 128
CELLS = SIDE - 1
NPT = 8
L0H, L0D = 4, 32
L1H, L1D = 4, 16
NMEM = 4
NE = 6
KEEP = 511
N = P * NT


def pack_columns(parts):
    at, out = 0, {}
    for name, width in parts:
        out[name] = (at, at + width)
        at += width
    return out, at


COLS, WIDTH = pack_columns([
    ("ident", 128), ("neg_mask", 128), ("lower", 128), ("head_mask", 128),
    ("ref_xy", NT * NPT * 2), ("q_corner", NT * 4), ("iota_e", NE),
    ("wq_o1", 80), ("b_o1", 16), ("ln_g", 16), ("ln_b", 16), ("w_o2", 128), ("b_o2", 16),
    ("w_kv", 256), ("w_qkv", 384), ("g_pre", 1), ("mem_k", NMEM), ("mem_v", 128), ("w_out", 64),
    ("b_out", 64), ("g_out", 64), ("wr", 128), ("br", 1), ("w1", 256), ("b1", 2), ("w2", 128),
    ("b2", 64), ("w_qk", 128), ("w_v1", 64), ("b_qk", 1),
    ("b_v1", 64), ("den_spread", 128), ("w_proj", 64), ("b_proj", 64), ("rw1", 32), ("rb1", 1), ("rw2", NE),
    ("rb2", NE), ("ew1", 384), ("eb1", 3), ("ew2", 384), ("eb2", 3), ("ew3", 192), ("eb3", 64),
    ("spread", 384),
])

Q_STEPS = 34
F_STEPS = 121
B_STEPS = 63
PAIRS = L1H * NT // 2
TOP_PAIRS = 2
MAXIMA = 3 * PAIRS + 1
PARTS = 3
SPLITS = ((0, 0), (1, 0), (2, 0), (0, 1), (1, 1), (0, 2))
STACK = len(SPLITS) * L1D
SENDS = 2 * len(SPLITS)
WAYS = 2 * L1D
SAMPLING_LENGTHS = (10,) * (NT + 1)
POSITION_LENGTHS = (6, 8, 5, 8)
NETWORK_LENGTHS = (4, 5, 10, 7, 6, 6, 6, 5, 4, 12, 8, 7, 8, 8, 8, 6, 8)
BACK_LENGTHS = ((4, 6, 5, 5, 5) + (4,) * (PAIRS // TOP_PAIRS) + (4, 4) + (2.2,) * (PAIRS + 2)
                + (5, 14) + (4, 9, 10, 8, 6, 4, 4, 4, 12))



def places(*names):
    return {name: k + 1 for k, name in enumerate(names)}


F_PE = places("x0T", "kT", "v_lo", "vq", "ek_tok", "ctxT", "lin_w", "q_tok", "lin_y", "x1T",
              "w_row", "w_col", "hid0", "hid1", "mlp_y")
F_ACT = places("x0T", "ekT", "v_hi", "q_exp", "ek_tok", "q_tok", "x1T", "w_row", "hid0", "hid1")
F_VEC = places("x0", "neg_kmax", "q_shift", "q_soft", "ctx", "lin_w", "x1", "w_col", "x2")
B_PE = places("x2T", "qk", "v1", "q_top", "attended", "dens", "proj", "x3T", "router_h", "e1_0", "logits", "e2_0",
              "e1_1", "e2_1", "e1_2", "e2_2", "gate_t", "gb_0", "gb_1", "gb_2", "moe_y")
B_ACT = places("x2T", "part_0", "part_1", "q_top", "att", "x3T", "router_h", "e1_0", "r_exp", "e2_0", "e1_1",
               "d_exp", "e2_1", "e1_2", "e2_2", "gate_t")
B_VEC = places("v1", "rest", "part_2", "tops", "o", "x3", "r_shift", "d21", "gates", "g_0", "g_1", "g_2")


def pair_of(u):
    return divmod(u, NT // 2)


def pair_chunks(p):
    return (NT - 1 - p, 0, 4), (NT - 1 - p, 4, 4 - p), (p, 0, p + 1)


def weave(front, front_lengths, back, back_lengths):
    i = j = 0
    while i < len(front_lengths) or j < len(back_lengths):
        front_at = sum(front_lengths[:i + 1]) / sum(front_lengths)
        back_at = sum(back_lengths[:j + 1]) / sum(back_lengths)
        if i < len(front_lengths) and (j == len(back_lengths) or front_at <= back_at):
            next(front)
            i += 1
        else:
            next(back)
            j += 1
    assert next(front, None) is None and next(back, None) is None


def tower(nc, xq, table, packed, out, bounced):
    nb = xq.shape[0]
    ctx = ExitStack()
    with ctx:
        def sb(name, shape, dt=F32):
            return ctx.enter_context(nc.sbuf_tensor(name, shape, dt))

        def sem(name):
            return ctx.enter_context(nc.semaphore(name))

        bank = [ctx.enter_context(nc.psum_tensor(f"bank{i}", [P, 512], F32)) for i in range(8)]

        consts = sb("consts", [P, WIDTH])

        def con(name, rows=P):
            a, z = COLS[name]
            return consts[0:rows, a:z]

        gathered = sb("gathered", [P, NT, NPT * 4 * C])
        cells_q = sb("cells_q", [P, NT, 4, C])
        corner_w = sb("corner_w", [P, NT * NPT, 4])
        cell_idx = sb("cell_idx", [P, NT * NPT], U32)
        base_cell = sb("base_cell", [P, 1])
        queries = sb("queries", [P, NT, C])
        samples = sb("samples", [P, 2, NPT * C])
        samples_t = sb("samples_t", [P, 2, 512])
        front_work = sb("front_work", [P, 5120])
        back_work = sb("back_work", [P, 5120])
        feats_f = sb("feats_f", [P, 1024])
        feats_b = sb("feats_b", [P, 1024])
        parts = sb("parts", [P, PARTS, 1024], BF16)
        q_stack = sb("q_stack", [P, L1H, 1024], BF16)
        k_stack = sb("k_stack", [P, L1H, 1024], BF16)
        top_rows = parts[0:L1H * PARTS, 0, :]
        ident_h = sb("ident_h", [P, P], BF16)
        mask_h = sb("mask_h", [P, P], BF16)
        tops = sb("tops", [P, NT, L1H, PARTS], BF16)
        prod = sb("prod", [P, 512])
        score = sb("score", [P, 512])
        h_f = sb("h_f", [P, NT * C])
        h_mid = sb("h_mid", [P, NT * C])
        h_b = sb("h_b", [P, NT * C])
        z_f = sb("z_f", [P, NT * C])
        z_b = sb("z_b", [P, NT * L1H * WAYS])
        sq_f = sb("sq_f", [P, NT * C])
        sq_b = sb("sq_b", [P, NT * C])
        small_f = sb("small_f", [P, 16, 64])
        small_b = sb("small_b", [P, 16, 64])
        qs = sb("qs", [P, 11, 128])
        wsum = sb("wsum", [P, 4])
        mem_max = sb("mem_max", [P, 1])
        w_lin = sb("w_lin", [P, 64])
        ctx_m = sb("ctx_m", [P, 128])
        emk = sb("emk", [P, NMEM])
        emk_t = sb("emk_t", [NMEM, 128])
        gates = sb("gates", [P, NT, NE])

        loaded = sem("consts_loaded")
        const_ready = sem("const_ready")
        qcells = sem("qcells_loaded")
        q_step = sem("positions_step")
        f_step = sem("front_step")
        b_step = sem("back_step")
        qfeat_ready = sem("qfeat_ready")
        q_pe = sem("positions_product")
        q_act = sem("positions_copied")
        q_read = sem("hidden_normed")
        offs_ready = sem("hidden_ready")
        idx_ready = sem("idx_ready")
        tile_gathered = [sem(f"tile_gathered{t}") for t in range(NT)]
        samp_ready = sem("samp_ready")
        samp_turned = sem("samp_turned")
        samp_copied = sem("samp_copied")
        kv_ready = sem("kv_ready")
        v_copied = sem("v_copied")
        k_used = sem("k_used")
        shifted = sem("score_shifted")
        exped = sem("score_exped")
        f_pe, f_act, f_vec = sem("front_product"), sem("front_mapped"), sem("front_vector")
        b_pe, b_act, b_vec = sem("back_product"), sem("back_mapped"), sem("back_vector")
        s_scores = sem("scores_ready")
        s_rowmax = sem("rowmax_ready")
        s_logits = sem("shifted_scores_ready")
        s_probs = sem("probs_ready")
        pe_passed = sem("pe_passed")
        pool_passed = sem("pool_passed")
        stored = sem("stored")
        parts_sent = sem("parts_sent")
        parts_stacked = sem("parts_stacked")
        tops_stacked = sem("tops_stacked")
        out_free = sem("out_free")
        y_free = sem("experts_sum_read")

        ident = con("ident")

        def fw(col0, width, rows=P):
            return front_work[0:rows, col0:col0 + width]

        def bw(col0, width, rows=P):
            return back_work[0:rows, col0:col0 + width]

        values = fw(0, 4096).rearrange("p (t m) -> p t m", t=NT)
        v_lin, ek_t, ek, q_soft, q_t = (fw(1024 * k, 1024) for k in range(5))
        hidden, w_row, junk = fw(0, 2048), fw(2048, 1024), fw(3072, 1024)
        qk, rest = bw(0, 1024), bw(1024, 1024)
        probs = bw(0, 4 * 9 * P).rearrange("p (s c) -> p s c", s=4)
        att, per_den = bw(0, 1024), bw(1024, 1024)
        a1, a2, r_h, g_t = bw(0, 1024), bw(1024, 3072), bw(4096, 1024, 32), bw(4096, 1024, NE)

        def whole_program(engine, positions, front, back):
            for _ in positions(0):
                pass
            for _ in front(0, positions):
                pass
            with engine.Fori(0, nb - 2) as b:
                weave(front(b + 1, positions), SAMPLING_LENGTHS + POSITION_LENGTHS + NETWORK_LENGTHS,
                      back(b), BACK_LENGTHS)
            weave(front(nb - 1, None), SAMPLING_LENGTHS + NETWORK_LENGTHS, back(nb - 2), BACK_LENGTHS)
            for _ in back(nb - 1):
                pass

        block = ctx.enter_context(nc.Block())

        @block.sync
        def _(sp):
            sp.dma_start(consts[:, :], packed).then_inc(loaded, 16)

            def load_cells(b, first):
                if not first:
                    sp.wait_ge(qfeat_ready, b)
                sp.dma_start(cells_q[:, :, :, :].rearrange("p t k c -> p (t k c)"),
                             xq[b]).then_inc(qcells, 16)

            def stack_parts(b):
                for i in range(PARTS):
                    if i < 2:
                        sp.wait_ge(b_act, b * len(B_ACT) + B_ACT[f"part_{i}"])
                    else:
                        sp.wait_ge(b_vec, b * len(B_VEC) + B_VEC["part_2"])
                    sp.dma_start(bounced[:, i, :], parts[:, i, :]).then_inc(parts_sent, 16)
                sp.wait_ge(parts_sent, 16 * PARTS * b + 16 * PARTS)
                for n, of_pair in enumerate(SPLITS):
                    for side, stack in enumerate((q_stack, k_stack)):
                        src = bounced[side * C:(side + 1) * C, of_pair[side], :]
                        sp.dma_start(stack[n * L1D:(n + 1) * L1D, :, :],
                                     src.rearrange("(a d) c -> d a c", d=L1D)).then_inc(parts_stacked, 16)

            def stack_tops(b):
                sp.wait_ge(b_act, b * len(B_ACT) + B_ACT["q_top"])
                for hd in range(L1H):
                    sp.dma_start(q_stack[STACK:STACK + PARTS, hd, :],
                                 parts[hd * PARTS:(hd + 1) * PARTS, 0, :]).then_inc(tops_stacked, 16)

            def store(b):
                sp.wait_ge(b_step, b * B_STEPS + B_STEPS)
                sp.dma_start(out[b], h_b[:, :]).then_inc(stored, 16)
                sp.wait_ge(stored, 16 * b + 16)
                sp.sem_inc(out_free, 1)

            sp.sem_inc(out_free, 1)
            load_cells(0, True)
            load_cells(1, False)
            with sp.Fori(0, nb - 2) as b:
                load_cells(b + 2, False)
                stack_parts(b)
                stack_tops(b)
                store(b)
            for last in (nb - 2, nb - 1):
                stack_parts(last)
                stack_tops(last)
                store(last)

        @block.gpsimd
        def _(pool):
            def gather(b, first):
                pool.wait_ge(idx_ready, b + 1)
                for t in range(NT):
                    if not first:
                        pool.wait_ge(samp_ready, (b - 1) * NT + t + 1)
                        pool.sem_inc(pool_passed, 1)
                    for p in range(NPT):
                        j = t * NPT + p
                        pool.indirect_dma_start(
                            out=gathered[:, t, p * 4 * C:(p + 1) * 4 * C], out_offset=None,
                            in_=table,
                            in_offset=bass.IndirectOffsetOnAxis(ap=cell_idx[:, j:j + 1], axis=0),
                        ).then_inc(tile_gathered[t], 16)

            gather(0, True)
            with pool.Fori(1, nb) as b:
                gather(b, False)

        @block.tensor
        def _(pe):
            pe.wait_ge(const_ready, 1)
            pe.sem_inc(y_free, 1)

            def alone():
                pe.sem_inc(pe_passed, 1)

            def turn_tiles(src, lo, hi):
                for t in range(NT):
                    dst = (lo if t < 4 else hi)[0:C, (t % 4) * P:(t % 4 + 1) * P]
                    last = nc.tensor.transpose(dst, src[:, t * C:(t + 1) * C], ident)
                return last

            def wide(weights, rows, lo, hi, src):
                for n, bk in enumerate((lo, hi)):
                    last = nc.tensor.matmul(bk[0:rows, :], weights, src[:, n * 512:(n + 1) * 512],
                                            start=True, stop=True)
                return last

            def per_tile(weights, width, dst, src, tiles=range(NT)):
                for n, t in enumerate(tiles):
                    last = nc.tensor.matmul(dst[:, n * width:(n + 1) * width],
                                            src[:, t * P:(t + 1) * P], weights, start=True, stop=True)
                return last

            xf, xb = feats_f[0:C, :], feats_b[0:C, :]

            def positions(b):
                pe.wait_ge(qfeat_ready, b + 1)
                alone()
                turn_tiles(sq_f, bank[0], bank[1]).then_inc(q_pe, 1)
                yield
                pe.wait_ge(q_act, b * 2 + 1)
                for t in range(NT):
                    last = nc.tensor.matmul(bank[t // 4][:, (t % 4) * 80:(t % 4 + 1) * 80],
                                            xf[:, t * P:(t + 1) * P], con("wq_o1", C),
                                            start=True, stop=True)
                last.then_inc(q_pe, 1)
                yield
                pe.wait_ge(offs_ready, b + 1)
                nc.tensor.transpose(bank[2][:, 0:P], qs[:, 1, :], ident).then_inc(q_pe, 1)
                yield
                pe.wait_ge(q_act, b * 2 + 2)
                nc.tensor.matmul(bank[2][:, P:2 * P], qs[:, 2, :], con("w_o2"),
                                 start=True, stop=True).then_inc(q_pe, 1)
                yield

            def front(b, following):
                def given(sem_, table_, name):
                    pe.wait_ge(sem_, b * len(table_) + table_[name])

                def done(ins):
                    ins.then_inc(f_pe, 1)

                def project(t):
                    pe.wait_ge(samp_copied, b * NT + t + 1)
                    if t >= 1:
                        pe.wait_ge(k_used, b * NT + t)
                        pe.wait_ge(v_copied, b * NT + t)
                    for kv in range(2):
                        for g in range(4):
                            last = nc.tensor.matmul(bank[1 + kv][:, g * P:(g + 1) * P],
                                                    samples_t[:, t % 2, g * P:(g + 1) * P],
                                                    con("w_kv")[:, kv * P:(kv + 1) * P],
                                                    start=True, stop=True)
                    last.then_inc(kv_ready, 1)

                def turn(t):
                    pe.wait_ge(samp_ready, b * NT + t + 1)
                    for g in range(4):
                        last = nc.tensor.transpose(bank[0][:, g * P:(g + 1) * P],
                                                   samples[:, t % 2, g * P:(g + 1) * P], ident)
                    last.then_inc(samp_turned, 1)

                for t in range(NT + 1):
                    if t >= 1:
                        project(t - 1)
                    if t < NT:
                        turn(t)
                    yield
                if following:
                    yield from following(b + 1)
                yield
                yield
                yield
                given(f_vec, F_VEC, "x0")
                alone()
                done(turn_tiles(z_f, bank[0], bank[1]))
                yield
                given(f_act, F_ACT, "x0T")
                wq = con("w_qkv", C)
                done(wide(wq[:, 128:256], P, bank[0], bank[1], xf))
                done(per_tile(wq[:, 256:384], P, bank[2], xf, range(0, 4)))
                yield
                given(f_act, F_ACT, "ekT")
                per_tile(wq[:, 256:384], P, bank[0], xf, range(4, 8))
                per_tile(wq[:, 0:128], P, bank[1], xf, range(0, 4))
                done(per_tile(wq[:, 0:128], P, bank[2], xf, range(4, 8)))
                yield
                given(f_act, F_ACT, "v_hi")
                given(f_vec, F_VEC, "q_shift")
                for t in range(NT):
                    nc.tensor.transpose(bank[t // 4][:, (t % 4) * P:(t % 4 + 1) * P],
                                        ek_t[:, t * P:(t + 1) * P], ident)
                done(nc.tensor.transpose(bank[2][0:NMEM, 0:P], emk[:, :], ident))
                yield
                given(f_act, F_ACT, "ek_tok")
                for t in range(NT):
                    nc.tensor.matmul(bank[2][:, 0:P], v_lin[:, t * P:(t + 1) * P],
                                     ek[:, t * P:(t + 1) * P], start=(t == 0), stop=False)
                done(nc.tensor.matmul(bank[2][:, 0:P], con("mem_v", NMEM), emk_t[:, :],
                                      start=False, stop=True))
                yield
                given(f_vec, F_VEC, "ctx")
                done(nc.tensor.matmul(bank[2][:, P:P + C], ctx_m[:, :], con("w_out"), start=True, stop=True))
                given(f_vec, F_VEC, "q_soft")
                for t in range(NT):
                    last = nc.tensor.transpose(bank[t // 4][:, (t % 4) * P:(t % 4 + 1) * P],
                                               q_soft[:, t * P:(t + 1) * P], ident)
                done(last)
                yield
                given(f_act, F_ACT, "q_tok")
                given(f_vec, F_VEC, "lin_w")
                done(per_tile(w_lin[:, :], C, bank[2], q_t))
                yield
                given(f_vec, F_VEC, "x1")
                alone()
                done(turn_tiles(h_f, bank[0], bank[1]))
                yield
                given(f_act, F_ACT, "x1T")
                done(wide(con("wr", C), P, bank[0], bank[1], xf))
                given(f_act, F_ACT, "w_row")
                alone()
                for t in range(NT):
                    last = nc.tensor.transpose(bank[2][:, t:t + 1], w_row[0:1, t * P:(t + 1) * P],
                                               ident[0:1, 0:1])
                done(last)
                yield
                done(wide(con("w1", C)[:, 0:P], P, bank[0], bank[1], xf))
                yield
                given(f_act, F_ACT, "hid0")
                done(wide(con("w1", C)[:, P:2 * P], P, bank[0], bank[1], xf))
                yield
                given(f_act, F_ACT, "hid1")
                given(f_vec, F_VEC, "w_col")
                for t in range(NT):
                    for half in range(2):
                        last = nc.tensor.matmul(bank[2][:, t * C:(t + 1) * C],
                                                hidden[:, half * 1024 + t * P:half * 1024 + (t + 1) * P],
                                                con("w2")[:, half * C:(half + 1) * C],
                                                start=(half == 0), stop=(half == 1))
                done(last)
                yield
                yield
                yield

            def back(b):
                def given(sem_, table_, name):
                    pe.wait_ge(sem_, b * len(table_) + table_[name])

                def done(ins):
                    ins.then_inc(b_pe, 1)

                given(f_vec, F_VEC, "x2")
                alone()
                done(turn_tiles(h_mid, bank[3], bank[4]))
                yield
                given(b_act, B_ACT, "x2T")
                done(wide(con("w_qk", C), P, bank[3], bank[4], xb))
                pe.wait_ge(y_free, b + 1)
                alone()
                done(per_tile(con("w_v1", C), C, bank[7], xb))
                yield
                yield
                yield
                yield

                def top_scores(u):
                    hd, p = pair_of(u)
                    for n, (qt, k0, wide_) in enumerate(pair_chunks(p)):
                        if u:
                            pe.wait_ge(s_rowmax, b * MAXIMA + 3 * (u - 1) + n + 1)
                        diag = qt < k0 + wide_
                        last = nc.tensor.matmul(bank[3 + n][:, 0:wide_ * P], q_stack[0:STACK, hd, qt * P:(qt + 1) * P],
                                                k_stack[0:STACK, hd, k0 * P:(k0 + wide_) * P], start=True, stop=not diag)
                        if diag:
                            at = (qt - k0) * P
                            last = nc.tensor.matmul(bank[3 + n][:, at:at + P], ident_h[:, :], mask_h[:, :],
                                                    start=False, stop=True)
                        last.then_inc(s_scores, 1)

                def shifted_scores(u):
                    hd, p = pair_of(u)
                    for n, (far, q0, wide_) in enumerate(pair_chunks(p)):
                        if u:
                            pe.wait_ge(s_probs, b * 3 * PAIRS + 3 * (u - 1) + n + 1)
                        kt, q0 = NT - 1 - far, NT - q0 - wide_
                        diag = kt >= q0
                        last = nc.tensor.matmul(bank[3 + n][:, 0:wide_ * P], k_stack[0:STACK + PARTS, hd, kt * P:(kt + 1) * P],
                                                q_stack[0:STACK + PARTS, hd, q0 * P:(q0 + wide_) * P], start=True, stop=not diag)
                        if diag:
                            at = (kt - q0) * P
                            last = nc.tensor.matmul(bank[3 + n][:, at:at + P], mask_h[:, :], ident_h[:, :],
                                                    start=False, stop=True)
                        last.then_inc(s_logits, 1)

                def attend(u):
                    hd, p = pair_of(u)
                    col = 0
                    for n, (far, q0, wide_) in enumerate(pair_chunks(p)):
                        pe.wait_ge(s_probs, b * 3 * PAIRS + 3 * u + n + 1)
                        kt, q0 = NT - 1 - far, NT - q0 - wide_
                        at = q0 % 4 * P
                        last = nc.tensor.matmul(bank[6 + q0 // 4][hd * WAYS:(hd + 1) * WAYS, at:at + wide_ * P],
                                                z_b[:, (kt * L1H + hd) * WAYS:(kt * L1H + hd + 1) * WAYS],
                                                probs[:, u % 4, col:col + wide_ * P],
                                                start=(kt == 0), stop=(kt == 3 + q0 // 4))
                        col += wide_ * P
                    return last

                pe.wait_ge(parts_stacked, 16 * SENDS * b + 16 * SENDS)
                for u in range(PAIRS):
                    top_scores(u)
                    if u % TOP_PAIRS == TOP_PAIRS - 1:
                        yield
                given(b_vec, B_VEC, "tops")
                alone()
                for t in range(NT):
                    last = nc.tensor.matmul(bank[3 + t // 4][0:L1H * PARTS, (t % 4) * P:(t % 4 + 1) * P],
                                            tops[:, t, :, :].rearrange("p a i -> p (a i)"), ident_h[:, :],
                                            start=True, stop=True)
                done(last)
                yield
                yield
                pe.wait_ge(tops_stacked, 16 * L1H * b + 16 * L1H)
                for u in range(PAIRS + 2):
                    if u < PAIRS:
                        shifted_scores(u)
                    if u == PAIRS + 1:
                        done(attend(u - 2))
                    elif u >= 2:
                        attend(u - 2)
                    yield
                given(b_act, B_ACT, "att")
                done(wide(con("den_spread"), P, bank[3], bank[4], att))
                yield
                given(b_vec, B_VEC, "o")
                done(per_tile(con("w_proj"), C, bank[5], att))
                yield
                given(b_vec, B_VEC, "x3")
                alone()
                done(turn_tiles(h_b, bank[3], bank[4]))
                yield

                def layer1(pr):
                    done(wide(con("ew1", C)[:, pr * P:(pr + 1) * P], P, bank[3], bank[4], xb))

                def layer2(pr):
                    done(wide(con("ew2")[:, pr * P:(pr + 1) * P], P, bank[5], bank[6], a1))

                def spread_gates(pr, lo, hi):
                    done(wide(con("spread", NE)[:, pr * P:(pr + 1) * P], P, bank[lo], bank[hi], g_t))

                given(b_act, B_ACT, "x3T")
                alone()
                done(wide(con("rw1", C), 32, bank[5], bank[6], xb))
                layer1(0)
                given(b_act, B_ACT, "router_h")
                done(per_tile(con("rw2", 32), NE, bank[7], r_h))
                yield
                given(b_act, B_ACT, "e1_0")
                layer2(0)
                layer1(1)
                yield
                given(b_act, B_ACT, "e1_1")
                layer2(1)
                layer1(2)
                yield
                given(b_act, B_ACT, "e1_2")
                layer2(2)
                given(b_vec, B_VEC, "gates")
                for t in range(NT):
                    last = nc.tensor.transpose(bank[3 + t // 4][0:NE, (t % 4) * P:(t % 4 + 1) * P],
                                               gates[:, t, :], ident)
                done(last)
                yield
                given(b_act, B_ACT, "gate_t")
                spread_gates(0, 5, 6)
                yield
                spread_gates(1, 3, 4)
                yield
                given(b_vec, B_VEC, "g_0")
                spread_gates(2, 5, 6)
                yield
                given(b_vec, B_VEC, "g_2")
                for t in range(NT):
                    dst = bank[7][:, t * C:(t + 1) * C]
                    for pr in range(3):
                        nc.tensor.matmul(dst, a2[:, pr * 1024 + t * P:pr * 1024 + (t + 1) * P],
                                         con("ew3")[:, pr * C:(pr + 1) * C], start=(pr == 0), stop=False)
                    last = nc.tensor.matmul(dst, g_t[:, t * P:(t + 1) * P], con("eb3", NE),
                                            start=False, stop=True)
                done(last)
                yield

            whole_program(pe, positions, front, back)

        @block.scalar
        def _(act):
            act.wait_ge(const_ready, 1)

            def copy_pair(dst, lo, hi, rows=P):
                nc.scalar.copy(dst[:, 0:512], bank[lo][0:rows, :])
                return nc.scalar.copy(dst[:, 512:1024], bank[hi][0:rows, :])

            def mapped(dst, lo, hi, func, bias, rows=P, scale=1.0):
                nc.scalar.activation(dst[:, 0:512], bank[lo][0:rows, :], func, bias=bias, scale=scale)
                return nc.scalar.activation(dst[:, 512:1024], bank[hi][0:rows, :], func, bias=bias, scale=scale)

            def positions(b):
                act.wait_ge(q_pe, b * 4 + 1)
                copy_pair(feats_f[0:C, :], 0, 1, C).then_inc(q_act, 1)
                yield
                act.wait_ge(q_read, b + 1)
                nc.scalar.activation(qs[:, 1, :], qs[:, 0, :], ACT.Gelu_apprx_tanh).then_inc(offs_ready, 1)
                yield
                act.wait_ge(q_pe, b * 4 + 3)
                nc.scalar.copy(qs[:, 2, :], bank[2][:, 0:P]).then_inc(q_act, 1)
                yield
                yield

            def front(b, following):
                def pe_gave(name):
                    act.wait_ge(f_pe, b * len(F_PE) + F_PE[name])

                def vec_gave(name):
                    act.wait_ge(f_vec, b * len(F_VEC) + F_VEC[name])

                def done(ins):
                    ins.then_inc(f_act, 1)

                for t in range(NT + 1):
                    if t >= 1:
                        act.wait_ge(kv_ready, b * NT + t)
                        nc.scalar.copy(values[:, t - 1, :], bank[2][:, :]).then_inc(v_copied, 1)
                    if t < NT:
                        act.wait_ge(samp_turned, b * NT + t + 1)
                        nc.scalar.copy(samples_t[:, t % 2, :], bank[0][:, :]).then_inc(samp_copied, 1)
                    yield
                if following:
                    yield from following(b + 1)
                act.wait_ge(shifted, b + 1)
                nc.scalar.activation(score[:, :], score[:, :], ACT.Exp,
                                     scale=float(C // NPT) ** -0.5).then_inc(exped, 1)
                yield
                yield
                yield
                pe_gave("x0T")
                done(copy_pair(feats_f[0:C, :], 0, 1, C))
                yield
                vec_gave("neg_kmax")
                neg = small_f[:, 3, 3:4]
                nc.scalar.activation(ek_t[:, 0:512], bank[0][:, :], ACT.Exp, bias=neg, accum_out=wsum[:, 0:1])
                nc.scalar.activation(ek_t[:, 512:1024], bank[1][:, :], ACT.Exp, bias=neg, accum_out=wsum[:, 1:2])
                nc.scalar.activation(emk[:, :], con("mem_k"), ACT.Exp, bias=neg, accum_out=wsum[:, 2:3])
                pe_gave("v_lo")
                done(nc.scalar.copy(v_lin[:, 0:512], bank[2][:, :]))
                yield
                pe_gave("vq")
                done(nc.scalar.copy(v_lin[:, 512:1024], bank[0][:, :]))
                vec_gave("q_shift")
                done(nc.scalar.activation(q_soft, q_soft, ACT.Exp))
                yield
                pe_gave("ek_tok")
                copy_pair(ek, 0, 1)
                done(nc.scalar.copy(emk_t[:, :], bank[2][0:NMEM, 0:P]))
                yield
                yield
                pe_gave("q_tok")
                done(copy_pair(q_t, 0, 1))
                yield
                yield
                pe_gave("x1T")
                done(copy_pair(feats_f[0:C, :], 0, 1, C))
                yield
                pe_gave("w_row")
                done(mapped(w_row, 0, 1, ACT.Identity, con("br")))
                yield
                pe_gave("hid0")
                done(mapped(hidden[:, 0:1024], 0, 1, ACT.Gelu_apprx_tanh, con("b1")[:, 0:1]))
                yield
                pe_gave("hid1")
                done(mapped(hidden[:, 1024:2048], 0, 1, ACT.Gelu_apprx_tanh, con("b1")[:, 1:2]))
                yield
                yield
                yield
                yield

            def back(b):
                def pe_gave(name):
                    act.wait_ge(b_pe, b * len(B_PE) + B_PE[name])

                def vec_gave(name):
                    act.wait_ge(b_vec, b * len(B_VEC) + B_VEC[name])

                def done(ins):
                    ins.then_inc(b_act, 1)

                pe_gave("x2T")
                done(copy_pair(feats_b[0:C, :], 3, 4, C))
                yield
                pe_gave("qk")
                mapped(qk, 3, 4, ACT.Identity, con("b_qk"))
                done(mapped(parts[:, 0, :], 3, 4, ACT.Identity, con("b_qk")))
                yield
                vec_gave("rest")
                done(nc.scalar.copy(parts[:, 1, :], rest))
                yield
                yield
                yield
                for _ in range(PAIRS // TOP_PAIRS):
                    yield
                pe_gave("q_top")
                done(copy_pair(top_rows, 3, 4, L1H * PARTS))
                yield
                yield
                for u in range(PAIRS + 2):
                    if u < PAIRS:
                        col = 0
                        for n, (_, _, wide_) in enumerate(pair_chunks(pair_of(u)[1])):
                            act.wait_ge(s_logits, b * 3 * PAIRS + 3 * u + n + 1)
                            nc.scalar.activation(probs[:, u % 4, col:col + wide_ * P],
                                                 bank[3 + n][:, 0:wide_ * P], ACT.Exp).then_inc(s_probs, 1)
                            col += wide_ * P
                    yield
                pe_gave("attended")
                done(copy_pair(att, 6, 7))
                yield
                yield
                pe_gave("x3T")
                done(copy_pair(feats_b[0:C, :], 3, 4, C))
                yield

                def relu1(pr):
                    pe_gave(f"e1_{pr}")
                    done(mapped(a1, 3, 4, ACT.Relu, con("eb1")[:, pr:pr + 1]))

                def relu2(pr):
                    pe_gave(f"e2_{pr}")
                    done(mapped(a2[:, pr * 1024:(pr + 1) * 1024], 5, 6, ACT.Relu, con("eb2")[:, pr:pr + 1]))

                lg, d21 = small_b[:, 7, 0:48], small_b[:, 11, 24:32]
                pe_gave("router_h")
                done(mapped(r_h, 5, 6, ACT.Relu, con("rb1", 32), rows=32))
                relu1(0)
                vec_gave("r_shift")
                done(nc.scalar.activation(lg, lg, ACT.Exp))
                yield
                relu2(0)
                relu1(1)
                vec_gave("d21")
                done(nc.scalar.activation(d21, d21, ACT.Exp))
                yield
                relu2(1)
                relu1(2)
                yield
                relu2(2)
                pe_gave("gate_t")
                done(copy_pair(g_t, 3, 4, NE))
                yield
                yield
                yield
                yield
                yield

            whole_program(act, positions, front, back)

        @block.vector
        def _(dve):
            v = nc.vector

            class Steps:

                def __init__(self, sem_, base):
                    self.sem, self.base, self.n = sem_, base, 0

                def __call__(self, ins):
                    self.n += 1
                    ins.then_inc(self.sem, 1)
                    dve.wait_ge(self.sem, self.base + self.n)

                def end(self, per, what):
                    assert self.n == per, (what, self.n)

            def v3(ap, a):
                return ap.rearrange("p (a c) -> p a c", a=a)

            def rows_of(ap, n, m):
                return ap.unsqueeze(1).to_broadcast([P, n, m])

            def over(ap, m):
                return ap.unsqueeze(2).to_broadcast([P, ap.shape[1], m])

            def inverse_root(step, sm, x, n):
                y, half, t = sm[:, 13, 0:n], sm[:, 14, 0:n], sm[:, 15, 0:n]
                v.tensor_scalar(half, x, -0.5, None, ALU.mult)
                step(v.tensor_scalar(y.bitcast(I32), x.bitcast(I32), -0.5, 1597463007.0, ALU.mult, ALU.add))
                for last in (False, False, True):
                    step(v.tensor_tensor(t, y, y, ALU.mult))
                    step(v.tensor_tensor(t, t, half, ALU.mult))
                    step(v.scalar_tensor_tensor(x if last else y, t, 1.5, y, ALU.add, ALU.mult))

            def layernorm(step, sm, sq, x, dst, groups, width):
                s, d = sm[:, 0, 0:groups], v3(x, groups)
                step(v.tensor_reduce(s, d, AX.X, ALU.add))
                step(v.tensor_scalar(s, s, 1.0 / width, None, ALU.mult))
                step(v.tensor_tensor(d, d, over(s, width), ALU.subtract))
                q = v3(sq[:, 0:groups * width], groups)
                step(v.tensor_tensor(q, d, d, ALU.mult))
                step(v.tensor_reduce(s, q, AX.X, ALU.add))
                step(v.tensor_scalar(s, s, 1.0 / width, 1e-5, ALU.mult, ALU.add))
                inverse_root(step, sm, s, groups)
                return v.tensor_tensor(v3(dst, groups), d, over(s, width), ALU.mult)

            def inverse_norm(step, x):
                s = small_f[:, 0, 0:NT]
                step(v.tensor_tensor(sq_f[:, :], x, x, ALU.mult))
                step(v.tensor_reduce(s, v3(sq_f[:, :], NT), AX.X, ALU.add))
                step(v.tensor_scalar(s, s, 1e-24, None, ALU.max))
                inverse_root(step, small_f, s, NT)
                return s

            def prepare():
                dve.wait_ge(loaded, 16)
                v.tensor_scalar(con("w_qkv", C), con("w_qkv", C), con("g_pre", C), float(C) ** 0.5,
                                ALU.mult, ALU.mult)
                v.tensor_scalar(con("g_out"), con("g_out"), float(C) ** 0.5, None, ALU.mult)
                v.tensor_scalar(con("w_qk")[:, 0:C], con("w_qk")[:, 0:C], L1D ** -0.5, None, ALU.mult)
                v.tensor_scalar(con("b_qk", C), con("b_qk", C), L1D ** -0.5, None, ALU.mult)
                v.tensor_reduce(mem_max[:, :], con("mem_k"), AX.X, ALU.max)
                v.tensor_copy(ident_h[:, :], ident)
                v.tensor_copy(mask_h[:, :], con("neg_mask"))
                v.memset(k_stack[STACK:P, :, :], 1.0)
                v.memset(base_cell[:, :], 0.0).then_inc(const_ready, 1)
                dve.wait_ge(const_ready, 1)

            def positions(b):
                step = Steps(q_step, b * Q_STEPS)
                dve.wait_ge(qcells, 16 * b + 16)
                cw = con("q_corner").unsqueeze(2).to_broadcast([P, NT * 4, C])
                c3 = cells_q[:, :, :, :].rearrange("p t k c -> p (t k) c")
                step(v.tensor_tensor(c3, c3, cw, ALU.mult))
                c4 = cells_q[:, :, :, :].rearrange("p t (y x) c -> p t y (x c)", y=2)
                step(v.tensor_tensor(c4[:, :, 0, :], c4[:, :, 0, :], c4[:, :, 1, :], ALU.add))
                v.tensor_tensor(v3(sq_f[:, :], NT), cells_q[:, :, 0, :], cells_q[:, :, 1, :],
                                ALU.add).then_inc(qfeat_ready, 1)
                yield
                dve.wait_ge(q_pe, b * 4 + 2)
                for g in range(2):
                    src = bank[g][:, 0:320].rearrange("p (t c) -> p t c", t=4)
                    v.tensor_copy(queries[:, 4 * g:4 * g + 4, :], src[:, :, 0:C])
                    step(v.tensor_tensor(v3(qs[:, 0, g * 64:(g + 1) * 64], 4), src[:, :, C:C + 16],
                                         rows_of(con("b_o1"), 4, 16), ALU.add))
                hid = qs[:, 0, :]
                step(layernorm(step, small_f, sq_f, hid, hid, NT, 16))
                step(v.tensor_tensor(v3(hid, NT), v3(hid, NT), rows_of(con("ln_g"), NT, 16), ALU.mult))
                v.tensor_tensor(v3(hid, NT), v3(hid, NT), rows_of(con("ln_b"), NT, 16),
                                ALU.add).then_inc(q_read, 1)
                yield
                yield
                dve.wait_ge(q_pe, b * 4 + 4)
                px, cl, fl, ge, wt, om = (qs[:, k, :] for k in range(3, 9))
                step(v.tensor_tensor(v3(px, NT), v3(bank[2][:, P:2 * P], NT), rows_of(con("b_o2"), NT, 16), ALU.add))
                step(v.scalar_tensor_tensor(px, px, 4.0, con("ref_xy"), ALU.mult, ALU.add))
                step(v.tensor_scalar(cl, px, 0.0, float(SIDE - 2), ALU.max, ALU.min))
                whole = qs[:, 9, :].bitcast(I32)
                step(v.tensor_copy(whole, cl))
                step(v.tensor_copy(fl, whole))
                step(v.tensor_tensor(ge, fl, cl, ALU.is_gt))
                step(v.tensor_tensor(fl, fl, ge, ALU.subtract))
                cell = qs[:, 10, 0:64]
                step(v.scalar_tensor_tensor(cell, fl[:, 1:128:2], float(CELLS), fl[:, 0:128:2], ALU.mult, ALU.add))
                v.tensor_scalar(cell_idx[:, :], cell, base_cell[:, 0:1], None, ALU.add).then_inc(idx_ready, 1)
                step(v.tensor_tensor(wt, px, fl, ALU.subtract))
                step(v.tensor_scalar(wt, wt, 0.0, 1.0, ALU.max, ALU.min))
                step(v.tensor_scalar(om, wt, -1.0, 1.0, ALU.mult, ALU.add))
                for k, (fy, fx) in enumerate(((om, om), (om, wt), (wt, om), (wt, wt))):
                    v.tensor_tensor(corner_w[:, :, k], fy[:, 1:128:2], fx[:, 0:128:2], ALU.mult)
                dve.wait_ge(idx_ready, b + 1)
                step(v.tensor_scalar(base_cell[:, :], base_cell[:, :], float(CELLS * CELLS), None, ALU.add))
                step.end(Q_STEPS, "Q_STEPS")
                yield

            def front(b, following):
                step = Steps(f_step, b * F_STEPS)

                def pe_gave(name):
                    dve.wait_ge(f_pe, b * len(F_PE) + F_PE[name])

                def act_gave(name):
                    dve.wait_ge(f_act, b * len(F_ACT) + F_ACT[name])

                def done(ins):
                    ins.then_inc(f_vec, 1)

                def sum_corners(t):
                    dve.wait_ge(tile_gathered[t], b * (16 * NPT) + 16 * NPT)
                    g = gathered[:, t, :]
                    step(v.tensor_tensor(v3(g, 32), v3(g, 32),
                                         over(corner_w[:, t * NPT:(t + 1) * NPT, :]
                                              .rearrange("p a k -> p (a k)"), C), ALU.mult))
                    g4 = g.rearrange("p (s y c) -> p s y c", s=NPT, y=2)
                    step(v.tensor_tensor(g4[:, :, 0, :], g4[:, :, 0, :], g4[:, :, 1, :], ALU.add))
                    if t >= 2:
                        dve.wait_ge(samp_turned, b * NT + t - 1)
                    v.tensor_tensor(v3(samples[:, t % 2, :], NPT), g4[:, :, 0, 0:C], g4[:, :, 0, C:2 * C],
                                    ALU.add).then_inc(samp_ready, 1)

                def score_tile(t):
                    dve.wait_ge(kv_ready, b * NT + t + 1)
                    v.tensor_tensor(v3(prod[:, :], NPT), v3(bank[1][:, :], NPT),
                                    queries[:, t:t + 1, :].to_broadcast([P, NPT, C]),
                                    ALU.mult).then_inc(k_used, 1)
                    dve.wait_ge(k_used, b * NT + t + 1)
                    step(v.tensor_reduce(score[:, t * 64:(t + 1) * 64], v3(prod[:, :], 64), AX.X, ALU.add))

                for t in range(NT + 1):
                    if t < NT:
                        sum_corners(t)
                    if t >= 1:
                        score_tile(t - 1)
                    yield
                if following:
                    yield from following(b + 1)
                s4 = score[:, :].rearrange("p (t s h) -> p t s h", t=NT, s=NPT)
                by_head = score[:, :].rearrange("p (t s h) -> p t h s", t=NT, s=NPT)
                top, tot = small_f[:, 1, :], small_f[:, 2, :]
                step(v.tensor_reduce(v3(top, NT), by_head, AX.X, ALU.max))
                tb = v3(top, NT).unsqueeze(2).to_broadcast([P, NT, NPT, NPT])
                v.tensor_tensor(s4, s4, tb, ALU.subtract).then_inc(shifted, 1)
                yield
                dve.wait_ge(exped, b + 1)
                v.tensor_reduce(v3(tot, NT), by_head, AX.X, ALU.add)
                dve.wait_ge(v_copied, b * NT + NT)

                def weigh_values(t0, t1):
                    vals = values[:, t0:t1, :].rearrange("p t (s d) -> p (t s) d", s=64)
                    step(v.tensor_tensor(vals, vals, over(score[:, t0 * 64:t1 * 64], 8), ALU.mult))

                weigh_values(0, 4)
                step(v.reciprocal(tot, tot))
                yield
                weigh_values(4, NT)
                for t in range(NT):
                    last = v.tensor_reduce(z_f[:, t * C:(t + 1) * C],
                                           values[:, t, :].rearrange("p (s c) -> p c s", s=NPT), AX.X, ALU.add)
                step(last)
                yield
                step(v.tensor_tensor(v3(h_f[:, :], 64), v3(z_f[:, :], 64), over(tot, 8), ALU.mult))
                s = inverse_norm(step, h_f[:, :])
                done(v.tensor_tensor(v3(z_f[:, :], NT), v3(h_f[:, :], NT), over(s, C), ALU.mult))
                yield
                pe_gave("kT")
                km = small_f[:, 3, :]
                v.tensor_reduce(km[:, 0:1], bank[0][:, :], AX.X, ALU.max)
                v.tensor_copy(km[:, 2:3], mem_max[:, :])
                step(v.tensor_reduce(km[:, 1:2], bank[1][:, :], AX.X, ALU.max))
                done(v.tensor_reduce(km[:, 3:4], km[:, 0:3], AX.X, ALU.max, negate=True))
                yield
                pe_gave("vq")
                qm = small_f[:, 4, 0:32]
                for g in range(2):
                    step(v.tensor_reduce(qm[:, 16 * g:16 * g + 16], v3(bank[1 + g][:, :], 16), AX.X, ALU.max))
                for g in range(2):
                    last = v.tensor_tensor(v3(q_soft[:, 512 * g:512 * g + 512], 16), v3(bank[1 + g][:, :], 16),
                                           over(qm[:, 16 * g:16 * g + 16], L0D), ALU.subtract)
                done(last)
                yield
                act_gave("q_exp")
                step(v.tensor_reduce(qm, v3(q_soft, 32), AX.X, ALU.add))
                step(v.reciprocal(qm, qm))
                done(v.tensor_tensor(v3(q_soft, 32), v3(q_soft, 32), over(qm, L0D), ALU.mult))
                ksum = small_f[:, 5, 0:1]
                step(v.tensor_reduce(ksum, wsum[:, 0:3], AX.X, ALU.add))
                step(v.reciprocal(ksum, ksum))
                yield
                pe_gave("ctxT")
                done(v.tensor_tensor(ctx_m[:, :], bank[2][:, 0:P], con("head_mask"), ALU.mult))
                yield
                pe_gave("lin_w")
                done(v.tensor_scalar(w_lin[:, :], bank[2][:, P:P + C], ksum, L0D ** -0.5,
                                     ALU.mult, ALU.mult))
                yield
                pe_gave("lin_y")
                z3 = v3(z_f[:, :], NT)
                step(v.tensor_tensor(z3, v3(bank[2][:, :], NT), rows_of(con("b_out"), NT, C), ALU.add))
                s = inverse_norm(step, z_f[:, :])
                step(v.tensor_tensor(z3, z3, over(s, C), ALU.mult))
                step(v.tensor_tensor(z3, z3, rows_of(con("g_out"), NT, C), ALU.mult))
                step(v.scalar_tensor_tensor(z_f[:, :], h_f[:, :], 2.0, z_f[:, :], ALU.mult, ALU.add))
                yield
                done(layernorm(step, small_f, sq_f, z_f[:, :], h_f[:, :], NT, C))
                yield
                pe_gave("w_col")
                wc, rank = small_f[:, 6, 0:NT], small_f[:, 7, :]
                v.memset(rank, 0.0)
                done(v.tensor_copy(wc, bank[2][:, 0:NT]))
                dve.wait_ge(f_vec, b * len(F_VEC) + F_VEC["w_col"])

                def rank_tile(t):
                    v.tensor_scalar(junk[:, t * P:N], w_row[:, t * P:N], wc[:, t:t + 1], None,
                                    ALU.is_gt, ALU.add, accum_out=rank[:, t:t + 1])
                    if t:
                        v.tensor_scalar(junk[:, 0:t * P], w_row[:, 0:t * P], wc[:, t:t + 1], None,
                                        ALU.is_ge, ALU.add, accum_out=rank[:, 8 + t:9 + t])
                    same = sq_f[:, 0:P]
                    step(v.scalar_tensor_tensor(same, w_row[:, t * P:(t + 1) * P], wc[:, t:t + 1], con("lower"),
                                                ALU.is_equal, ALU.mult))
                    step(v.tensor_reduce(rank[:, 16 + t:17 + t], same, AX.X, ALU.add))

                yield
                for part in range(3):
                    for t in ((0, 1, 2), (3, 4, 5), (6, 7))[part]:
                        rank_tile(t)
                    yield
                step(v.tensor_tensor(rank[:, 0:8], rank[:, 0:8], rank[:, 8:16], ALU.add))
                step(v.tensor_tensor(rank[:, 0:8], rank[:, 0:8], rank[:, 16:24], ALU.add))
                step(v.scalar_tensor_tensor(wc, rank[:, 0:8], float(KEEP), wc, ALU.is_lt, ALU.mult))
                pe_gave("mlp_y")
                step(v.tensor_tensor(z3, v3(bank[2][:, :], NT), rows_of(con("b2"), NT, C), ALU.add))
                step(v.tensor_tensor(z3, z3, over(wc, C), ALU.mult))
                step(v.scalar_tensor_tensor(z_f[:, :], h_f[:, :], 2.0, z_f[:, :], ALU.mult, ALU.add))
                yield
                done(layernorm(step, small_f, sq_f, z_f[:, :], h_mid[:, :], NT, C))
                step.end(F_STEPS, "F_STEPS")
                yield

            def back(b):
                step = Steps(b_step, b * B_STEPS)

                def pe_gave(name):
                    dve.wait_ge(b_pe, b * len(B_PE) + B_PE[name])

                def act_gave(name):
                    dve.wait_ge(b_act, b * len(B_ACT) + B_ACT[name])

                def done(ins):
                    ins.then_inc(b_vec, 1)

                yield
                pe_gave("v1")
                z_sum = z_b[:, 0:NT * C]
                v4 = z_b[:, :].rearrange("p (t a d) -> p t a d", t=NT, a=L1H)
                v.memset(v4[:, :, :, L1D + 1:WAYS], 0.0)
                v.memset(v4[:, :, :, L1D], 1.0)
                for half in range(2):
                    heads = slice(half * 2, half * 2 + 2)
                    last = v.tensor_tensor(
                        v4[:, :, heads, 0:L1D],
                        bank[7][:, :].rearrange("p (t a d) -> p t a d", t=NT, a=L1H)[:, :, heads, :],
                        con("b_v1")[:, half * 32:half * 32 + 32].rearrange("p (a d) -> p a d", a=2)
                        .unsqueeze(1).to_broadcast([P, NT, 2, L1D]), ALU.add)
                done(last)
                act_gave("part_0")
                done(v.tensor_tensor(rest, qk, parts[:, 0, :], ALU.subtract))
                yield

                act_gave("part_1")
                done(v.tensor_tensor(parts[:, 2, :], rest, parts[:, 1, :], ALU.subtract))
                yield
                yield
                yield
                top = small_b[:, 4:6, 0:32].rearrange("p k (t a) -> p k t a", t=NT)
                step(v.memset(small_b[:, 5, 0:32], -3e38))
                for u in range(PAIRS):
                    hd, p = pair_of(u)
                    for n, (qt, k0, wide_) in enumerate(pair_chunks(p)):
                        dve.wait_ge(s_scores, b * 3 * PAIRS + 3 * u + n + 1)
                        v.tensor_reduce(top[:, k0 // 4, qt, hd:hd + 1], bank[3 + n][:, 0:wide_ * P],
                                        AX.X, ALU.max).then_inc(s_rowmax, 1)
                    if u % TOP_PAIRS == TOP_PAIRS - 1:
                        yield
                dve.wait_ge(s_rowmax, b * MAXIMA + 3 * PAIRS)
                top0, top1 = small_b[:, 4, 0:32], small_b[:, 5, 0:32]
                part = [tops[:, :, :, i].rearrange("p t a -> p (t a)") for i in range(PARTS)]
                v.tensor_tensor(top0, top0, top1, ALU.max).then_inc(s_rowmax, 1)
                dve.wait_ge(s_rowmax, b * MAXIMA + MAXIMA)
                step(v.tensor_scalar(top0, top0, -1.0, None, ALU.mult))
                for i in range(PARTS - 1):
                    step(v.tensor_copy(part[i], top0))
                    step(v.tensor_tensor(top0, top0, part[i], ALU.subtract))
                done(v.tensor_copy(part[PARTS - 1], top0))
                yield
                yield
                for _ in range(PAIRS + 2):
                    yield
                pe_gave("dens")
                for half in range(2):
                    cols = slice(half * 512, (half + 1) * 512)
                    step(v.reciprocal(per_den[:, cols], bank[3 + half][:, :]))
                    last = v.tensor_tensor(att[:, cols], att[:, cols], per_den[:, cols], ALU.mult)
                done(last)
                yield
                pe_gave("proj")
                step(v.tensor_tensor(v3(z_sum, NT), v3(bank[5][:, :], NT), rows_of(con("b_proj"), NT, C), ALU.add))
                step(v.tensor_tensor(z_sum, z_sum, h_mid[:, :], ALU.add))
                dve.wait_ge(out_free, b + 1)
                done(layernorm(step, small_b, sq_b, z_sum, h_b[:, :], NT, C))
                yield
                yield

                lg, e1, e2, tmp = (small_b[:, k, 0:48] for k in (7, 8, 9, 10))
                m1, m2, i1, d21 = (small_b[:, 11, k * 8:k * 8 + 8] for k in range(4))
                iota = rows_of(con("iota_e"), NT, NE)
                pe_gave("logits")
                step(v.tensor_tensor(v3(lg, NT), v3(bank[7][:, 0:48], NT), rows_of(con("rb2"), NT, NE), ALU.add))
                step(v.tensor_reduce(m1, v3(lg, NT), AX.X, ALU.max))
                done(v.tensor_tensor(v3(lg, NT), v3(lg, NT), over(m1, NE), ALU.subtract))
                yield
                act_gave("r_exp")
                step(v.tensor_reduce(m1, v3(lg, NT), AX.X, ALU.add))
                step(v.reciprocal(m1, m1))
                step(v.tensor_tensor(v3(lg, NT), v3(lg, NT), over(m1, NE), ALU.mult))

                def pick(onehot, best):
                    step(v.tensor_reduce(best, v3(lg, NT), AX.X, ALU.max))
                    step(v.tensor_tensor(v3(tmp, NT), v3(lg, NT), over(best, NE), ALU.is_lt))
                    step(v.scalar_tensor_tensor(v3(tmp, NT), v3(tmp, NT), float(2 * NE), iota, ALU.mult, ALU.add))
                    step(v.tensor_reduce(i1, v3(tmp, NT), AX.X, ALU.min))
                    step(v.tensor_tensor(v3(onehot, NT), iota, over(i1, NE), ALU.is_equal))

                pick(e1, m1)
                step(v.scalar_tensor_tensor(lg, e1, -2.0, lg, ALU.mult, ALU.add))
                pick(e2, m2)
                done(v.tensor_tensor(d21, m2, m1, ALU.subtract))
                yield
                act_gave("d_exp")
                step(v.tensor_scalar(m1, d21, 1.0, None, ALU.add))
                step(v.reciprocal(m1, m1))
                step(v.tensor_tensor(m2, d21, m1, ALU.mult))
                v.tensor_tensor(v3(e1, NT), v3(e1, NT), over(m1, NE), ALU.mult)
                step(v.tensor_tensor(v3(e2, NT), v3(e2, NT), over(m2, NE), ALU.mult))
                done(v.tensor_tensor(gates[:, :, :], v3(e1, NT), v3(e2, NT), ALU.add))
                yield
                yield
                for pr in range(3):
                    act_gave(f"e2_{pr}")
                    pe_gave(f"gb_{pr}")
                    part = a2[:, pr * 1024:(pr + 1) * 1024]
                    lo, hi = ((5, 6), (3, 4), (5, 6))[pr]
                    v.tensor_tensor(part[:, 0:512], part[:, 0:512], bank[lo][:, :], ALU.mult)
                    done(v.tensor_tensor(part[:, 512:1024], part[:, 512:1024], bank[hi][:, :], ALU.mult))
                    yield
                pe_gave("moe_y")
                v.tensor_tensor(z_sum, bank[7][:, :], h_b[:, :], ALU.add).then_inc(y_free, 1)
                dve.wait_ge(y_free, b + 2)
                step(layernorm(step, small_b, sq_b, z_sum, h_b[:, :], NT, C))
                step.end(B_STEPS, "B_STEPS")
                yield

            prepare()
            whole_program(dve, positions, front, back)


def _rows(v, n=P):
    return np.broadcast_to(np.asarray(v).reshape(1, -1), (n, np.asarray(v).size))


def _blocks(mats):
    rows, cols = sum(m.shape[0] for m in mats), sum(m.shape[1] for m in mats)
    out = np.zeros((rows, cols), np.float32)
    r = c = 0
    for m in mats:
        out[r:r + m.shape[0], c:c + m.shape[1]] = m
        r, c = r + m.shape[0], c + m.shape[1]
    return out


def _apart(m):
    out = np.zeros((P, m.shape[1]), np.float32)
    for hd in range(L1H):
        out[WAYS * hd:WAYS * hd + L1D] = m[hd * L1D:(hd + 1) * L1D]
    return out


def _shape_constants():
    line = np.linspace(-1.0, 1.0, GRID, dtype=np.float32)
    pix = (line + np.float32(1)) * np.float32(0.5) * np.float32(SIDE - 1)
    cell = np.clip(np.floor(pix), 0, SIDE - 2).astype(np.float32)
    frac = np.clip(pix - cell, 0, 1).astype(np.float32)
    tok = np.arange(N)
    gx, gy = tok % GRID, tok // GRID
    ref = np.tile(np.stack([pix[gx], pix[gy]], -1), (1, NPT))
    wx, wy = frac[gx], frac[gy]
    one = np.float32(1)
    corner = np.stack([(one - wx) * (one - wy), wx * (one - wy), (one - wx) * wy, wx * wy], -1)
    by_tile = lambda a: a.reshape(NT, P, -1).transpose(1, 0, 2).reshape(P, -1)
    i = np.arange(P)
    head = (i[:, None] // L0D == i[None, :] // L0D)
    den_spread = (i[:, None] == i[None, :] // WAYS * WAYS + L1D)
    spread = np.zeros((NE, 3 * P))
    for e in range(NE):
        spread[e, e * C:(e + 1) * C] = 1
    return cell.astype(np.int64), {
        "ident": np.eye(P), "neg_mask": np.where(i[None, :] > i[:, None], -1e30, 0.0),
        "lower": (i[None, :] < i[:, None]), "head_mask": head,
        "ref_xy": by_tile(ref), "q_corner": by_tile(corner), "iota_e": _rows(np.arange(NE)),
        "spread": spread, "den_spread": den_spread,
    }


def _layout(a):
    cell, parts = _shape_constants()
    x = a["x"]
    nb = x.shape[0]
    xc = x.transpose(0, 2, 3, 1)
    cells = np.concatenate([xc[:, :-1, :-1], xc[:, :-1, 1:], xc[:, 1:, :-1], xc[:, 1:, 1:]], -1)
    table = cells.reshape(nb * CELLS * CELLS, 4 * C)
    xq = cells[:, cell][:, :, cell].reshape(nb, NT, P, 4 * C).transpose(0, 2, 1, 3)
    xq = np.ascontiguousarray(xq).reshape(nb, P, NT * 4 * C)
    kv = np.concatenate([_blocks([a[f"L0_tok_W_{m}"].T] * 2) for m in "kv"], 1)
    mem = a["L0_attn_mem_kv"]
    w3, b3 = a["L1_attn_Wqkv"], a["L1_attn_bqkv"]
    e1, e2, e3 = (a[f"L1_ffn_expert_w{k}"] for k in (1, 2, 3))
    pairs = range(0, NE, 2)
    parts.update({
        "wq_o1": np.concatenate([a["L0_tok_W_q"].T, a["L0_tok_W_o1"]], 1),
        "b_o1": _rows(a["L0_tok_b_o1"]), "ln_g": _rows(a["L0_tok_ln_g"]), "ln_b": _rows(a["L0_tok_ln_b"]),
        "w_o2": _blocks([a["L0_tok_W_o2"]] * NT), "b_o2": _rows(a["L0_tok_b_o2"]),
        "w_kv": kv, "w_qkv": a["L0_attn_w_qkv"], "g_pre": a["L0_attn_g_pre"][:, None],
        "mem_k": mem[0].reshape(P, NMEM), "mem_v": mem[1].reshape(P, NMEM).T,
        "w_out": a["L0_attn_w_out"], "b_out": _rows(a["L0_attn_b_out"]), "g_out": _rows(a["L0_attn_g_out"]),
        "wr": np.broadcast_to(a["L0_ffn_wr"], (C, P)), "br": _rows(a["L0_ffn_br"]),
        "w1": a["L0_ffn_w1"], "b1": a["L0_ffn_b1"].reshape(2, P).T,
        "w2": np.concatenate([a["L0_ffn_w2"][:P], a["L0_ffn_w2"][P:]], 1), "b2": _rows(a["L0_ffn_b2"]),
        "w_qk": w3[:, 0:2 * C], "w_v1": w3[:, 2 * C:],
        "b_qk": b3[0:2 * C, None], "b_v1": _rows(b3[2 * C:]),
        "w_proj": _apart(a["L1_attn_Wproj"]), "b_proj": _rows(a["L1_attn_bproj"]),
        "rw1": a["L1_ffn_router_w1"], "rb1": a["L1_ffn_router_b1"][:, None],
        "rw2": a["L1_ffn_router_w2"], "rb2": _rows(a["L1_ffn_router_b2"]),
        "ew1": e1.transpose(1, 0, 2).reshape(C, NE * C), "eb1": a["L1_ffn_expert_b1"].reshape(3, P).T,
        "ew2": np.concatenate([_blocks([e2[e], e2[e + 1]]) for e in pairs], 1),
        "eb2": a["L1_ffn_expert_b2"].reshape(3, P).T,
        "ew3": np.concatenate([e3[e:e + 2].reshape(P, C) for e in pairs], 1),
        "eb3": a["L1_ffn_expert_b3"],
    })
    packed = np.zeros((P, WIDTH), np.float32)
    for name, m in parts.items():
        lo, hi = COLS[name]
        assert m.shape[1] == hi - lo, name
        packed[:m.shape[0], lo:hi] = m
    return xq, table, packed


def kernel(**inputs):
    import concourse.bacc as _bacc
    from concourse.bass_utils import run_bass_kernel_spmd as _run

    xq, table, packed = _layout({k: np.asarray(v) for k, v in inputs.items()})
    nb = xq.shape[0]
    nc = _bacc.Bacc("TRN2", target_bir_lowering=False, num_devices=1)
    arrays, args = {}, []
    for name, a in (("cells", xq), ("table", table), ("weights", packed)):
        arrays[f"in_{name}_dram"] = a
        args.append(nc.dram_tensor(f"in_{name}_dram", a.shape, F32, kind="ExternalInput").ap())
    args.append(nc.dram_tensor("out_0_dram", (nb, P, NT * C), F32, kind="ExternalOutput").ap())
    args.append(nc.dram_tensor("bounced_parts", (P, PARTS, N), BF16, kind="Internal").ap())
    tower(nc, *args)
    r = _run(nc, [arrays], core_ids=[0])
    got = r.results[0]["out_0_dram"]
    return np.ascontiguousarray(got.reshape(nb, P, NT, C).transpose(0, 2, 1, 3)).reshape(nb, N, C)
```

```python
from contextlib import ExitStack

import numpy as np

import concourse.bass as bass
from concourse import mybir

F32 = mybir.dt.float32
BF16 = mybir.dt.bfloat16
I32 = mybir.dt.int32
U32 = mybir.dt.uint32
ALU = mybir.AluOpType
ACT = mybir.ActivationFunctionType
AX = mybir.AxisListType

P = 128
NT = 8
C = 64
GRID = 32
SIDE = 128
CELLS = SIDE - 1
NPT = 8
L0H, L0D = 4, 32
L1H, L1D = 4, 16
NMEM = 4
NE = 6
KEEP = 511
N = P * NT


def pack_columns(parts):
    at, out = 0, {}
    for name, width in parts:
        out[name] = (at, at + width)
        at += width
    return out, at


COLS, WIDTH = pack_columns([
    ("ident", 128), ("neg_mask", 128), ("lower", 128), ("head_mask", 128),
    ("ref_xy", NT * NPT * 2), ("q_corner", NT * 4), ("iota_e", NE),
    ("wq_o1", 80), ("b_o1", 16), ("ln_g", 16), ("ln_b", 16), ("w_o2", 128), ("b_o2", 16),
    ("w_kv", 256), ("w_qkv", 384), ("g_pre", 1), ("mem_k", NMEM), ("mem_v", 128), ("w_out", 64),
    ("b_out", 64), ("g_out", 64), ("wr", 128), ("br", 1), ("w1", 256), ("b1", 2), ("w2", 128),
    ("b2", 64), ("w_qk", 128), ("w_v1", 64), ("b_qk", 1),
    ("b_v1", 64), ("den_spread", 128), ("w_proj", 64), ("b_proj", 64), ("rw1", 32), ("rb1", 1), ("rw2", NE),
    ("rb2", NE), ("ew1", 384), ("eb1", 3), ("ew2", 384), ("eb2", 3), ("ew3", 192), ("eb3", 64),
    ("spread", 384),
])

Q_STEPS = 33
F_STEPS = 103
B_STEPS = 66
PAIRS = L1H * NT // 2
TOP_PAIRS = 2
MAXIMA = 3 * PAIRS + 1
PARTS = 3
SPLITS = ((0, 0), (1, 0), (2, 0), (0, 1), (1, 1), (0, 2))
STACK = len(SPLITS) * L1D
SENDS = 2 * len(SPLITS)
WAYS = 2 * L1D
SAMPLING_LENGTHS = (10, 10, 10, 10, 60, 10, 10, 10, 5)
POSITION_LENGTHS = (8.4, 8, 0.38, 8)
NETWORK_LENGTHS = (7.84, 5, 19.6, 7, 6, 12, 6, 5, 4, 1.8, 8, 1.05, 8, 8, 8, 6, 8)
BACK_LENGTHS = ((4, 6, 5, 5, 60) + (10.976,) * (PAIRS // TOP_PAIRS) + (1.68, 24) + (3.08,) * (PAIRS + 2)
                + (4.9, 14, 4, 9, 10, 8, 2.94, 8, 2.8, 4, 22.68))


def places(*names):
    return {name: k + 1 for k, name in enumerate(names)}


F_PE = places("x0T", "kT", "v_lo", "vq", "ek_tok", "ctxT", "lin_w", "q_tok", "lin_y", "x1T",
              "w_row", "w_col", "hid0", "hid1", "mlp_y")
F_ACT = places("x0T", "ekT", "v_hi", "q_exp", "ek_tok", "q_tok", "x1T", "w_row", "hid0", "hid1")
F_VEC = places("x0", "neg_kmax", "q_shift", "q_soft", "ctx", "lin_w", "x1", "w_col", "x2")
B_PE = places("x2T", "qk", "v1", "q_top", "attended", "dens", "proj", "x3T", "router_h", "e1_0", "logits", "e2_0",
              "e1_1", "e2_1", "e1_2", "e2_2", "gate_t", "gb_0", "gb_1", "gb_2", "moe_y")
B_ACT = places("x2T", "part_0", "part_1", "q_top", "att", "x3T", "router_h", "e1_0", "r_exp", "e2_0", "e1_1",
               "d_exp", "e2_1", "e1_2", "e2_2", "gate_t")
B_VEC = places("v1", "rest", "part_2", "tops", "o", "x3", "r_shift", "d21", "gates", "g_0", "g_1", "g_2")


def pair_of(u):
    return divmod(u, NT // 2)


def pair_chunks(p):
    return (NT - 1 - p, 0, 4), (NT - 1 - p, 4, 4 - p), (p, 0, p + 1)


def weave(front, front_lengths, back, back_lengths):
    i = j = 0
    while i < len(front_lengths) or j < len(back_lengths):
        front_at = sum(front_lengths[:i + 1]) / sum(front_lengths)
        back_at = sum(back_lengths[:j + 1]) / sum(back_lengths)
        if i < len(front_lengths) and (j == len(back_lengths) or front_at <= back_at):
            next(front)
            i += 1
        else:
            next(back)
            j += 1
    assert next(front, None) is None and next(back, None) is None


def tower(nc, xq, table, packed, out, bounced):
    nb = xq.shape[0]
    ctx = ExitStack()
    with ctx:
        def sb(name, shape, dt=F32):
            return ctx.enter_context(nc.sbuf_tensor(name, shape, dt))

        def sem(name):
            return ctx.enter_context(nc.semaphore(name))

        bank = [ctx.enter_context(nc.psum_tensor(f"bank{i}", [P, 512], F32)) for i in range(8)]

        consts = sb("consts", [P, WIDTH])

        def con(name, rows=P):
            a, z = COLS[name]
            return consts[0:rows, a:z]

        gathered = sb("gathered", [P, NT, NPT * 4 * C])
        cells_q = sb("cells_q", [P, NT, 4, C])
        corner_w = sb("corner_w", [P, NT * NPT, 4])
        cell_idx = sb("cell_idx", [P, NT * NPT], U32)
        base_cell = sb("base_cell", [P, 1])
        queries = sb("queries", [P, NT, C])
        samples = sb("samples", [P, 2, NPT * C])
        samples_t = sb("samples_t", [P, 2, 512])
        front_work = sb("front_work", [P, 5120])
        back_work = sb("back_work", [P, 5120])
        feats_f = sb("feats_f", [P, 512])
        feats_b = sb("feats_b", [P, 512])
        parts = sb("parts", [P, PARTS, 1024], BF16)
        q_stack = sb("q_stack", [P, L1H, 1024], BF16)
        k_stack = sb("k_stack", [P, L1H, 1024], BF16)
        top_rows = parts[0:L1H * PARTS, 0, :]
        ident_h = sb("ident_h", [P, P], BF16)
        mask_h = sb("mask_h", [P, P], BF16)
        tops = sb("tops", [P, NT, L1H, PARTS], BF16)
        prod = sb("prod", [P, 512])
        score = sb("score", [P, 512])
        h_f = sb("h_f", [P, NT * C])
        h_mid = sb("h_mid", [P, NT * C])
        h_b = sb("h_b", [P, NT * C])
        z_f = sb("z_f", [P, NT * C])
        z_b = sb("z_b", [P, NT * L1H * WAYS])
        sq_f = sb("sq_f", [P, NT * C])
        sq_b = sb("sq_b", [P, NT * C])
        small_f = sb("small_f", [P, 16, 64])
        small_b = sb("small_b", [P, 16, 64])
        qs = sb("qs", [P, 11, 128])
        wsum = sb("wsum", [P, 4])
        mem_max = sb("mem_max", [P, 1])
        w_lin = sb("w_lin", [P, 64])
        ctx_m = sb("ctx_m", [P, 128])
        emk = sb("emk", [P, NMEM])
        emk_t = sb("emk_t", [NMEM, 128])
        gate_parts = sb("gate_parts", [P, NT, PARTS * NE], BF16)
        spread_h = sb("spread_h", [PARTS * NE, 3 * P], BF16)
        eb3_h = sb("eb3_h", [PARTS * NE, PARTS * C], BF16)

        loaded = sem("consts_loaded")
        const_ready = sem("const_ready")
        prepared = sem("bias_part_ready")
        qcells = sem("qcells_loaded")
        q_step = sem("positions_step")
        f_step = sem("front_step")
        b_step = sem("back_step")
        qfeat_ready = sem("qfeat_ready")
        q_pe = sem("positions_product")
        q_act = sem("positions_copied")
        q_read = sem("hidden_normed")
        offs_ready = sem("hidden_ready")
        idx_ready = sem("idx_ready")
        tile_gathered = [sem(f"tile_gathered{t}") for t in range(NT)]
        weighed = sem("corners_weighed")
        added = sem("corners_added")
        samp_ready = sem("samp_ready")
        samp_turned = sem("samp_turned")
        samp_copied = sem("samp_copied")
        kv_ready = sem("kv_ready")
        v_copied = sem("v_copied")
        k_used = sem("k_used")
        shifted = sem("score_shifted")
        exped = sem("score_exped")
        f_pe, f_act, f_vec = sem("front_product"), sem("front_mapped"), sem("front_vector")
        b_pe, b_act, b_vec = sem("back_product"), sem("back_mapped"), sem("back_vector")
        s_scores = sem("scores_ready")
        s_rowmax = sem("rowmax_ready")
        s_logits = sem("shifted_scores_ready")
        s_probs = sem("probs_ready")
        pe_passed = sem("pe_passed")
        pool_passed = sem("pool_passed")
        stored = sem("stored")
        parts_sent = sem("parts_sent")
        parts_stacked = sem("parts_stacked")
        tops_stacked = sem("tops_stacked")
        out_free = sem("out_free")
        y_free = sem("experts_sum_read")

        ident = con("ident")

        def fw(col0, width, rows=P):
            return front_work[0:rows, col0:col0 + width]

        def bw(col0, width, rows=P):
            return back_work[0:rows, col0:col0 + width]

        values = fw(0, 4096).rearrange("p (t m) -> p t m", t=NT)
        v_lin, ek_t, ek, q_soft, q_t = (fw(1024 * k, 1024) for k in range(5))
        hidden, w_row, junk = fw(0, 2048), fw(2048, 1024), fw(3072, 1024)
        qk, rest = bw(0, 1024), bw(1024, 1024)
        probs = bw(0, 4 * 9 * P).rearrange("p (s c) -> p s c", s=4)
        att, per_den = bw(0, 1024), bw(1024, 1024)
        a1, a2, r_h, g_t = bw(0, 1024), bw(1024, 3072), bw(4096, 1024, 32), parts[0:PARTS * NE, 0, :]

        def whole_program(engine, positions, front, back):
            for _ in positions(0):
                pass
            for _ in front(0, positions):
                pass
            with engine.Fori(0, nb - 2) as b:
                weave(front(b + 1, positions), SAMPLING_LENGTHS + POSITION_LENGTHS + NETWORK_LENGTHS,
                      back(b), BACK_LENGTHS)
            weave(front(nb - 1, None), SAMPLING_LENGTHS + NETWORK_LENGTHS, back(nb - 2), BACK_LENGTHS)
            for _ in back(nb - 1):
                pass

        block = ctx.enter_context(nc.Block())

        @block.sync
        def _(sp):
            sp.dma_start(consts[:, :], packed).then_inc(loaded, 16)

            def load_cells(b, first):
                if not first:
                    sp.wait_ge(qfeat_ready, b)
                sp.dma_start(cells_q[:, :, :, :].rearrange("p t k c -> p (t k c)"),
                             xq[b]).then_inc(qcells, 16)

            def stack_parts(b):
                for i in range(PARTS):
                    if i < 2:
                        sp.wait_ge(b_act, b * len(B_ACT) + B_ACT[f"part_{i}"])
                    else:
                        sp.wait_ge(b_vec, b * len(B_VEC) + B_VEC["part_2"])
                    sp.dma_start(bounced[:, i, :], parts[:, i, :]).then_inc(parts_sent, 16)
                sp.wait_ge(parts_sent, 16 * PARTS * b + 16 * PARTS)
                for n, of_pair in enumerate(SPLITS):
                    for side, stack in enumerate((q_stack, k_stack)):
                        src = bounced[side * C:(side + 1) * C, of_pair[side], :]
                        sp.dma_start(stack[n * L1D:(n + 1) * L1D, :, :],
                                     src.rearrange("(a d) c -> d a c", d=L1D)).then_inc(parts_stacked, 16)

            def stack_tops(b):
                sp.wait_ge(b_act, b * len(B_ACT) + B_ACT["q_top"])
                for hd in range(L1H):
                    sp.dma_start(q_stack[STACK:STACK + PARTS, hd, :],
                                 parts[hd * PARTS:(hd + 1) * PARTS, 0, :]).then_inc(tops_stacked, 16)

            def store(b):
                sp.wait_ge(b_step, b * B_STEPS + B_STEPS)
                sp.dma_start(out[b], h_b[:, :]).then_inc(stored, 16)
                sp.wait_ge(stored, 16 * b + 16)
                sp.sem_inc(out_free, 1)

            sp.sem_inc(out_free, 1)
            load_cells(0, True)
            load_cells(1, False)
            with sp.Fori(0, nb - 2) as b:
                load_cells(b + 2, False)
                stack_parts(b)
                stack_tops(b)
                store(b)
            for last in (nb - 2, nb - 1):
                stack_parts(last)
                stack_tops(last)
                store(last)

        @block.gpsimd
        def _(pool):
            def gather(b, t, first):
                if not first:
                    pool.wait_ge(samp_ready, (b - 1) * NT + t + 1)
                    pool.sem_inc(pool_passed, 1)
                for p in range(NPT):
                    j = t * NPT + p
                    pool.indirect_dma_start(
                        out=gathered[:, t, p * 4 * C:(p + 1) * 4 * C], out_offset=None,
                        in_=table,
                        in_offset=bass.IndirectOffsetOnAxis(ap=cell_idx[:, j:j + 1], axis=0),
                    ).then_inc(tile_gathered[t], 16)

            def add_corners(b, t):
                pool.wait_ge(weighed, b * NT + t + 1)
                pool.sem_inc(pool_passed, 1)
                g4 = gathered[:, t, :].rearrange("p (s y c) -> p s y c", s=NPT, y=2)
                nc.gpsimd.tensor_tensor(g4[:, :, 0, :], g4[:, :, 0, :], g4[:, :, 1, :],
                                        ALU.add).then_inc(added, 1)
                pool.wait_ge(added, b * NT + t + 1)
                if t >= 2:
                    pool.wait_ge(samp_turned, b * NT + t - 1)
                pool.sem_inc(pool_passed, 1)
                nc.gpsimd.tensor_tensor(samples[:, t % 2, :].rearrange("p (s c) -> p s c", s=NPT),
                                        g4[:, :, 0, 0:C], g4[:, :, 0, C:2 * C], ALU.add).then_inc(samp_ready, 1)

            pool.wait_ge(idx_ready, 1)
            for t in range(NT):
                gather(0, t, True)
                if t >= 2:
                    add_corners(0, t - 2)
            add_corners(0, NT - 2)
            add_corners(0, NT - 1)
            with pool.Fori(1, nb) as b:
                pool.wait_ge(idx_ready, b + 1)
                for t in range(NT):
                    gather(b, t, False)
                for t in range(NT):
                    add_corners(b, t)

        @block.tensor
        def _(pe):
            pe.wait_ge(const_ready, 1)
            pe.sem_inc(y_free, 1)

            def alone():
                pe.sem_inc(pe_passed, 1)

            def turn_tiles(src, bk):
                for t in range(0, NT, 2):
                    last = nc.tensor.transpose(bk[:, t * C:t * C + P], src[:, t * C:t * C + P], ident)
                return last

            def of_parity(odd):
                return slice(odd * C, odd * C + C)

            def wide_pairs(weights, rows, lo, hi, src):
                for odd, bk in enumerate((lo, hi)):
                    last = nc.tensor.matmul(bk[0:rows, :], weights[of_parity(odd), :],
                                            src[of_parity(odd), :], start=True, stop=True)
                return last

            def per_tile_of(odd, weights, width, dst, src):
                for n in range(NT // 2):
                    last = nc.tensor.matmul(dst[:, n * width:(n + 1) * width],
                                            src[of_parity(odd), n * P:(n + 1) * P],
                                            weights[of_parity(odd), :], start=True, stop=True)
                return last

            def wide(weights, rows, lo, hi, src):
                for n, bk in enumerate((lo, hi)):
                    last = nc.tensor.matmul(bk[0:rows, :], weights, src[:, n * 512:(n + 1) * 512],
                                            start=True, stop=True)
                return last

            def per_tile(weights, width, dst, src, tiles=range(NT)):
                for n, t in enumerate(tiles):
                    last = nc.tensor.matmul(dst[:, n * width:(n + 1) * width],
                                            src[:, t * P:(t + 1) * P], weights, start=True, stop=True)
                return last

            def positions(b):
                pe.wait_ge(qfeat_ready, b + 1)
                alone()
                turn_tiles(sq_f, bank[0]).then_inc(q_pe, 1)
                yield
                pe.wait_ge(q_act, b * 2 + 1)
                for odd in range(2):
                    last = per_tile_of(odd, con("wq_o1"), 80, bank[odd], feats_f)
                last.then_inc(q_pe, 1)
                yield
                pe.wait_ge(offs_ready, b + 1)
                nc.tensor.transpose(bank[2][:, 0:P], qs[:, 1, :], ident).then_inc(q_pe, 1)
                yield
                pe.wait_ge(q_act, b * 2 + 2)
                nc.tensor.matmul(bank[2][:, P:2 * P], qs[:, 2, :], con("w_o2"),
                                 start=True, stop=True).then_inc(q_pe, 1)
                yield

            def front(b, following):
                def given(sem_, table_, name):
                    pe.wait_ge(sem_, b * len(table_) + table_[name])

                def done(ins):
                    ins.then_inc(f_pe, 1)

                def project(t):
                    pe.wait_ge(samp_copied, b * NT + t + 1)
                    if t >= 1:
                        pe.wait_ge(k_used, b * NT + t)
                        pe.wait_ge(v_copied, b * NT + t)
                    for kv in range(2):
                        for g in range(4):
                            last = nc.tensor.matmul(bank[1 + kv][:, g * P:(g + 1) * P],
                                                    samples_t[:, t % 2, g * P:(g + 1) * P],
                                                    con("w_kv")[:, kv * P:(kv + 1) * P],
                                                    start=True, stop=True)
                    last.then_inc(kv_ready, 1)

                def turn(t):
                    pe.wait_ge(samp_ready, b * NT + t + 1)
                    for g in range(4):
                        last = nc.tensor.transpose(bank[0][:, g * P:(g + 1) * P],
                                                   samples[:, t % 2, g * P:(g + 1) * P], ident)
                    last.then_inc(samp_turned, 1)

                for t in range(NT + 1):
                    if t >= 1:
                        project(t - 1)
                    if t < NT:
                        turn(t)
                    yield
                if following:
                    yield from following(b + 1)
                yield
                yield
                yield
                given(f_vec, F_VEC, "x0")
                alone()
                done(turn_tiles(z_f, bank[0]))
                yield
                given(f_act, F_ACT, "x0T")
                wq = con("w_qkv")
                done(wide_pairs(wq[:, 128:256], P, bank[0], bank[1], feats_f))
                done(per_tile_of(0, wq[:, 256:384], P, bank[2], feats_f))
                yield
                given(f_act, F_ACT, "ekT")
                per_tile_of(1, wq[:, 256:384], P, bank[0], feats_f)
                per_tile_of(0, wq[:, 0:128], P, bank[1], feats_f)
                done(per_tile_of(1, wq[:, 0:128], P, bank[2], feats_f))
                yield
                given(f_act, F_ACT, "v_hi")
                given(f_vec, F_VEC, "q_shift")
                for t in range(NT):
                    nc.tensor.transpose(bank[t // 4][:, (t % 4) * P:(t % 4 + 1) * P],
                                        ek_t[:, t * P:(t + 1) * P], ident)
                done(nc.tensor.transpose(bank[2][0:NMEM, 0:P], emk[:, :], ident))
                yield
                given(f_act, F_ACT, "ek_tok")
                for t in range(NT):
                    nc.tensor.matmul(bank[2][:, 0:P], v_lin[:, t * P:(t + 1) * P],
                                     ek[:, t * P:(t + 1) * P], start=(t == 0), stop=False)
                done(nc.tensor.matmul(bank[2][:, 0:P], con("mem_v", NMEM), emk_t[:, :],
                                      start=False, stop=True))
                yield
                given(f_vec, F_VEC, "ctx")
                done(nc.tensor.matmul(bank[2][:, P:P + C], ctx_m[:, :], con("w_out"), start=True, stop=True))
                given(f_vec, F_VEC, "q_soft")
                for t in range(NT):
                    last = nc.tensor.transpose(bank[t // 4][:, (t % 4) * P:(t % 4 + 1) * P],
                                               q_soft[:, (t % 2 * 4 + t // 2) * P:(t % 2 * 4 + t // 2 + 1) * P],
                                               ident)
                done(last)
                yield
                given(f_act, F_ACT, "q_tok")
                given(f_vec, F_VEC, "lin_w")
                done(per_tile(w_lin[:, :], C, bank[2], q_t))
                yield
                given(f_vec, F_VEC, "x1")
                alone()
                done(turn_tiles(h_f, bank[0]))
                yield
                given(f_act, F_ACT, "x1T")
                done(wide_pairs(con("wr"), P, bank[0], bank[1], feats_f))
                given(f_act, F_ACT, "w_row")
                alone()
                for t in range(NT):
                    last = nc.tensor.transpose(bank[2][:, t:t + 1], w_row[0:1, t * P:(t + 1) * P],
                                               ident[0:1, 0:1])
                done(last)
                yield
                done(wide_pairs(con("w1")[:, 0:P], P, bank[0], bank[1], feats_f))
                yield
                given(f_act, F_ACT, "hid0")
                done(wide_pairs(con("w1")[:, P:2 * P], P, bank[0], bank[1], feats_f))
                yield
                given(f_act, F_ACT, "hid1")
                given(f_vec, F_VEC, "w_col")
                for t in range(NT):
                    for half in range(2):
                        last = nc.tensor.matmul(bank[2][:, t * C:(t + 1) * C],
                                                hidden[:, half * 1024 + t * P:half * 1024 + (t + 1) * P],
                                                con("w2")[:, half * C:(half + 1) * C],
                                                start=(half == 0), stop=(half == 1))
                done(last)
                yield
                yield
                yield

            def back(b):
                def given(sem_, table_, name):
                    pe.wait_ge(sem_, b * len(table_) + table_[name])

                def done(ins):
                    ins.then_inc(b_pe, 1)

                given(f_vec, F_VEC, "x2")
                alone()
                done(turn_tiles(h_mid, bank[3]))
                yield
                given(b_act, B_ACT, "x2T")
                done(wide_pairs(con("w_qk"), P, bank[3], bank[4], feats_b))
                pe.wait_ge(y_free, b + 1)
                alone()
                per_tile_of(0, con("w_v1"), C, bank[7], feats_b)
                done(per_tile_of(1, con("w_v1"), C, bank[5], feats_b))
                yield
                yield
                yield
                yield

                def top_scores(u):
                    hd, p = pair_of(u)
                    for n, (qt, k0, wide_) in enumerate(pair_chunks(p)):
                        if u:
                            pe.wait_ge(s_rowmax, b * MAXIMA + 3 * (u - 1) + n + 1)
                        diag = qt < k0 + wide_
                        last = nc.tensor.matmul(bank[3 + n][:, 0:wide_ * P], q_stack[0:STACK, hd, qt * P:(qt + 1) * P],
                                                k_stack[0:STACK, hd, k0 * P:(k0 + wide_) * P], start=True, stop=not diag)
                        if diag:
                            at = (qt - k0) * P
                            last = nc.tensor.matmul(bank[3 + n][:, at:at + P], ident_h[:, :], mask_h[:, :],
                                                    start=False, stop=True)
                        last.then_inc(s_scores, 1)

                def shifted_scores(u):
                    hd, p = pair_of(u)
                    for n, (far, q0, wide_) in enumerate(pair_chunks(p)):
                        if u:
                            pe.wait_ge(s_probs, b * 3 * PAIRS + 3 * (u - 1) + n + 1)
                        kt, q0 = NT - 1 - far, NT - q0 - wide_
                        diag = kt >= q0
                        last = nc.tensor.matmul(bank[3 + n][:, 0:wide_ * P], k_stack[0:STACK + PARTS, hd, kt * P:(kt + 1) * P],
                                                q_stack[0:STACK + PARTS, hd, q0 * P:(q0 + wide_) * P], start=True, stop=not diag)
                        if diag:
                            at = (kt - q0) * P
                            last = nc.tensor.matmul(bank[3 + n][:, at:at + P], mask_h[:, :], ident_h[:, :],
                                                    start=False, stop=True)
                        last.then_inc(s_logits, 1)

                def attend(u):
                    hd, p = pair_of(u)
                    col = 0
                    for n, (far, q0, wide_) in enumerate(pair_chunks(p)):
                        pe.wait_ge(s_probs, b * 3 * PAIRS + 3 * u + n + 1)
                        kt, q0 = NT - 1 - far, NT - q0 - wide_
                        at = q0 % 4 * P
                        last = nc.tensor.matmul(bank[6 + q0 // 4][hd * WAYS:(hd + 1) * WAYS, at:at + wide_ * P],
                                                z_b[:, (kt * L1H + hd) * WAYS:(kt * L1H + hd + 1) * WAYS],
                                                probs[:, u % 4, col:col + wide_ * P],
                                                start=(kt == 0), stop=(kt == 3 + q0 // 4))
                        col += wide_ * P
                    return last

                pe.wait_ge(parts_stacked, 16 * SENDS * b + 16 * SENDS)
                for u in range(PAIRS):
                    top_scores(u)
                    if u % TOP_PAIRS == TOP_PAIRS - 1:
                        yield
                given(b_vec, B_VEC, "tops")
                alone()
                for t in range(NT):
                    last = nc.tensor.matmul(bank[3 + t // 4][0:L1H * PARTS, (t % 4) * P:(t % 4 + 1) * P],
                                            tops[:, t, :, :].rearrange("p a i -> p (a i)"), ident_h[:, :],
                                            start=True, stop=True)
                done(last)
                yield
                yield
                pe.wait_ge(tops_stacked, 16 * L1H * b + 16 * L1H)
                for u in range(PAIRS + 2):
                    if u < PAIRS:
                        shifted_scores(u)
                    if u == PAIRS + 1:
                        done(attend(u - 2))
                    elif u >= 2:
                        attend(u - 2)
                    yield
                given(b_act, B_ACT, "att")
                done(wide(con("den_spread"), P, bank[3], bank[4], att))
                yield
                given(b_vec, B_VEC, "o")
                done(per_tile(con("w_proj"), C, bank[5], att))
                yield
                given(b_vec, B_VEC, "x3")
                alone()
                done(turn_tiles(h_b, bank[3]))
                yield

                def layer1(pr):
                    done(wide_pairs(con("ew1")[:, pr * P:(pr + 1) * P], P, bank[3], bank[4], feats_b))

                def layer2(pr):
                    done(wide(con("ew2")[:, pr * P:(pr + 1) * P], P, bank[5], bank[6], a1))

                def spread_gates(pr, lo, hi):
                    done(wide(spread_h[:, pr * P:(pr + 1) * P], P, bank[lo], bank[hi], g_t))

                given(b_act, B_ACT, "x3T")
                alone()
                done(wide_pairs(con("rw1"), 32, bank[5], bank[6], feats_b))
                layer1(0)
                given(b_act, B_ACT, "router_h")
                done(per_tile(con("rw2", 32), NE, bank[7], r_h))
                yield
                given(b_act, B_ACT, "e1_0")
                layer2(0)
                layer1(1)
                yield
                given(b_act, B_ACT, "e1_1")
                layer2(1)
                layer1(2)
                yield
                given(b_act, B_ACT, "e1_2")
                layer2(2)
                given(b_vec, B_VEC, "gates")
                for t in range(NT):
                    last = nc.tensor.matmul(bank[3 + t // 4][0:PARTS * NE, (t % 4) * P:(t % 4 + 1) * P],
                                            gate_parts[:, t, :], ident_h[:, :], start=True, stop=True)
                done(last)
                yield
                given(b_act, B_ACT, "gate_t")
                spread_gates(0, 5, 6)
                yield
                spread_gates(1, 3, 4)
                yield
                given(b_vec, B_VEC, "g_0")
                spread_gates(2, 5, 6)
                yield
                given(b_vec, B_VEC, "g_2")
                for t in range(NT):
                    dst = bank[7][:, t * C:(t + 1) * C]
                    for pr in range(3):
                        nc.tensor.matmul(dst, a2[:, pr * 1024 + t * P:pr * 1024 + (t + 1) * P],
                                         con("ew3")[:, pr * C:(pr + 1) * C], start=(pr == 0), stop=False)
                    for i in range(PARTS):
                        last = nc.tensor.matmul(dst, g_t[:, t * P:(t + 1) * P], eb3_h[:, i * C:(i + 1) * C],
                                                start=False, stop=(i == PARTS - 1))
                done(last)
                yield

            whole_program(pe, positions, front, back)

        @block.scalar
        def _(act):
            act.wait_ge(const_ready, 1)

            def copy_pair(dst, lo, hi, rows=P):
                nc.scalar.copy(dst[:, 0:512], bank[lo][0:rows, :])
                return nc.scalar.copy(dst[:, 512:1024], bank[hi][0:rows, :])

            def mapped(dst, lo, hi, func, bias, rows=P, scale=1.0):
                nc.scalar.activation(dst[:, 0:512], bank[lo][0:rows, :], func, bias=bias, scale=scale)
                return nc.scalar.activation(dst[:, 512:1024], bank[hi][0:rows, :], func, bias=bias, scale=scale)

            def tiles_of(ap, odd):
                return ap.rearrange("p (t o c) -> p t o c", o=2, c=P)[:, :, odd, :]

            def by_tile(ap):
                return ap.rearrange("p (t c) -> p t c", c=P)

            def mapped_pairs(dst, lo, hi, func, bias, rows=P):
                for odd, bk in enumerate((lo, hi)):
                    last = nc.scalar.activation(tiles_of(dst, odd), by_tile(bank[bk][0:rows, :]), func, bias=bias)
                return last

            def positions(b):
                act.wait_ge(q_pe, b * 4 + 1)
                nc.scalar.copy(feats_f[:, :], bank[0][:, :]).then_inc(q_act, 1)
                yield
                act.wait_ge(q_read, b + 1)
                nc.scalar.activation(qs[:, 1, :], qs[:, 0, :], ACT.Gelu_apprx_tanh).then_inc(offs_ready, 1)
                yield
                act.wait_ge(q_pe, b * 4 + 3)
                nc.scalar.copy(qs[:, 2, :], bank[2][:, 0:P]).then_inc(q_act, 1)
                yield
                yield

            def front(b, following):
                def pe_gave(name):
                    act.wait_ge(f_pe, b * len(F_PE) + F_PE[name])

                def vec_gave(name):
                    act.wait_ge(f_vec, b * len(F_VEC) + F_VEC[name])

                def done(ins):
                    ins.then_inc(f_act, 1)

                for t in range(NT + 1):
                    if t >= 1:
                        act.wait_ge(kv_ready, b * NT + t)
                        nc.scalar.copy(values[:, t - 1, :], bank[2][:, :]).then_inc(v_copied, 1)
                    if t < NT:
                        act.wait_ge(samp_turned, b * NT + t + 1)
                        nc.scalar.copy(samples_t[:, t % 2, :], bank[0][:, :]).then_inc(samp_copied, 1)
                    yield
                if following:
                    yield from following(b + 1)
                act.wait_ge(shifted, b + 1)
                nc.scalar.activation(score[:, :], score[:, :], ACT.Exp,
                                     scale=float(C // NPT) ** -0.5).then_inc(exped, 1)
                yield
                yield
                yield
                pe_gave("x0T")
                done(nc.scalar.copy(feats_f[:, :], bank[0][:, :]))
                yield
                vec_gave("neg_kmax")
                neg = small_f[:, 3, 3:4]
                nc.scalar.activation(tiles_of(ek_t, 0), by_tile(bank[0][:, :]), ACT.Exp, bias=neg, accum_out=wsum[:, 0:1])
                nc.scalar.activation(tiles_of(ek_t, 1), by_tile(bank[1][:, :]), ACT.Exp, bias=neg, accum_out=wsum[:, 1:2])
                nc.scalar.activation(emk[:, :], con("mem_k"), ACT.Exp, bias=neg, accum_out=wsum[:, 2:3])
                pe_gave("v_lo")
                done(nc.scalar.copy(tiles_of(v_lin, 0), by_tile(bank[2][:, :])))
                yield
                pe_gave("vq")
                done(nc.scalar.copy(tiles_of(v_lin, 1), by_tile(bank[0][:, :])))
                vec_gave("q_shift")
                done(nc.scalar.activation(q_soft, q_soft, ACT.Exp))
                yield
                pe_gave("ek_tok")
                copy_pair(ek, 0, 1)
                done(nc.scalar.copy(emk_t[:, :], bank[2][0:NMEM, 0:P]))
                yield
                yield
                pe_gave("q_tok")
                done(copy_pair(q_t, 0, 1))
                yield
                yield
                pe_gave("x1T")
                done(nc.scalar.copy(feats_f[:, :], bank[0][:, :]))
                yield
                pe_gave("w_row")
                done(mapped_pairs(w_row, 0, 1, ACT.Identity, con("br")))
                yield
                pe_gave("hid0")
                done(mapped_pairs(hidden[:, 0:1024], 0, 1, ACT.Gelu_apprx_tanh, con("b1")[:, 0:1]))
                yield
                pe_gave("hid1")
                done(mapped_pairs(hidden[:, 1024:2048], 0, 1, ACT.Gelu_apprx_tanh, con("b1")[:, 1:2]))
                yield
                yield
                yield
                yield

            def back(b):
                def pe_gave(name):
                    act.wait_ge(b_pe, b * len(B_PE) + B_PE[name])

                def vec_gave(name):
                    act.wait_ge(b_vec, b * len(B_VEC) + B_VEC[name])

                def done(ins):
                    ins.then_inc(b_act, 1)

                pe_gave("x2T")
                done(nc.scalar.copy(feats_b[:, :], bank[3][:, :]))
                yield
                pe_gave("qk")
                mapped_pairs(qk, 3, 4, ACT.Identity, con("b_qk"))
                done(mapped_pairs(parts[:, 0, :], 3, 4, ACT.Identity, con("b_qk")))
                yield
                vec_gave("rest")
                done(nc.scalar.copy(parts[:, 1, :], rest))
                yield
                yield
                yield
                for _ in range(PAIRS // TOP_PAIRS):
                    yield
                pe_gave("q_top")
                done(copy_pair(top_rows, 3, 4, L1H * PARTS))
                yield
                yield
                for u in range(PAIRS + 2):
                    if u < PAIRS:
                        col = 0
                        for n, (_, _, wide_) in enumerate(pair_chunks(pair_of(u)[1])):
                            act.wait_ge(s_logits, b * 3 * PAIRS + 3 * u + n + 1)
                            nc.scalar.activation(probs[:, u % 4, col:col + wide_ * P],
                                                 bank[3 + n][:, 0:wide_ * P], ACT.Exp).then_inc(s_probs, 1)
                            col += wide_ * P
                    yield
                pe_gave("attended")
                done(copy_pair(att, 6, 7))
                yield
                yield
                pe_gave("x3T")
                done(nc.scalar.copy(feats_b[:, :], bank[3][:, :]))
                yield

                def relu1(pr):
                    pe_gave(f"e1_{pr}")
                    done(mapped_pairs(a1, 3, 4, ACT.Relu, con("eb1")[:, pr:pr + 1]))

                def relu2(pr):
                    pe_gave(f"e2_{pr}")
                    done(mapped(a2[:, pr * 1024:(pr + 1) * 1024], 5, 6, ACT.Relu, con("eb2")[:, pr:pr + 1]))

                lg, d21 = small_b[:, 7, 0:48], small_b[:, 11, 24:32]
                pe_gave("router_h")
                done(mapped_pairs(r_h, 5, 6, ACT.Relu, con("rb1", 32), rows=32))
                relu1(0)
                vec_gave("r_shift")
                done(nc.scalar.activation(lg, lg, ACT.Exp))
                yield
                relu2(0)
                relu1(1)
                vec_gave("d21")
                done(nc.scalar.activation(d21, d21, ACT.Exp))
                yield
                relu2(1)
                relu1(2)
                yield
                relu2(2)
                pe_gave("gate_t")
                done(copy_pair(g_t, 3, 4, PARTS * NE))
                yield
                yield
                yield
                yield
                yield

            whole_program(act, positions, front, back)

        @block.vector
        def _(dve):
            v = nc.vector

            class Steps:

                def __init__(self, sem_, base):
                    self.sem, self.base, self.n = sem_, base, 0

                def __call__(self, ins):
                    self.n += 1
                    ins.then_inc(self.sem, 1)
                    dve.wait_ge(self.sem, self.base + self.n)

                def end(self, per, what):
                    assert self.n == per, (what, self.n)

            def v3(ap, a):
                return ap.rearrange("p (a c) -> p a c", a=a)

            def rows_of(ap, n, m):
                return ap.unsqueeze(1).to_broadcast([P, n, m])

            def over(ap, m):
                return ap.unsqueeze(2).to_broadcast([P, ap.shape[1], m])

            def inverse_root(step, sm, x, n):
                y, half, t = sm[:, 13, 0:n], sm[:, 14, 0:n], sm[:, 15, 0:n]
                v.tensor_scalar(half, x, -0.5, None, ALU.mult)
                step(v.tensor_scalar(y.bitcast(I32), x.bitcast(I32), -0.5, 1597463007.0, ALU.mult, ALU.add))
                for last in (False, False, True):
                    step(v.tensor_tensor(t, y, y, ALU.mult))
                    step(v.tensor_tensor(t, t, half, ALU.mult))
                    step(v.scalar_tensor_tensor(x if last else y, t, 1.5, y, ALU.add, ALU.mult))

            def layernorm(step, sm, sq, x, dst, groups, width):
                s, d = sm[:, 0, 0:groups], v3(x, groups)
                step(v.tensor_reduce(s, d, AX.X, ALU.add))
                step(v.scalar_tensor_tensor(d, over(s, width), -1.0 / width, d, ALU.mult, ALU.add))
                q = v3(sq[:, 0:groups * width], groups)
                step(v.tensor_tensor(q, d, d, ALU.mult))
                step(v.tensor_reduce(s, q, AX.X, ALU.add))
                step(v.tensor_scalar(s, s, 1.0 / width, 1e-5, ALU.mult, ALU.add))
                inverse_root(step, sm, s, groups)
                return v.tensor_tensor(v3(dst, groups), d, over(s, width), ALU.mult)

            def in_parts(step, x, dst, groups, done):
                for i in range(PARTS - 1):
                    step(v.tensor_copy(dst[i], v3(x, groups)))
                    step(v.tensor_tensor(v3(x, groups), v3(x, groups), dst[i], ALU.subtract))
                done(v.tensor_copy(dst[PARTS - 1], v3(x, groups)))

            def inverse_norm(step, x):
                s = small_f[:, 0, 0:NT]
                step(v.tensor_tensor(sq_f[:, :], x, x, ALU.mult))
                step(v.tensor_reduce(s, v3(sq_f[:, :], NT), AX.X, ALU.add))
                step(v.tensor_scalar(s, s, 1e-24, None, ALU.max))
                inverse_root(step, small_f, s, NT)
                return s

            def prepare():
                dve.wait_ge(loaded, 16)
                v.tensor_scalar(con("w_qkv"), con("w_qkv"), con("g_pre"), float(C) ** 0.5,
                                ALU.mult, ALU.mult)
                v.tensor_scalar(con("g_out"), con("g_out"), float(C) ** 0.5, None, ALU.mult)
                v.tensor_scalar(con("w_qk")[:, 0:C], con("w_qk")[:, 0:C], L1D ** -0.5, None, ALU.mult)
                v.tensor_scalar(con("b_qk", C), con("b_qk", C), L1D ** -0.5, None, ALU.mult)
                v.tensor_reduce(mem_max[:, :], con("mem_k"), AX.X, ALU.max)
                v.tensor_copy(ident_h[:, :], ident)
                v.tensor_copy(mask_h[:, :], con("neg_mask"))
                v.tensor_copy(spread_h[:, :], con("spread", PARTS * NE))
                b3 = con("eb3", PARTS * NE)
                for i in range(PARTS):
                    v.tensor_copy(eb3_h[:, i * C:(i + 1) * C], b3).then_inc(prepared, 1)
                    dve.wait_ge(prepared, 2 * i + 1)
                    v.tensor_tensor(b3, b3, eb3_h[:, i * C:(i + 1) * C], ALU.subtract).then_inc(prepared, 1)
                    dve.wait_ge(prepared, 2 * i + 2)
                v.memset(k_stack[STACK:P, :, :], 1.0)
                v.memset(base_cell[:, :], 0.0).then_inc(const_ready, 1)
                dve.wait_ge(const_ready, 1)

            def positions(b):
                step = Steps(q_step, b * Q_STEPS)
                dve.wait_ge(qcells, 16 * b + 16)
                cw = con("q_corner").unsqueeze(2).to_broadcast([P, NT * 4, C])
                c3 = cells_q[:, :, :, :].rearrange("p t k c -> p (t k) c")
                step(v.tensor_tensor(c3, c3, cw, ALU.mult))
                c4 = cells_q[:, :, :, :].rearrange("p t (y x) c -> p t y (x c)", y=2)
                step(v.tensor_tensor(c4[:, :, 0, :], c4[:, :, 0, :], c4[:, :, 1, :], ALU.add))
                v.tensor_tensor(v3(sq_f[:, :], NT), cells_q[:, :, 0, :], cells_q[:, :, 1, :],
                                ALU.add).then_inc(qfeat_ready, 1)
                yield
                dve.wait_ge(q_pe, b * 4 + 2)
                for g in range(2):
                    src = bank[g][:, 0:320].rearrange("p (t c) -> p t c", t=4)
                    v.tensor_copy(queries[:, g:NT:2, :], src[:, :, 0:C])
                    step(v.tensor_tensor(v3(qs[:, 0, :], NT)[:, g:NT:2, :], src[:, :, C:C + 16],
                                         rows_of(con("b_o1"), 4, 16), ALU.add))
                hid = qs[:, 0, :]
                step(layernorm(step, small_f, sq_f, hid, hid, NT, 16))
                step(v.tensor_tensor(v3(hid, NT), v3(hid, NT), rows_of(con("ln_g"), NT, 16), ALU.mult))
                v.tensor_tensor(v3(hid, NT), v3(hid, NT), rows_of(con("ln_b"), NT, 16),
                                ALU.add).then_inc(q_read, 1)
                yield
                yield
                dve.wait_ge(q_pe, b * 4 + 4)
                px, cl, fl, ge, wt, om = (qs[:, k, :] for k in range(3, 9))
                step(v.tensor_tensor(v3(px, NT), v3(bank[2][:, P:2 * P], NT), rows_of(con("b_o2"), NT, 16), ALU.add))
                step(v.scalar_tensor_tensor(px, px, 4.0, con("ref_xy"), ALU.mult, ALU.add))
                step(v.tensor_scalar(cl, px, 0.0, float(SIDE - 2), ALU.max, ALU.min))
                whole = qs[:, 9, :].bitcast(I32)
                step(v.tensor_copy(whole, cl))
                step(v.tensor_copy(fl, whole))
                step(v.tensor_tensor(ge, fl, cl, ALU.is_gt))
                step(v.tensor_tensor(fl, fl, ge, ALU.subtract))
                cell = qs[:, 10, 0:64]
                step(v.scalar_tensor_tensor(cell, fl[:, 1:128:2], float(CELLS), fl[:, 0:128:2], ALU.mult, ALU.add))
                v.tensor_scalar(cell_idx[:, :], cell, base_cell[:, 0:1], None, ALU.add).then_inc(idx_ready, 1)
                step(v.tensor_tensor(wt, px, fl, ALU.subtract))
                step(v.tensor_scalar(wt, wt, 0.0, 1.0, ALU.max, ALU.min))
                step(v.tensor_scalar(om, wt, -1.0, 1.0, ALU.mult, ALU.add))
                for k, (fy, fx) in enumerate(((om, om), (om, wt), (wt, om), (wt, wt))):
                    v.tensor_tensor(corner_w[:, :, k], fy[:, 1:128:2], fx[:, 0:128:2], ALU.mult)
                dve.wait_ge(idx_ready, b + 1)
                step(v.tensor_scalar(base_cell[:, :], base_cell[:, :], float(CELLS * CELLS), None, ALU.add))
                step.end(Q_STEPS, "Q_STEPS")
                yield

            def front(b, following):
                step = Steps(f_step, b * F_STEPS)

                def pe_gave(name):
                    dve.wait_ge(f_pe, b * len(F_PE) + F_PE[name])

                def act_gave(name):
                    dve.wait_ge(f_act, b * len(F_ACT) + F_ACT[name])

                def done(ins):
                    ins.then_inc(f_vec, 1)

                def weigh_corners(t):
                    dve.wait_ge(tile_gathered[t], b * (16 * NPT) + 16 * NPT)
                    g = v3(gathered[:, t, :], 32)
                    v.tensor_tensor(g, g, over(corner_w[:, t * NPT:(t + 1) * NPT, :]
                                               .rearrange("p a k -> p (a k)"), C),
                                    ALU.mult).then_inc(weighed, 1)

                def score_tile(t):
                    dve.wait_ge(kv_ready, b * NT + t + 1)
                    v.tensor_tensor(v3(prod[:, :], NPT), v3(bank[1][:, :], NPT),
                                    queries[:, t:t + 1, :].to_broadcast([P, NPT, C]),
                                    ALU.mult).then_inc(k_used, 1)
                    dve.wait_ge(k_used, b * NT + t + 1)
                    step(v.tensor_reduce(score[:, t * 64:(t + 1) * 64], v3(prod[:, :], 64), AX.X, ALU.add))

                weigh_corners(0)
                for t in range(NT + 1):
                    if t + 1 < NT:
                        weigh_corners(t + 1)
                    if t >= 1:
                        score_tile(t - 1)
                    yield
                if following:
                    yield from following(b + 1)
                s4 = score[:, :].rearrange("p (t s h) -> p t s h", t=NT, s=NPT)
                by_head = score[:, :].rearrange("p (t s h) -> p t h s", t=NT, s=NPT)
                top, tot = small_f[:, 1, :], small_f[:, 2, :]
                step(v.tensor_reduce(v3(top, NT), by_head, AX.X, ALU.max))
                tb = v3(top, NT).unsqueeze(2).to_broadcast([P, NT, NPT, NPT])
                v.tensor_tensor(s4, s4, tb, ALU.subtract).then_inc(shifted, 1)
                yield
                dve.wait_ge(exped, b + 1)
                v.tensor_reduce(v3(tot, NT), by_head, AX.X, ALU.add)
                dve.wait_ge(v_copied, b * NT + NT)

                def weigh_values(t0, t1):
                    vals = values[:, t0:t1, :].rearrange("p t (s d) -> p (t s) d", s=64)
                    step(v.tensor_tensor(vals, vals, over(score[:, t0 * 64:t1 * 64], 8), ALU.mult))

                weigh_values(0, 4)
                step(v.reciprocal(tot, tot))
                yield
                weigh_values(4, NT)
                for t in range(NT):
                    last = v.tensor_reduce(z_f[:, t * C:(t + 1) * C],
                                           values[:, t, :].rearrange("p (s c) -> p c s", s=NPT), AX.X, ALU.add)
                step(last)
                yield
                step(v.tensor_tensor(v3(h_f[:, :], 64), v3(z_f[:, :], 64), over(tot, 8), ALU.mult))
                s = inverse_norm(step, h_f[:, :])
                done(v.tensor_tensor(v3(z_f[:, :], NT), v3(h_f[:, :], NT), over(s, C), ALU.mult))
                yield
                pe_gave("kT")
                km = small_f[:, 3, :]
                v.tensor_reduce(km[:, 0:1], bank[0][:, :], AX.X, ALU.max)
                v.tensor_copy(km[:, 2:3], mem_max[:, :])
                step(v.tensor_reduce(km[:, 1:2], bank[1][:, :], AX.X, ALU.max))
                done(v.tensor_reduce(km[:, 3:4], km[:, 0:3], AX.X, ALU.max, negate=True))
                yield
                pe_gave("vq")
                qm = small_f[:, 4, 0:32]
                for g in range(2):
                    step(v.tensor_reduce(qm[:, 16 * g:16 * g + 16], v3(bank[1 + g][:, :], 16), AX.X, ALU.max))
                for g in range(2):
                    last = v.tensor_tensor(v3(q_soft[:, 512 * g:512 * g + 512], 16), v3(bank[1 + g][:, :], 16),
                                           over(qm[:, 16 * g:16 * g + 16], L0D), ALU.subtract)
                done(last)
                yield
                act_gave("q_exp")
                step(v.tensor_reduce(qm, v3(q_soft, 32), AX.X, ALU.add))
                step(v.reciprocal(qm, qm))
                done(v.tensor_tensor(v3(q_soft, 32), v3(q_soft, 32), over(qm, L0D), ALU.mult))
                ksum = small_f[:, 5, 0:1]
                step(v.tensor_reduce(ksum, wsum[:, 0:3], AX.X, ALU.add))
                step(v.reciprocal(ksum, ksum))
                yield
                pe_gave("ctxT")
                done(v.tensor_tensor(ctx_m[:, :], bank[2][:, 0:P], con("head_mask"), ALU.mult))
                yield
                pe_gave("lin_w")
                done(v.tensor_scalar(w_lin[:, :], bank[2][:, P:P + C], ksum, L0D ** -0.5,
                                     ALU.mult, ALU.mult))
                yield
                pe_gave("lin_y")
                z3 = v3(z_f[:, :], NT)
                step(v.tensor_tensor(z3, v3(bank[2][:, :], NT), rows_of(con("b_out"), NT, C), ALU.add))
                s = inverse_norm(step, z_f[:, :])
                step(v.tensor_tensor(z3, z3, over(s, C), ALU.mult))
                step(v.tensor_tensor(z3, z3, rows_of(con("g_out"), NT, C), ALU.mult))
                step(v.scalar_tensor_tensor(z_f[:, :], h_f[:, :], 2.0, z_f[:, :], ALU.mult, ALU.add))
                yield
                done(layernorm(step, small_f, sq_f, z_f[:, :], h_f[:, :], NT, C))
                yield
                pe_gave("w_col")
                wc, rank = small_f[:, 6, 0:NT], small_f[:, 7, :]
                v.memset(rank, 0.0)
                done(v.tensor_copy(wc, bank[2][:, 0:NT]))
                dve.wait_ge(f_vec, b * len(F_VEC) + F_VEC["w_col"])

                def rank_tile(t):
                    v.tensor_scalar(junk[:, t * P:N], w_row[:, t * P:N], wc[:, t:t + 1], None,
                                    ALU.is_gt, ALU.add, accum_out=rank[:, t:t + 1])
                    if t:
                        v.tensor_scalar(junk[:, 0:t * P], w_row[:, 0:t * P], wc[:, t:t + 1], None,
                                        ALU.is_ge, ALU.add, accum_out=rank[:, 8 + t:9 + t])
                    same = sq_f[:, 0:P]
                    step(v.scalar_tensor_tensor(same, w_row[:, t * P:(t + 1) * P], wc[:, t:t + 1], con("lower"),
                                                ALU.is_equal, ALU.mult))
                    step(v.tensor_reduce(rank[:, 16 + t:17 + t], same, AX.X, ALU.add))

                yield
                for part in range(3):
                    for t in ((0, 1, 2), (3, 4, 5), (6, 7))[part]:
                        rank_tile(t)
                    yield
                step(v.tensor_tensor(rank[:, 0:8], rank[:, 0:8], rank[:, 8:16], ALU.add))
                step(v.tensor_tensor(rank[:, 0:8], rank[:, 0:8], rank[:, 16:24], ALU.add))
                step(v.scalar_tensor_tensor(wc, rank[:, 0:8], float(KEEP), wc, ALU.is_lt, ALU.mult))
                pe_gave("mlp_y")
                step(v.tensor_tensor(z3, v3(bank[2][:, :], NT), rows_of(con("b2"), NT, C), ALU.add))
                step(v.tensor_tensor(z3, z3, over(wc, C), ALU.mult))
                step(v.scalar_tensor_tensor(z_f[:, :], h_f[:, :], 2.0, z_f[:, :], ALU.mult, ALU.add))
                yield
                done(layernorm(step, small_f, sq_f, z_f[:, :], h_mid[:, :], NT, C))
                step.end(F_STEPS, "F_STEPS")
                yield

            def back(b):
                step = Steps(b_step, b * B_STEPS)

                def pe_gave(name):
                    dve.wait_ge(b_pe, b * len(B_PE) + B_PE[name])

                def act_gave(name):
                    dve.wait_ge(b_act, b * len(B_ACT) + B_ACT[name])

                def done(ins):
                    ins.then_inc(b_vec, 1)

                yield
                pe_gave("v1")
                z_sum = z_b[:, 0:NT * C]
                v4 = z_b[:, :].rearrange("p (t a d) -> p t a d", t=NT, a=L1H)
                v.memset(v4[:, :, :, L1D + 1:WAYS], 0.0)
                v.memset(v4[:, :, :, L1D], 1.0)
                for odd in range(2):
                    last = v.tensor_tensor(
                        v4[:, odd:NT:2, :, 0:L1D],
                        bank[(7, 5)[odd]][:, 0:256].rearrange("p (t a d) -> p t a d", t=NT // 2, a=L1H),
                        con("b_v1").rearrange("p (a d) -> p a d", a=L1H)
                        .unsqueeze(1).to_broadcast([P, NT // 2, L1H, L1D]), ALU.add)
                done(last)
                act_gave("part_0")
                done(v.tensor_tensor(rest, qk, parts[:, 0, :], ALU.subtract))
                yield

                act_gave("part_1")
                done(v.tensor_tensor(parts[:, 2, :], rest, parts[:, 1, :], ALU.subtract))
                yield
                yield
                yield
                top = small_b[:, 4:6, 0:32].rearrange("p k (t a) -> p k t a", t=NT)
                step(v.memset(small_b[:, 5, 0:32], -3e38))
                for u in range(PAIRS):
                    hd, p = pair_of(u)
                    for n, (qt, k0, wide_) in enumerate(pair_chunks(p)):
                        dve.wait_ge(s_scores, b * 3 * PAIRS + 3 * u + n + 1)
                        v.tensor_reduce(top[:, k0 // 4, qt, hd:hd + 1], bank[3 + n][:, 0:wide_ * P],
                                        AX.X, ALU.max).then_inc(s_rowmax, 1)
                    if u % TOP_PAIRS == TOP_PAIRS - 1:
                        yield
                dve.wait_ge(s_rowmax, b * MAXIMA + 3 * PAIRS)
                top0, top1 = small_b[:, 4, 0:32], small_b[:, 5, 0:32]
                v.tensor_tensor(top0, top0, top1, ALU.max).then_inc(s_rowmax, 1)
                dve.wait_ge(s_rowmax, b * MAXIMA + MAXIMA)
                step(v.tensor_scalar(top0, top0, -1.0, None, ALU.mult))
                in_parts(step, top0, [tops[:, :, :, i] for i in range(PARTS)], NT, done)
                yield
                yield
                for _ in range(PAIRS + 2):
                    yield
                pe_gave("dens")
                for half in range(2):
                    cols = slice(half * 512, (half + 1) * 512)
                    step(v.reciprocal(per_den[:, cols], bank[3 + half][:, :]))
                    last = v.tensor_tensor(att[:, cols], att[:, cols], per_den[:, cols], ALU.mult)
                done(last)
                yield
                pe_gave("proj")
                step(v.tensor_tensor(v3(z_sum, NT), v3(bank[5][:, :], NT), rows_of(con("b_proj"), NT, C), ALU.add))
                step(v.tensor_tensor(z_sum, z_sum, h_mid[:, :], ALU.add))
                dve.wait_ge(out_free, b + 1)
                done(layernorm(step, small_b, sq_b, z_sum, h_b[:, :], NT, C))
                yield
                yield

                lg, e1, e2, tmp = (small_b[:, k, 0:48] for k in (7, 8, 9, 10))
                m1, m2, i1, d21 = (small_b[:, 11, k * 8:k * 8 + 8] for k in range(4))
                iota = rows_of(con("iota_e"), NT, NE)
                pe_gave("logits")
                step(v.tensor_tensor(v3(lg, NT), v3(bank[7][:, 0:48], NT), rows_of(con("rb2"), NT, NE), ALU.add))
                step(v.tensor_reduce(m1, v3(lg, NT), AX.X, ALU.max))
                done(v.tensor_tensor(v3(lg, NT), v3(lg, NT), over(m1, NE), ALU.subtract))
                yield
                act_gave("r_exp")
                step(v.tensor_reduce(m1, v3(lg, NT), AX.X, ALU.add))
                step(v.reciprocal(m1, m1))
                step(v.tensor_tensor(v3(lg, NT), v3(lg, NT), over(m1, NE), ALU.mult))

                def pick(onehot, best):
                    step(v.tensor_reduce(best, v3(lg, NT), AX.X, ALU.max))
                    step(v.tensor_tensor(v3(tmp, NT), v3(lg, NT), over(best, NE), ALU.is_lt))
                    step(v.scalar_tensor_tensor(v3(tmp, NT), v3(tmp, NT), float(2 * NE), iota, ALU.mult, ALU.add))
                    step(v.tensor_reduce(i1, v3(tmp, NT), AX.X, ALU.min))
                    step(v.tensor_tensor(v3(onehot, NT), iota, over(i1, NE), ALU.is_equal))

                pick(e1, m1)
                step(v.scalar_tensor_tensor(lg, e1, -2.0, lg, ALU.mult, ALU.add))
                pick(e2, m2)
                done(v.tensor_tensor(d21, m2, m1, ALU.subtract))
                yield
                act_gave("d_exp")
                step(v.tensor_scalar(m1, d21, 1.0, None, ALU.add))
                step(v.reciprocal(m1, m1))
                step(v.tensor_tensor(m2, d21, m1, ALU.mult))
                v.tensor_tensor(v3(e1, NT), v3(e1, NT), over(m1, NE), ALU.mult)
                step(v.tensor_tensor(v3(e2, NT), v3(e2, NT), over(m2, NE), ALU.mult))
                step(v.tensor_tensor(lg, e1, e2, ALU.add))
                in_parts(step, lg, [gate_parts[:, :, i * NE:(i + 1) * NE] for i in range(PARTS)], NT, done)
                yield
                yield
                for pr in range(3):
                    act_gave(f"e2_{pr}")
                    pe_gave(f"gb_{pr}")
                    part = a2[:, pr * 1024:(pr + 1) * 1024]
                    lo, hi = ((5, 6), (3, 4), (5, 6))[pr]
                    v.tensor_tensor(part[:, 0:512], part[:, 0:512], bank[lo][:, :], ALU.mult)
                    done(v.tensor_tensor(part[:, 512:1024], part[:, 512:1024], bank[hi][:, :], ALU.mult))
                    yield
                pe_gave("moe_y")
                v.tensor_tensor(z_sum, bank[7][:, :], h_b[:, :], ALU.add).then_inc(y_free, 1)
                dve.wait_ge(y_free, b + 2)
                step(layernorm(step, small_b, sq_b, z_sum, h_b[:, :], NT, C))
                step.end(B_STEPS, "B_STEPS")
                yield

            prepare()
            whole_program(dve, positions, front, back)


def _rows(v, n=P):
    return np.broadcast_to(np.asarray(v).reshape(1, -1), (n, np.asarray(v).size))


def _blocks(mats):
    rows, cols = sum(m.shape[0] for m in mats), sum(m.shape[1] for m in mats)
    out = np.zeros((rows, cols), np.float32)
    r = c = 0
    for m in mats:
        out[r:r + m.shape[0], c:c + m.shape[1]] = m
        r, c = r + m.shape[0], c + m.shape[1]
    return out


def _apart(m):
    out = np.zeros((P, m.shape[1]), np.float32)
    for hd in range(L1H):
        out[WAYS * hd:WAYS * hd + L1D] = m[hd * L1D:(hd + 1) * L1D]
    return out


def _shape_constants():
    line = np.linspace(-1.0, 1.0, GRID, dtype=np.float32)
    pix = (line + np.float32(1)) * np.float32(0.5) * np.float32(SIDE - 1)
    cell = np.clip(np.floor(pix), 0, SIDE - 2).astype(np.float32)
    frac = np.clip(pix - cell, 0, 1).astype(np.float32)
    tok = np.arange(N)
    gx, gy = tok % GRID, tok // GRID
    ref = np.tile(np.stack([pix[gx], pix[gy]], -1), (1, NPT))
    wx, wy = frac[gx], frac[gy]
    one = np.float32(1)
    corner = np.stack([(one - wx) * (one - wy), wx * (one - wy), (one - wx) * wy, wx * wy], -1)
    by_tile = lambda a: a.reshape(NT, P, -1).transpose(1, 0, 2).reshape(P, -1)
    i = np.arange(P)
    head = (i[:, None] // L0D == i[None, :] // L0D)
    den_spread = (i[:, None] == i[None, :] // WAYS * WAYS + L1D)
    spread = np.zeros((PARTS * NE, 3 * P))
    for e in range(NE):
        spread[e::NE, e * C:(e + 1) * C] = 1
    return cell.astype(np.int64), {
        "ident": np.eye(P), "neg_mask": np.where(i[None, :] > i[:, None], -1e30, 0.0),
        "lower": (i[None, :] < i[:, None]), "head_mask": head,
        "ref_xy": by_tile(ref), "q_corner": by_tile(corner), "iota_e": _rows(np.arange(NE)),
        "spread": spread, "den_spread": den_spread,
    }


def _layout(a):
    cell, parts = _shape_constants()
    x = a["x"]
    nb = x.shape[0]
    xc = x.transpose(0, 2, 3, 1)
    cells = np.concatenate([xc[:, :-1, :-1], xc[:, :-1, 1:], xc[:, 1:, :-1], xc[:, 1:, 1:]], -1)
    table = cells.reshape(nb * CELLS * CELLS, 4 * C)
    xq = cells[:, cell][:, :, cell].reshape(nb, NT, P, 4 * C).transpose(0, 2, 1, 3)
    xq = np.ascontiguousarray(xq).reshape(nb, P, NT * 4 * C)
    kv = np.concatenate([_blocks([a[f"L0_tok_W_{m}"].T] * 2) for m in "kv"], 1)
    mem = a["L0_attn_mem_kv"]
    w3, b3 = a["L1_attn_Wqkv"], a["L1_attn_bqkv"]
    e1, e2, e3 = (a[f"L1_ffn_expert_w{k}"] for k in (1, 2, 3))
    pairs = range(0, NE, 2)
    parts.update({
        "wq_o1": np.concatenate([a["L0_tok_W_q"].T, a["L0_tok_W_o1"]], 1),
        "b_o1": _rows(a["L0_tok_b_o1"]), "ln_g": _rows(a["L0_tok_ln_g"]), "ln_b": _rows(a["L0_tok_ln_b"]),
        "w_o2": _blocks([a["L0_tok_W_o2"]] * NT), "b_o2": _rows(a["L0_tok_b_o2"]),
        "w_kv": kv, "w_qkv": a["L0_attn_w_qkv"], "g_pre": a["L0_attn_g_pre"][:, None],
        "mem_k": mem[0].reshape(P, NMEM), "mem_v": mem[1].reshape(P, NMEM).T,
        "w_out": a["L0_attn_w_out"], "b_out": _rows(a["L0_attn_b_out"]), "g_out": _rows(a["L0_attn_g_out"]),
        "wr": np.broadcast_to(a["L0_ffn_wr"], (C, P)), "br": _rows(a["L0_ffn_br"]),
        "w1": a["L0_ffn_w1"], "b1": a["L0_ffn_b1"].reshape(2, P).T,
        "w2": np.concatenate([a["L0_ffn_w2"][:P], a["L0_ffn_w2"][P:]], 1), "b2": _rows(a["L0_ffn_b2"]),
        "w_qk": w3[:, 0:2 * C], "w_v1": w3[:, 2 * C:],
        "b_qk": b3[0:2 * C, None], "b_v1": _rows(b3[2 * C:]),
        "w_proj": _apart(a["L1_attn_Wproj"]), "b_proj": _rows(a["L1_attn_bproj"]),
        "rw1": a["L1_ffn_router_w1"], "rb1": a["L1_ffn_router_b1"][:, None],
        "rw2": a["L1_ffn_router_w2"], "rb2": _rows(a["L1_ffn_router_b2"]),
        "ew1": e1.transpose(1, 0, 2).reshape(C, NE * C), "eb1": a["L1_ffn_expert_b1"].reshape(3, P).T,
        "ew2": np.concatenate([_blocks([e2[e], e2[e + 1]]) for e in pairs], 1),
        "eb2": a["L1_ffn_expert_b2"].reshape(3, P).T,
        "ew3": np.concatenate([e3[e:e + 2].reshape(P, C) for e in pairs], 1),
        "eb3": np.concatenate([a["L1_ffn_expert_b3"]] * PARTS),
    })
    packed = np.zeros((P, WIDTH), np.float32)
    for name in ("wq_o1", "w_qkv", "g_pre", "wr", "w1", "w_qk", "w_v1", "rw1", "ew1"):
        parts[name] = np.concatenate([parts[name]] * 2)
    for name, m in parts.items():
        lo, hi = COLS[name]
        assert m.shape[1] == hi - lo, name
        packed[:m.shape[0], lo:hi] = m
    return xq, table, packed


def kernel(**inputs):
    import concourse.bacc as _bacc
    from concourse.bass_utils import run_bass_kernel_spmd as _run

    xq, table, packed = _layout({k: np.asarray(v) for k, v in inputs.items()})
    nb = xq.shape[0]
    nc = _bacc.Bacc("TRN2", target_bir_lowering=False, num_devices=1)
    arrays, args = {}, []
    for name, a in (("cells", xq), ("table", table), ("weights", packed)):
        arrays[f"in_{name}_dram"] = a
        args.append(nc.dram_tensor(f"in_{name}_dram", a.shape, F32, kind="ExternalInput").ap())
    args.append(nc.dram_tensor("out_0_dram", (nb, P, NT * C), F32, kind="ExternalOutput").ap())
    args.append(nc.dram_tensor("bounced_parts", (P, PARTS, N), BF16, kind="Internal").ap())
    tower(nc, *args)
    r = _run(nc, [arrays], core_ids=[0])
    got = r.results[0]["out_0_dram"]
    return np.ascontiguousarray(got.reshape(nb, P, NT, C).transpose(0, 2, 1, 3)).reshape(nb, N, C)
```
